# Optimizing a Trainium2 kernel written in Bass

```python
import numpy as np
import jax
import jax.numpy as jnp

def _softmax(x, axis=-1):
    return jax.nn.softmax(x, axis=axis)

def _gelu(x):
    return jax.nn.gelu(x, approximate=True)

def _silu(x):
    return jax.nn.silu(x)

def _sigmoid(x):
    return jax.nn.sigmoid(x)

def _layernorm(x, axis=-1, eps=1e-05):
    m = jnp.mean(x, axis=axis, keepdims=True)
    v = jnp.var(x, axis=axis, keepdims=True)
    return (x - m) / jnp.sqrt(v + eps)

def _scatter_add(tgt, idx, src, axis=0):
    return tgt.at[idx].add(src)

def _segment_sum(src, seg, n):
    return jax.ops.segment_sum(src, seg, n)
kernel_name = 'mk_adaln_ffn_d2_seqx_r8_c8caee'

def setup_inputs(seed: int=0):
    np.random.seed(seed)
    _w = jnp.asarray

    def _rec_inputs():
        import jax
        import jax.numpy as jnp
        _rk = jax.random.key(seed)
        x = -0.0003929 + 0.9999 * jax.random.normal(jax.random.fold_in(_rk, 1), (128, 32, 128), jnp.float32)
        _lenS = 32 - jax.random.randint(jax.random.fold_in(_rk, 7), (128,), 0, max(1, 32 // 4) + 1, jnp.int32)
        _lenS2 = 32 - jax.random.randint(jax.random.fold_in(_rk, 8), (128,), 0, max(1, 32 // 4) + 1, jnp.int32)
        itok_B_0_2 = jax.random.randint(jax.random.fold_in(_rk, 11), (128,), 0, 3, jnp.int32)
        itok_B_0_7 = jax.random.randint(jax.random.fold_in(_rk, 12), (128,), 0, 8, jnp.int32)
        return (x, itok_B_0_2, itok_B_0_7)
    x, itok_B_0_2, itok_B_0_7 = _rec_inputs()

    def _L0_cond_setup():
        import jax, jax.numpy as jnp
        import numpy as np
        NEG_INF = -1e+30
        key = jax.random.key(seed)
        k1, k2, k3, k4, k5 = jax.random.split(key, 5)
        B, S, D, A = (16, 128, 128, 32)
        hidden = jax.random.normal(k1, (B, S, D), dtype=jnp.float32)
        W1 = jax.random.normal(k2, (D, A), dtype=jnp.float32) / np.sqrt(D)
        b1 = jax.random.normal(k3, (A,), dtype=jnp.float32) * 0.01
        v = jax.random.normal(k4, (A,), dtype=jnp.float32) / np.sqrt(A)
        prompt_type_ids = jax.random.randint(k5, (B,), 0, 3, dtype=jnp.int32)
        return {'hidden': hidden, 'W1': W1, 'b1': b1, 'v': v, 'prompt_type_ids': prompt_type_ids}
    _L0_cond_all = _L0_cond_setup()
    _L0_cond_in = {k: v for k, v in _L0_cond_all.items() if k in ('W1', 'b1', 'v')}
    del _L0_cond_all

    def _L0_ffn_setup():
        import jax, jax.numpy as jnp
        import numpy as np
        B, N, C, H, REG = (1, 2309, 128, 16, 5)
        D = C // H
        key = jax.random.key(seed)
        k0, k1, k2, k3 = jax.random.split(key, 4)
        x = jax.random.normal(k0, (B, N, C), dtype=jnp.float32)
        g_info = jax.random.normal(k1, (12, 2, C), dtype=jnp.float32)
        W_qkv = jax.random.normal(k2, (C, 3 * C), dtype=jnp.float32) * 0.02
        W_proj = jax.random.normal(k3, (C, C), dtype=jnp.float32) * 0.02
        b_proj = jnp.zeros((C,), dtype=jnp.float32)
        return {'x': x, 'g_info': g_info, 'W_qkv': W_qkv, 'W_proj': W_proj, 'b_proj': b_proj}
    _L0_ffn_all = _L0_ffn_setup()
    _L0_ffn_in = {k: v for k, v in _L0_ffn_all.items() if k in ('g_info', 'W_qkv', 'W_proj', 'b_proj')}
    del _L0_ffn_all

    def _L1_cond_setup():
        import jax, jax.numpy as jnp
        import numpy as np
        S, O, H = (8, 128, 128)
        B, N = (32, 64)
        key = jax.random.key(seed)
        k1, k2, k3, k4 = jax.random.split(key, 4)
        x = jax.random.normal(k1, (B, N, H), dtype=jnp.float32)
        subject_id = jax.random.randint(k2, (B,), 0, S)
        wbound = jnp.sqrt(2.0 / 6.0) * jnp.sqrt(3.0 / H)
        weight = jax.random.uniform(k3, (S, O, H), minval=-wbound, maxval=wbound, dtype=jnp.float32)
        bbound = 1.0 / jnp.sqrt(H)
        bias = jax.random.uniform(k4, (S, O), minval=-bbound, maxval=bbound, dtype=jnp.float32)
        return {'x': x, 'subject_id': subject_id, 'weight': weight, 'bias': bias}
    _L1_cond_all = _L1_cond_setup()
    _L1_cond_in = {k: v for k, v in _L1_cond_all.items() if k in ('weight', 'bias')}
    del _L1_cond_all

    def _L1_ffn_setup():
        import jax, jax.numpy as jnp
        import numpy as np
        B, T, C = (2, 256, 128)
        H, D = (16, 64)
        CR = 8
        R = C // CR
        ROPE = D // 2
        NOPE = D - ROPE
        E, K, I, S = (8, 2, 64, 1)
        THETA = 100000.0
        EPS = 1e-05

        def _rmsnorm(x, w):
            rms = jnp.sqrt(jnp.mean(x * x, axis=-1, keepdims=True) + EPS)
            return w * (x / rms)

        def _rope(xh):
            d = xh.shape[-1]
            t = jnp.arange(xh.shape[2], dtype=jnp.float32)
            freqs = 1.0 / THETA ** (jnp.arange(0, d, 2, dtype=jnp.float32) / d)
            ang = jnp.outer(t, freqs)
            cos, sin = (jnp.cos(ang), jnp.sin(ang))
            xr = xh.reshape(xh.shape[:-1] + (d // 2, 2))
            x0, x1 = (xr[..., 0], xr[..., 1])
            rot = jnp.stack([x0 * cos - x1 * sin, x0 * sin + x1 * cos], axis=-1)
            return rot.reshape(xh.shape)

        def _attention(x, Wq, Wkva, Wkvb, Wo):
            b, t, _ = x.shape
            q = (x @ Wq).reshape(b, t, H, D).transpose(0, 2, 1, 3)
            ckv = x @ Wkva
            kv_latent, k_rope = (ckv[:, :, :R], ckv[:, :, R:])
            kv = (kv_latent @ Wkvb).reshape(b, t, H, NOPE).transpose(0, 2, 1, 3)
            k_rope = jnp.broadcast_to(k_rope[:, None, :, :], (b, H, t, ROPE))
            q_nope, q_rope = (q[..., :NOPE], q[..., NOPE:])
            q = jnp.concatenate([q_nope, _rope(q_rope)], axis=-1)
            k = jnp.concatenate([kv, _rope(k_rope)], axis=-1)
            v = jnp.concatenate([kv, jnp.zeros_like(k_rope)], axis=-1)
            att = jnp.einsum('bhqd,bhkd->bhqk', q, k) / jnp.sqrt(jnp.float32(D))
            mask = jnp.tril(jnp.ones((t, t), dtype=bool))
            att = jnp.where(mask, att, jnp.float32(-jnp.inf))
            att = jax.nn.softmax(att, axis=-1)
            y = jnp.einsum('bhqk,bhkd->bhqd', att, v)
            y = y.transpose(0, 2, 1, 3).reshape(b, t, H * D)
            return y @ Wo

        def _experts(x_flat, Wg, Wu, Wd):
            g = jax.nn.silu(jnp.einsum('nc,eci->nei', x_flat, Wg))
            u = jnp.einsum('nc,eci->nei', x_flat, Wu)
            return jnp.einsum('nei,eic->nec', g * u, Wd)

        def _moe(x, Wgate, expert_bias, Wg, Wu, Wd, sWg, sWu, sWd):
            b, t, c = x.shape
            xf = x.reshape(-1, c)
            shared = jnp.mean(_experts(xf, sWg, sWu, sWd), axis=1)
            logits = xf @ Wgate + expert_bias
            probs = jax.nn.softmax(logits, axis=-1)
            topk_p, topk_i = jax.lax.top_k(probs, K)
            topk_p = topk_p / jnp.sum(topk_p, axis=-1, keepdims=True)
            comb = jnp.sum(jax.nn.one_hot(topk_i, E, dtype=xf.dtype) * topk_p[..., None], axis=1)
            routed = jnp.einsum('ne,nec->nc', comb, _experts(xf, Wg, Wu, Wd))
            return (shared + routed).reshape(b, t, c)
        key = jax.random.key(seed)
        ks = jax.random.split(key, 16)
        w = lambda k, shp: jax.random.normal(k, shp, dtype=jnp.float32) * 0.02
        return {'x': jax.random.normal(ks[0], (B, T, C), dtype=jnp.float32), 'w_ln1': jnp.ones((C,), jnp.float32), 'Wq': w(ks[1], (C, H * D)), 'Wkva': w(ks[2], (C, R + ROPE)), 'Wkvb': w(ks[3], (R, H * NOPE)), 'Wo': w(ks[4], (H * D, C)), 'w_ln2': jnp.ones((C,), jnp.float32), 'Wgate': w(ks[5], (C, E)), 'expert_bias': jnp.zeros((E,), jnp.float32), 'Wg': w(ks[6], (E, C, I)), 'Wu': w(ks[7], (E, C, I)), 'Wd': w(ks[8], (E, I, C)), 'sWg': w(ks[9], (S, C, I)), 'sWu': w(ks[10], (S, C, I)), 'sWd': w(ks[11], (S, I, C))}
    _L1_ffn_all = _L1_ffn_setup()
    _L1_ffn_in = {k: v for k, v in _L1_ffn_all.items() if k in ('w_ln1', 'Wq', 'Wkva', 'Wkvb', 'Wo', 'w_ln2', 'Wgate', 'expert_bias', 'Wg', 'Wu', 'Wd', 'sWg', 'sWu', 'sWd')}
    del _L1_ffn_all
    return {'x': x, 'itok_B_0_2': itok_B_0_2, 'itok_B_0_7': itok_B_0_7, 'L0_cond_W1': _L0_cond_in['W1'], 'L0_cond_b1': _L0_cond_in['b1'], 'L0_cond_v': _L0_cond_in['v'], 'L0_ffn_g_info': _L0_ffn_in['g_info'], 'L0_ffn_W_qkv': _L0_ffn_in['W_qkv'], 'L0_ffn_W_proj': _L0_ffn_in['W_proj'], 'L0_ffn_b_proj': _L0_ffn_in['b_proj'], 'L1_cond_weight': _L1_cond_in['weight'], 'L1_cond_bias': _L1_cond_in['bias'], 'L1_ffn_w_ln1': _L1_ffn_in['w_ln1'], 'L1_ffn_Wq': _L1_ffn_in['Wq'], 'L1_ffn_Wkva': _L1_ffn_in['Wkva'], 'L1_ffn_Wkvb': _L1_ffn_in['Wkvb'], 'L1_ffn_Wo': _L1_ffn_in['Wo'], 'L1_ffn_w_ln2': _L1_ffn_in['w_ln2'], 'L1_ffn_Wgate': _L1_ffn_in['Wgate'], 'L1_ffn_expert_bias': _L1_ffn_in['expert_bias'], 'L1_ffn_Wg': _L1_ffn_in['Wg'], 'L1_ffn_Wu': _L1_ffn_in['Wu'], 'L1_ffn_Wd': _L1_ffn_in['Wd'], 'L1_ffn_sWg': _L1_ffn_in['sWg'], 'L1_ffn_sWu': _L1_ffn_in['sWu'], 'L1_ffn_sWd': _L1_ffn_in['sWd']}

def reference(x, itok_B_0_2, itok_B_0_7, L0_cond_W1, L0_cond_b1, L0_cond_v, L0_ffn_g_info, L0_ffn_W_qkv, L0_ffn_W_proj, L0_ffn_b_proj, L1_cond_weight, L1_cond_bias, L1_ffn_w_ln1, L1_ffn_Wq, L1_ffn_Wkva, L1_ffn_Wkvb, L1_ffn_Wo, L1_ffn_w_ln2, L1_ffn_Wgate, L1_ffn_expert_bias, L1_ffn_Wg, L1_ffn_Wu, L1_ffn_Wd, L1_ffn_sWg, L1_ffn_sWu, L1_ffn_sWd):
    import jax
    import jax.numpy as jnp

    def _L0_cond_ref(hidden, W1, b1, v, prompt_type_ids):
        import jax, jax.numpy as jnp
        import numpy as np
        NEG_INF = -1e+30
        B, S, D = hidden.shape
        attn_in = jnp.tanh(jnp.einsum('bsd,da->bsa', hidden, W1) + b1)
        scores = jnp.einsum('bsa,a->bs', attn_in, v)
        idx = jnp.arange(S)
        j = idx[:, None]
        l = idx[None, :]
        prefix_m = l <= j
        postfix_m = l >= j
        cloze_m = l != j
        pt = prompt_type_ids[:, None, None]
        mask = jnp.where(pt == 0, prefix_m[None], jnp.where(pt == 1, postfix_m[None], cloze_m[None]))
        masked_scores = jnp.where(mask, scores[:, None, :], NEG_INF)
        p = jax.nn.softmax(masked_scores, axis=-1)
        cnt = jnp.sum(mask, axis=-1).astype(hidden.dtype)
        pooled = jnp.einsum('bjl,bld->bjd', p, hidden) / cnt[..., None]
        return pooled

    def _L0_ffn_ref(x, g_info, W_qkv, W_proj, b_proj):
        import jax, jax.numpy as jnp
        import numpy as np
        B, N, C, H, REG = (1, 2309, 128, 16, 5)
        D = C // H
        Bx, Nx, Cx = x.shape
        scale = D ** (-0.5)
        qkv = (x @ W_qkv).reshape(Bx, Nx, 3, H, D)
        q, k, v = (qkv[:, :, 0], qkv[:, :, 1], qkv[:, :, 2])
        g_layer = g_info[0].reshape(-1, H, D)
        q_g = g_layer[0]
        q_pure = q[:, REG:]
        q_n = q_pure / jnp.linalg.norm(q_pure, axis=-1, keepdims=True)
        qg_n = q_g / jnp.linalg.norm(q_g, axis=-1, keepdims=True)
        sim = (qg_n[None, None] * q_n).sum(-1).mean(-1)
        sim = (sim - sim.min()) / (sim.max() - sim.min())
        pos = sim > 0.9
        logits = jnp.einsum('bqhd,bkhd->bhqk', q * scale, k)

        def masked_attn(tok_mask):
            key_mask = jnp.concatenate([jnp.ones((Bx, REG), bool), tok_mask], axis=1)
            l = jnp.where(key_mask[:, None, None, :], logits, -jnp.inf)
            a = jax.nn.softmax(l, axis=-1)
            return jnp.einsum('bhqk,bkhd->bqhd', a, v)
        x_pos = masked_attn(pos)
        x_neg = masked_attn(~pos)
        reg_out = (x_pos[:, :REG] + x_neg[:, :REG]) * 0.5
        tok_out = jnp.where(pos[:, :, None, None], x_pos[:, REG:], x_neg[:, REG:])
        out = jnp.concatenate([reg_out, tok_out], axis=1).reshape(Bx, Nx, Cx)
        return out @ W_proj + b_proj

    def _L1_cond_ref(x, subject_id, weight, bias):
        import jax, jax.numpy as jnp
        import numpy as np
        S, O, H = (8, 128, 128)
        B, N = (32, 64)
        W = weight[subject_id]
        b = bias[subject_id]
        y = jnp.einsum('bnh,boh->bno', x, W) + b[:, None, :]
        return y

    def _L1_ffn_ref(x, w_ln1, Wq, Wkva, Wkvb, Wo, w_ln2, Wgate, expert_bias, Wg, Wu, Wd, sWg, sWu, sWd):
        import jax, jax.numpy as jnp
        import numpy as np
        B, T, C = (2, 256, 128)
        H, D = (16, 64)
        CR = 8
        R = C // CR
        ROPE = D // 2
        NOPE = D - ROPE
        E, K, I, S = (8, 2, 64, 1)
        THETA = 100000.0
        EPS = 1e-05

        def _rmsnorm(x, w):
            rms = jnp.sqrt(jnp.mean(x * x, axis=-1, keepdims=True) + EPS)
            return w * (x / rms)

        def _rope(xh):
            d = xh.shape[-1]
            t = jnp.arange(xh.shape[2], dtype=jnp.float32)
            freqs = 1.0 / THETA ** (jnp.arange(0, d, 2, dtype=jnp.float32) / d)
            ang = jnp.outer(t, freqs)
            cos, sin = (jnp.cos(ang), jnp.sin(ang))
            xr = xh.reshape(xh.shape[:-1] + (d // 2, 2))
            x0, x1 = (xr[..., 0], xr[..., 1])
            rot = jnp.stack([x0 * cos - x1 * sin, x0 * sin + x1 * cos], axis=-1)
            return rot.reshape(xh.shape)

        def _attention(x, Wq, Wkva, Wkvb, Wo):
            b, t, _ = x.shape
            q = (x @ Wq).reshape(b, t, H, D).transpose(0, 2, 1, 3)
            ckv = x @ Wkva
            kv_latent, k_rope = (ckv[:, :, :R], ckv[:, :, R:])
            kv = (kv_latent @ Wkvb).reshape(b, t, H, NOPE).transpose(0, 2, 1, 3)
            k_rope = jnp.broadcast_to(k_rope[:, None, :, :], (b, H, t, ROPE))
            q_nope, q_rope = (q[..., :NOPE], q[..., NOPE:])
            q = jnp.concatenate([q_nope, _rope(q_rope)], axis=-1)
            k = jnp.concatenate([kv, _rope(k_rope)], axis=-1)
            v = jnp.concatenate([kv, jnp.zeros_like(k_rope)], axis=-1)
            att = jnp.einsum('bhqd,bhkd->bhqk', q, k) / jnp.sqrt(jnp.float32(D))
            mask = jnp.tril(jnp.ones((t, t), dtype=bool))
            att = jnp.where(mask, att, jnp.float32(-jnp.inf))
            att = jax.nn.softmax(att, axis=-1)
            y = jnp.einsum('bhqk,bhkd->bhqd', att, v)
            y = y.transpose(0, 2, 1, 3).reshape(b, t, H * D)
            return y @ Wo

        def _experts(x_flat, Wg, Wu, Wd):
            g = jax.nn.silu(jnp.einsum('nc,eci->nei', x_flat, Wg))
            u = jnp.einsum('nc,eci->nei', x_flat, Wu)
            return jnp.einsum('nei,eic->nec', g * u, Wd)

        def _moe(x, Wgate, expert_bias, Wg, Wu, Wd, sWg, sWu, sWd):
            b, t, c = x.shape
            xf = x.reshape(-1, c)
            shared = jnp.mean(_experts(xf, sWg, sWu, sWd), axis=1)
            logits = xf @ Wgate + expert_bias
            probs = jax.nn.softmax(logits, axis=-1)
            topk_p, topk_i = jax.lax.top_k(probs, K)
            topk_p = topk_p / jnp.sum(topk_p, axis=-1, keepdims=True)
            comb = jnp.sum(jax.nn.one_hot(topk_i, E, dtype=xf.dtype) * topk_p[..., None], axis=1)
            routed = jnp.einsum('ne,nec->nc', comb, _experts(xf, Wg, Wu, Wd))
            return (shared + routed).reshape(b, t, c)
        x = x + _attention(_rmsnorm(x, w_ln1), Wq, Wkva, Wkvb, Wo)
        residual = x
        xn = _rmsnorm(x, w_ln2)
        x_out = _moe(xn, Wgate, expert_bias, Wg, Wu, Wd, sWg, sWu, sWd)
        return residual + x_out
    x = x + _L0_ffn_ref(_L0_cond_ref(x, L0_cond_W1, L0_cond_b1, L0_cond_v, itok_B_0_2), L0_ffn_g_info, L0_ffn_W_qkv, L0_ffn_W_proj, L0_ffn_b_proj)
    x = x + _L1_ffn_ref(_L1_cond_ref(x, itok_B_0_7, L1_cond_weight, L1_cond_bias), L1_ffn_w_ln1, L1_ffn_Wq, L1_ffn_Wkva, L1_ffn_Wkvb, L1_ffn_Wo, L1_ffn_w_ln2, L1_ffn_Wgate, L1_ffn_expert_bias, L1_ffn_Wg, L1_ffn_Wu, L1_ffn_Wd, L1_ffn_sWg, L1_ffn_sWu, L1_ffn_sWd)
    return x

_drawn_inputs = setup_inputs


def setup_inputs(seed=0):
    import zlib

    import numpy as np

    out = dict(_drawn_inputs(seed))
    spreads = {'L0_ffn_b_proj': (0.0, 0.1),
     'L1_ffn_w_ln1': (1.0, 0.6),
     'L1_ffn_w_ln2': (1.0, 0.6),
     'L1_ffn_expert_bias': (0.0, 0.8)}
    factors = {'L0_cond_W1': 8.0,
     'L0_cond_b1': 8.0,
     'L0_cond_v': 8.0,
     'L0_ffn_g_info': 8.0,
     'L0_ffn_W_qkv': 8.0,
     'L0_ffn_W_proj': 8.0,
     'L1_ffn_Wq': 8.0,
     'L1_ffn_Wkva': 8.0,
     'L1_ffn_Wkvb': 8.0,
     'L1_ffn_Wo': 8.0,
     'L1_ffn_Wgate': 8.0,
     'L1_ffn_Wg': 8.0,
     'L1_ffn_Wu': 8.0,
     'L1_ffn_Wd': 8.0,
     'L1_ffn_sWg': 8.0,
     'L1_ffn_sWu': 8.0,
     'L1_ffn_sWd': 8.0}
    for name, (base, spread) in spreads.items():
        noise = np.random.default_rng([zlib.crc32(name.encode()), seed]).standard_normal(out[name].shape)
        drawn = base * np.exp(spread * noise) if base else spread * noise
        out[name] = jnp.asarray(drawn.astype(out[name].dtype))
    for name, factor in factors.items():
        out[name] = (out[name] * factor).astype(out[name].dtype)
    return out
```

```python
from contextlib import ExitStack

import concourse.bass as bass
import numpy as np
from concourse import mybir

ALU = mybir.AluOpType
ACT = mybir.ActivationFunctionType
AX_X = mybir.AxisListType.X
F32 = mybir.dt.float32
BF16 = mybir.dt.bfloat16
I32 = mybir.dt.int32

P = 128
B, S, C = 128, 32, 128
TOK = B * S
SEQ = P // S
GROUPS = TOK // P
GPB = 4
BLK = GPB * P
NBLK = TOK // BLK
SPB = BLK // S
A = 32
H0, D0, REG = 16, 8, 5
HG = 4
HPG = H0 // HG
H1, D1, ROPE, R = 16, 64, 32, 16
NOPE = D1 - ROPE
E, K_TOP, I = 8, 2, 64
PAIRS = (E + 2) // 2
SUBJ = 8
EPS = 1e-5
THETA = 100000.0
QX = HPG * S + S
BIG = 1e30
MASK = -float(2 ** 100)


def shape_constants():
    p = np.arange(P)
    f = np.float32
    q, k = p % S, np.arange(S)
    cols = {}
    cols["ident"] = np.eye(P)
    cols["prefix"] = k[None] <= q[:, None]
    cols["postfix"] = k[None] >= q[:, None]
    cols["cloze"] = k[None] != q[:, None]
    cols["own"] = k[None] == q[:, None]
    cols["same_seq"] = (p[:, None] // S) == (p[None] // S)
    cols["is_reg_key"] = np.broadcast_to(k[None] < REG, (P, S))
    cols["is_reg_row"] = (q < REG)[:, None]
    head = (p // D0) % HPG
    cols["head_row"] = head[:, None] == np.arange(HPG)[None]
    share = np.where((q < REG)[:, None, None] | (np.arange(HPG + 1) == HPG)[None, None], 0.5, 1.0)
    cols["share"] = np.broadcast_to(share, (P, HG, HPG + 1)).reshape(P, -1)
    t = np.arange(S, dtype=f)
    freqs = (f(1.0) / f(THETA) ** (np.arange(0, ROPE, 2, dtype=f) / f(ROPE))).astype(f)
    angle = np.outer(t, freqs).astype(f)
    cos = np.repeat(np.cos(angle).T, 2, axis=0)
    sin = np.repeat(np.sin(angle).T, 2, axis=0)
    one, zero = np.ones((S, S)), np.zeros((S, S))
    causal = np.where(k[:, None] > k[None], MASK, 0.0)
    cols["q_turn"] = np.concatenate([cos, sin, one, zero]) * f(D1) ** f(-0.5)
    cols["k_turn"] = np.concatenate([cos, cos, one, zero])
    cols["k_cross"] = np.concatenate([sin, sin, zero, zero])
    cols["causal"] = np.concatenate([zero, zero, zero, causal])
    pick = np.zeros((P, PAIRS, P))
    for part in range(3):
        for e in range(E + 1):
            pick[part * (E + 1) + e, e // 2, (e % 2) * I:(e % 2) * I + I] = 0.5
    cols["pick"] = pick.reshape(P, -1)
    cols["first"] = np.broadcast_to(E - np.arange(E)[None], (P, E))
    at, n = {}, 0
    for name, v in cols.items():
        at[name] = (n, n + v.shape[1])
        n += v.shape[1]
    return at, np.concatenate([np.asarray(v, f) for v in cols.values()], axis=1).astype(f)


def pairs_of_blocks(eng):
    yield 0
    with eng.Fori(1, NBLK // 2) as i:
        yield i


def blocks(eng):
    for i in pairs_of_blocks(eng):
        for half in range(2):
            yield i, half


def after(eng, signal, count):
    if not isinstance(count, int) or count > 0:
        eng.wait_ge(signal, count)


def wait_apart(pe, signal, count):
    if not isinstance(count, int) or count > 0:
        pe.wait_ge(signal, count)
        pe.nop(nofuse=True)


SLOTS = 2 * GPB


def slots(eng, most):
    for j in range(SLOTS):
        yield 0, j, lambda lag, j=j: j >= lag
    with eng.Fori(1, GROUPS // SLOTS) as i:
        for j in range(SLOTS):
            yield i, j, lambda lag: True
    for j in range(most):
        yield GROUPS // SLOTS, j, lambda lag, j=j: lag > j


def build(nc, ins, const, const_at, out):
    v, act, pool = nc.vector, nc.scalar, nc.gpsimd
    x_d = ins["x"].rearrange("b s c -> (b s) c")
    x_groups = x_d.rearrange("(g p) c -> p g c", p=P)
    out_groups = out.rearrange("b s c -> (b s) c").rearrange("(g p) c -> p g c", p=P)

    top = ExitStack()
    with top:
        def sem(name):
            return top.enter_context(nc.semaphore(name))

        def sb(ctx, name, shape, dt=F32):
            return ctx.enter_context(nc.sbuf_tensor(name, shape, dt))

        def ps(ctx, name, shape, dt=F32):
            return ctx.enter_context(nc.psum_tensor(name, shape, dt))

        con = sb(top, "con", [P, const.shape[1]])

        def c(name):
            a, b = const_at[name]
            return con[:, a:b]

        ident = c("ident")
        x_f = sb(top, "x_f", [P, TOK])
        ones = sb(top, "ones", [P, P])
        w1 = sb(top, "w1", [P, A])
        b1 = sb(top, "b1", [A, 1])
        v_col = sb(top, "v_col", [A, 1])
        v_wide = sb(top, "v_wide", [A, S])
        prompt = sb(top, "prompt", [P, B], I32)
        wqkv = sb(top, "wqkv", [P, 3 * C])
        g_row = sb(top, "g_row", [P, C])
        wproj = sb(top, "wproj", [P, C])
        wproj_h = sb(top, "wproj_h", [P, HPG, C])
        bproj = sb(top, "bproj", [P, 1])
        w_subj = sb(top, "w_subj", [P, SUBJ, C])
        w_subj_t = sb(top, "w_subj_t", [P, SUBJ, C])
        ln1 = sb(top, "ln1", [P, 1])
        ln2 = sb(top, "ln2", [P, 1])
        wq_heads = sb(top, "wq_heads", [P, H1, 96])
        wk_a = sb(top, "wk_a", [P, 96])
        wk_b = sb(top, "wk_b", [P, 64])
        w_lat = sb(top, "w_lat", [P, S])
        w_o = sb(top, "w_o", [P, H1 // 4, C])
        wgate = sb(top, "wgate", [P, E])
        gate_b = sb(top, "gate_b", [P, E])
        wg = sb(top, "wg", [P, 2 * PAIRS, I])
        wu = sb(top, "wu", [P, 2 * PAIRS, I])
        wd = sb(top, "wd", [P, PAIRS, C])
        pick = sb(top, "pick", [3 * (E + 1), PAIRS, P], BF16)

        with ExitStack() as ph:
            wq = sb(ph, "wq", [P, H1 * D1])
            wka = sb(ph, "wka", [P, R + ROPE])
            wkvb = sb(ph, "wkvb", [R, H1 * NOPE])
            wkvb_t = sb(ph, "wkvb_t", [NOPE, H1, S])
            wq_nt = sb(ph, "wq_nt", [NOPE, H1, C])
            wo = sb(ph, "wo", [NOPE, H1, C])
            t_ps = [ps(ph, f"t_ps{n}", [P, BLK]) for n in range(4)]
            k_ps = ps(ph, "k_ps", [P, 4, R])
            a_ps = ps(ph, "a_ps", [P, H1, R])
            m_ps = ps(ph, "m_ps", [P, BLK])
            loads = [
                (con[:], const), (w_subj[:], ins["L1_cond_weight"].rearrange("s o h -> o s h")),
                (wq[:], ins["L1_ffn_Wq"]), (wkvb[:], ins["L1_ffn_Wkvb"]),
                (ln1[:], ins["L1_ffn_w_ln1"].rearrange("(p a) -> p a", a=1)),
                (ln2[:], ins["L1_ffn_w_ln2"].rearrange("(p a) -> p a", a=1)),
                (wka[:], ins["L1_ffn_Wkva"]),
                (wo[:], ins["L1_ffn_Wo"].rearrange("(h d) c -> d h c", d=D1)[0:NOPE, :, :]),
                (w1[:], ins["L0_cond_W1"]), (b1[:], ins["L0_cond_b1"].rearrange("(p a) -> p a", a=1)),
                (v_col[:], ins["L0_cond_v"].rearrange("(p a) -> p a", a=1)),
                (prompt[:], ins["itok_B_0_2"].partition_broadcast(P)),
                (wqkv[:], ins["L0_ffn_W_qkv"]),
                (g_row[:], ins["L0_ffn_g_info"][0, 0].partition_broadcast(P)),
                (wproj[:], ins["L0_ffn_W_proj"]),
                (bproj[:], ins["L0_ffn_b_proj"].rearrange("(p a) -> p a", a=1)),
                (wgate[:], ins["L1_ffn_Wgate"]),
                (gate_b[:], ins["L1_ffn_expert_bias"].partition_broadcast(P)),
                (wg[:, 0:E, :], ins["L1_ffn_Wg"].rearrange("e c i -> c e i")),
                (wg[:, E, :], ins["L1_ffn_sWg"][0]),
                (wu[:, 0:E, :], ins["L1_ffn_Wu"].rearrange("e c i -> c e i")),
                (wu[:, E, :], ins["L1_ffn_sWu"][0]),
                (wd[0:I, 0:E // 2, :], ins["L1_ffn_Wd"].rearrange("(p t) i c -> t i p c", t=2)[0]),
                (wd[I:P, 0:E // 2, :], ins["L1_ffn_Wd"].rearrange("(p t) i c -> t i p c", t=2)[1]),
                (wd[0:I, E // 2, :], ins["L1_ffn_sWd"][0]),
            ]
            loaded = sem("loaded")
            cleared = sem("cleared")
            wq_scaled = sem("wq_scaled")
            turned = sem("turned")
            untangled = sem("untangled")
            small_done = sem("small_done")
            absorbed = sem("absorbed")
            N_CLEAR = 4

            block = ph.enter_context(nc.Block())

            @block.sync
            def _(sp):
                for dst, src in loads:
                    sp.dma_start(dst, src).then_inc(loaded, 16)

            @block.gpsimd
            def _(eng):
                pool.memset(wkvb_t[:], 0.0).then_inc(cleared, 1)
                pool.memset(wq_heads[:], 0.0).then_inc(cleared, 1)
                pool.memset(wk_a[:], 0.0).then_inc(cleared, 1)
                pool.memset(w_lat[:], 0.0).then_inc(cleared, 1)
                pool.memset(ones[:], 1.0).then_inc(cleared, 1)

            @block.tensor
            def _(pe):
                pe.wait_ge(loaded, 16 * len(loads))
                for s in range(SUBJ):
                    ins_ = pe.transpose(t_ps[s // 4][:, (s % 4) * P:(s % 4 + 1) * P], w_subj[:, s, :], ident)
                    if s % 4 == 3:
                        ins_.then_inc(turned, 1)
                for n in range(4):
                    ins_ = pe.transpose(k_ps[:, n, :], wkvb[:, n * P:(n + 1) * P], ident[0:R, 0:R])
                ins_.then_inc(turned, 1)
                pe.wait_ge(wq_scaled, 1)
                for n in range(8):
                    ins_ = pe.transpose(t_ps[2 + n // 4][:, (n % 4) * P:(n % 4 + 1) * P], wq[:, n * P:(n + 1) * P], ident)
                    if n % 4 == 3:
                        ins_.then_inc(turned, 1)
                pe.wait_ge(untangled, 7)
                for h in range(H1):
                    pe.matmul(a_ps[:, h, :], wq_nt[:, h, :], wkvb_t[:, h, 0:R], start=True, stop=True)
                for h in range(H1):
                    ins_ = pe.matmul(m_ps[32 * (h // 4):32 * (h // 4) + 32, (h % 4) * C:(h % 4 + 1) * C],
                                     wkvb_t[:, h, :], wo[:, h, :], start=True, stop=True)
                ins_.then_inc(absorbed, 1)

            @block.vector
            def _(eng):
                v.wait_ge(loaded, 16 * len(loads))
                v.wait_ge(cleared, 5)
                v.tensor_scalar(wq[:], wq[:], ln1[:, 0:1], None, ALU.mult).then_inc(wq_scaled, 1)
                v.tensor_scalar(wka[:], wka[:], ln1[:, 0:1], None, ALU.mult).then_inc(wq_scaled, 1)
                v.tensor_scalar(wgate[:], wgate[:], ln2[:, 0:1], None, ALU.mult)
                v.tensor_scalar(wg[:, 0:E + 1, :], wg[:, 0:E + 1, :], ln2[:, 0:1], None, ALU.mult)
                v.tensor_scalar(wu[:, 0:E + 1, :], wu[:, 0:E + 1, :], ln2[:, 0:1], None, ALU.mult)
                v.tensor_copy(v_wide[:], v_col[:, 0:1].to_broadcast([A, S]))
                v.tensor_copy(pick[:], c("pick")[0:3 * (E + 1), :].rearrange("p (a b) -> p a b", a=PAIRS))
                for h in range(HPG):
                    v.tensor_scalar(wproj_h[:, h, :], wproj[:], c("head_row")[:, h:h + 1], None, ALU.mult)
                v.wait_ge(wq_scaled, 2)
                pairs = wq[:].rearrange("p (h a f t) -> p h a f t", h=H1, a=2, t=2)[:, :, 1, :, :]
                crossed = wq_heads[:, :, ROPE:2 * ROPE].rearrange("p h (f t) -> p h f t", t=2)
                v.tensor_copy(wq_heads[:, :, 0:ROPE], wq[:].rearrange("p (h a f) -> p h a f", h=H1, a=2)[:, :, 1, :])
                v.tensor_scalar(crossed[:, :, :, 0], pairs[:, :, :, 1], -1.0, None, ALU.mult)
                v.tensor_copy(crossed[:, :, :, 1], pairs[:, :, :, 0])
                rope = wka[:, R:R + ROPE]
                rope_pairs = rope.rearrange("p (f t) -> p f t", t=2)
                v.tensor_copy(wk_a[:, 0:ROPE], rope)
                v.tensor_copy(wk_a[:, ROPE:2 * ROPE], rope)
                v.tensor_copy(wk_a[:, 2 * ROPE:2 * ROPE + R], wka[:, 0:R])
                v.tensor_copy(w_lat[:, 0:R], wka[:, 0:R])
                for n in range(2):
                    cross = wk_b[:, n * ROPE:(n + 1) * ROPE].rearrange("p (f t) -> p f t", t=2)
                    v.tensor_scalar(cross[:, :, 0], rope_pairs[:, :, 1], -1.0, None, ALU.mult)
                    v.tensor_copy(cross[:, :, 1], rope_pairs[:, :, 0])
                for n in range(2):
                    v.wait_ge(turned, n + 1)
                    v.tensor_copy(w_subj_t[:, 4 * n:4 * n + 4, :].rearrange("p s o -> p (s o)"), t_ps[n][:]).then_inc(untangled, 1)
                v.wait_ge(turned, 3)
                for m in range(4):
                    ins_ = v.tensor_copy(wkvb_t[:, :, 0:R].rearrange("p (n m) r -> p n m r", m=4)[:, :, m, :],
                                         k_ps[32 * m:32 * m + 32, :, :])
                ins_.then_inc(untangled, 1)
                for n in range(2):
                    v.wait_ge(turned, 4 + n)
                    for m in range(2):
                        v.tensor_copy(wq_nt[:, 8 * n:8 * n + 8, :].rearrange("p (j m) c -> p j m c", m=2)[:, :, m, :],
                                      t_ps[2 + n][64 * m:64 * m + NOPE, :].rearrange("p (j c) -> p j c", j=4)).then_inc(untangled, 1)
                v.wait_ge(absorbed, 1)
                v.tensor_copy(wq_heads[:, :, 64:64 + R], a_ps[:])
                v.tensor_copy(w_o[:].rearrange("p h c -> p (h c)"), m_ps[:]).then_inc(small_done, 1)


        layer0 = top.enter_context(ExitStack())
        q_f = sb(layer0, "q_f", [P, TOK])
        k_f = sb(layer0, "k_f", [P, TOK])
        v_t = sb(layer0, "v_t", [P, GROUPS, C])
        class_mask = sb(layer0, "class_mask", [P, GROUPS, HPG + 1, S])

        similar = top.enter_context(ExitStack())
        lie = sb(similar, "lie", [P, 2, GROUPS, H0])
        guide = sb(similar, "guide", [P, C])

        pooling = top.enter_context(ExitStack())
        pooled_p = sb(pooling, "pooled_p", [P, GROUPS, P])

        scores_ctx = top.enter_context(ExitStack())
        score_ps = ps(scores_ctx, "score_ps", [P, GROUPS * S])
        with ExitStack() as ph:
            x_in = sb(ph, "x_in", [P, 2, GPB, C])
            hid = sb(ph, "hid", [A, TOK])
            x_ps = ps(ph, "x_ps", [P, 2, BLK])
            h_ps = ps(ph, "h_ps", [A, 2, BLK])
            a_in, a_in_free = [sem("a_in0"), sem("a_in1")], sem("a_in_free")
            a_x, a_xc, a_h, a_hc, a_sc, a_clear = (sem(n) for n in ("a_x", "a_xc", "a_h", "a_hc", "a_sc", "a_clear"))
            block = ph.enter_context(nc.Block())

            @block.sync
            def _(sp):
                for i, half in blocks(sp):
                    blk = 2 * i + half
                    sp.wait_ge(a_in_free, blk + 1)
                    sp.dma_start(x_in[:, half], x_groups[:, bass.ds(blk * GPB, GPB), :]).then_inc(a_in[half], 16)

            @block.gpsimd
            def _(eng):
                pool.memset(pooled_p[:], 0.0).then_inc(a_clear, 1)

            @block.tensor
            def _(pe):
                pe.sem_inc(a_in_free, 2)
                for i, half in blocks(pe):
                    blk = 2 * i + half
                    pe.wait_ge(a_in[half], 16 * i + 16)
                    after(pe, a_xc, blk)
                    for g in range(GPB):
                        ins_ = pe.transpose(x_ps[:, half, g * P:(g + 1) * P], x_in[:, half, g, :], ident)
                    ins_.then_inc(a_x, 1)
                    pe.wait_ge(a_x, blk + 1)
                    pe.sem_inc(a_in_free, 1)
                    pe.wait_ge(a_xc, blk + 1)
                    after(pe, a_hc, blk)
                    pe.matmul(h_ps[:, half, :], w1[:], x_f[:, bass.ds(blk * BLK, BLK)], start=True, stop=True).then_inc(a_h, 1)
                pe.wait_ge(a_hc, NBLK)
                hid_v = hid[:].rearrange("a (g s l) -> a g s l", s=SEQ, l=S)
                for n in range(2):
                    for s in range(SEQ):
                        ins_ = pe.matmul(score_ps[32 * s:32 * s + 32, n * BLK:(n + 1) * BLK], v_wide[:],
                                         hid_v[:, n * 16:(n + 1) * 16, s, :], start=True, stop=True)
                ins_.then_inc(a_sc, 1)

            @block.scalar
            def _(eng):
                for i, half in blocks(act):
                    blk = 2 * i + half
                    act.wait_ge(a_x, blk + 1)
                    act.activation(x_f[:, bass.ds(blk * BLK, BLK)], x_ps[:, half, :], ACT.Copy).then_inc(a_xc, 1)
                    act.wait_ge(a_h, blk + 1)
                    act.activation(hid[:, bass.ds(blk * BLK, BLK)], h_ps[:, half, :], ACT.Tanh, bias=b1[:, 0:1]).then_inc(a_hc, 1)
                act.wait_ge(a_sc, 1)

        with ExitStack() as ph:
            W = [P, GROUPS, S]
            types = sb(ph, "types", [P, GROUPS])
            kind = sb(ph, "kind", [P, 3, GROUPS])
            allow = sb(ph, "allow", W)
            part = sb(ph, "part", W)
            part2 = sb(ph, "part2", W)
            sc = sb(ph, "sc", W)
            row = sb(ph, "row", [P, 4, GROUPS])
            b_step, b_shift, b_exp = sem("b_step"), sem("b_shift"), sem("b_exp")
            block = ph.enter_context(nc.Block())

            @block.scalar
            def _(eng):
                act.wait_ge(b_shift, 1)
                act.activation(sc[:], sc[:], ACT.Exp).then_inc(b_exp, 1)

            @block.vector
            def _(eng):
                count = [0]

                def done(ins_):
                    count[0] += 1
                    ins_.then_inc(b_step, 1)
                    v.wait_ge(b_step, count[0])

                def over_l(a):
                    return a.unsqueeze(2).to_broadcast(W)

                def over_g(a):
                    return a.unsqueeze(1).to_broadcast(W)

                for s in range(SEQ):
                    r = slice(32 * s, 32 * s + 32)
                    ins_ = v.tensor_copy(types[r, :], prompt[r, :].rearrange("p (g s) -> p g s", s=SEQ)[:, :, s])
                done(ins_)
                v.tensor_scalar(kind[:, 0, :], types[:], 0.0, None, ALU.is_equal)
                done(v.tensor_scalar(kind[:, 1, :], types[:], 1.0, None, ALU.is_equal))
                done(v.tensor_tensor(kind[:, 2, :], kind[:, 0, :], kind[:, 1, :], ALU.add))
                done(v.tensor_scalar(kind[:, 2, :], kind[:, 2, :], -1.0, 1.0, ALU.mult, ALU.add))
                v.tensor_tensor(part[:], over_l(kind[:, 0, :]), over_g(c("prefix")), ALU.mult)
                v.tensor_tensor(part2[:], over_l(kind[:, 1, :]), over_g(c("postfix")), ALU.mult)
                done(v.tensor_tensor(allow[:], over_l(kind[:, 2, :]), over_g(c("cloze")), ALU.mult))
                done(v.tensor_tensor(allow[:], allow[:], part[:], ALU.add))
                done(v.tensor_tensor(allow[:], allow[:], part2[:], ALU.add))
                done(v.tensor_reduce(row[:, 0, :], allow[:], AX_X, ALU.add))
                done(v.tensor_scalar(part[:], allow[:], BIG, -BIG, ALU.mult, ALU.add))
                done(v.tensor_tensor(sc[:], part[:], score_ps[:].rearrange("p (g l) -> p g l", l=S), ALU.add))
                done(v.tensor_reduce(row[:, 1, :], sc[:], AX_X, ALU.max))
                v.tensor_tensor(sc[:], sc[:], over_l(row[:, 1, :]), ALU.subtract).then_inc(b_shift, 1)
                v.wait_ge(b_exp, 1)
                done(v.tensor_reduce(row[:, 2, :], sc[:], AX_X, ALU.add))
                done(v.tensor_tensor(row[:, 2, :], row[:, 2, :], row[:, 0, :], ALU.mult))
                done(v.reciprocal(row[:, 3, :], row[:, 2, :]))
                done(v.tensor_tensor(sc[:], sc[:], over_l(row[:, 3, :]), ALU.mult))
                v.wait_ge(a_clear, 1)
                for s in range(SEQ):
                    r = slice(32 * s, 32 * s + 32)
                    ins_ = v.transpose(pooled_p[r, :, r], sc[r, :, :])
                done(ins_)
        scores_ctx.close()

        with ExitStack() as ph:
            x_in = sb(ph, "x_in2", [P, 2, GPB, C])
            xc = sb(ph, "xc", [P, 2, BLK])
            q2 = sb(ph, "q2", [P, GPB, C])
            qg = sb(ph, "qg", [P, GPB, C])
            gh = sb(ph, "gh", [P, 2, H0])
            xc_ps = ps(ph, "xc_ps", [P, 2, BLK])
            qf_ps, kf_ps, qt_ps, vt_ps = (ps(ph, n, [P, BLK]) for n in ("qf_ps", "kf_ps", "qt_ps", "vt_ps"))
            c_in, c_xc, c_xcc = [sem("c_in0"), sem("c_in1")], sem("c_xc"), sem("c_xcc")
            c_qf, c_kf, c_qt, c_vt = (sem(n) for n in ("c_qf", "c_kf", "c_qt", "c_vt"))
            c_qfc, c_kfc, c_sq, c_vtc, c_qg, c_red, c_g = (sem(n) for n in ("c_qfc", "c_kfc", "c_sq", "c_vtc", "c_qg", "c_red", "c_g"))
            c_free, c_g2 = sem("c_free"), sem("c_g2")
            block = ph.enter_context(nc.Block())

            @block.sync
            def _(sp):
                for i, half in blocks(sp):
                    blk = 2 * i + half
                    sp.wait_ge(c_free, blk + 1)
                    sp.dma_start(x_in[:, half], x_groups[:, bass.ds(blk * GPB, GPB), :]).then_inc(c_in[half], 16)

            @block.tensor
            def _(pe):
                pe.sem_inc(c_free, 2)
                for i, half in blocks(pe):
                    blk = 2 * i + half
                    pe.wait_ge(c_in[half], 16 * i + 16)
                    after(pe, c_xcc, blk)
                    for g in range(GPB):
                        ins_ = pe.matmul(xc_ps[:, half, g * P:(g + 1) * P], x_in[:, half, g, :],
                                         pooled_p[:, blk * GPB + g, :], start=True, stop=True)
                    ins_.then_inc(c_xc, 1)
                    pe.wait_ge(c_xc, blk + 1)
                    pe.sem_inc(c_free, 1)
                    pe.wait_ge(c_xcc, blk + 1)
                    after(pe, c_qg, blk)
                    after(pe, c_sq, blk)
                    for g in range(GPB):
                        ins_ = pe.matmul(qt_ps[:, g * P:(g + 1) * P], xc[:, half, g * P:(g + 1) * P],
                                         wqkv[:, 0:C], start=True, stop=True)
                    ins_.then_inc(c_qt, 1)
                    after(pe, c_qfc, blk)
                    pe.matmul(qf_ps[:], wqkv[:, 0:C], xc[:, half, :], start=True, stop=True).then_inc(c_qf, 1)
                    after(pe, c_kfc, blk)
                    pe.matmul(kf_ps[:], wqkv[:, C:2 * C], xc[:, half, :], start=True, stop=True).then_inc(c_kf, 1)
                    after(pe, c_vtc, blk)
                    for g in range(GPB):
                        ins_ = pe.matmul(vt_ps[:, g * P:(g + 1) * P], xc[:, half, g * P:(g + 1) * P],
                                         wqkv[:, 2 * C:3 * C], start=True, stop=True)
                    ins_.then_inc(c_vt, 1)

            @block.scalar
            def _(eng):
                act.wait_ge(c_g, 1)
                act.activation(gh[:, 1, :], gh[:, 0, :], ACT.Sqrt).then_inc(c_g, 1)
                for i, half in blocks(act):
                    blk = 2 * i + half
                    act.wait_ge(c_xc, blk + 1)
                    if half:
                        after(act, c_vt, blk - 1)
                    else:
                        after(act, c_vt, blk)
                    act.activation(xc[:, half, :], xc_ps[:, half, :], ACT.Copy).then_inc(c_xcc, 1)
                    act.wait_ge(c_qt, blk + 1)
                    after(act, c_red, 2 * blk)
                    act.activation(q2[:].rearrange("p g c -> p (g c)"), qt_ps[:], ACT.Square).then_inc(c_sq, 1)
                    act.wait_ge(c_kf, blk + 1)
                    act.activation(k_f[:, bass.ds(blk * BLK, BLK)], kf_ps[:], ACT.Copy).then_inc(c_kfc, 1)
                    act.wait_ge(c_vt, blk + 1)
                    act.activation(v_t[:, bass.ds(blk * GPB, GPB), :], vt_ps[:].rearrange("p (g c) -> p g c", g=GPB),
                                   ACT.Copy).then_inc(c_vtc, 1)

            @block.vector
            def _(eng):
                def heads(a):
                    return a.rearrange("p (h d) -> p h d", d=D0)

                v.tensor_tensor(qg[:, 0, :], g_row[:], g_row[:], ALU.mult).then_inc(c_g2, 1)
                v.wait_ge(c_g2, 1)
                v.tensor_reduce(gh[:, 0, :], heads(qg[:, 0, :]), AX_X, ALU.add).then_inc(c_g, 1)
                v.wait_ge(c_g, 2)
                v.reciprocal(gh[:, 0, :], gh[:, 1, :]).then_inc(c_g, 1)
                v.wait_ge(c_g, 3)
                v.tensor_tensor(heads(guide[:]), heads(g_row[:]), gh[:, 0, :].unsqueeze(2).to_broadcast([P, H0, D0]),
                                ALU.mult).then_inc(c_g, 1)
                v.wait_ge(c_g, 4)
                for i, half in blocks(v):
                    blk = 2 * i + half
                    v.wait_ge(c_sq, blk + 1)
                    after(v, c_red, 2 * blk)
                    v.tensor_tensor(qg[:], qt_ps[:].rearrange("p (g c) -> p g c", g=GPB),
                                    guide[:].unsqueeze(1).to_broadcast([P, GPB, C]), ALU.mult).then_inc(c_qg, 1)
                    v.wait_ge(c_qf, blk + 1)
                    v.tensor_copy(q_f[:, bass.ds(blk * BLK, BLK)], qf_ps[:]).then_inc(c_qfc, 1)
                    v.wait_ge(c_qg, blk + 1)
                    v.tensor_reduce(lie[:, 0, bass.ds(blk * GPB, GPB), :], qg[:].rearrange("p g (h d) -> p g h d", d=D0),
                                    AX_X, ALU.add).then_inc(c_red, 1)
                    v.wait_ge(c_sq, blk + 1)
                    v.tensor_reduce(lie[:, 1, bass.ds(blk * GPB, GPB), :], q2[:].rearrange("p g (h d) -> p g h d", d=D0),
                                    AX_X, ALU.add).then_inc(c_red, 1)

        with ExitStack() as ph:
            W = [P, GROUPS, S]
            norm = sb(ph, "norm", [P, GROUPS, H0])
            inv = sb(ph, "inv", [P, GROUPS, H0])
            sim = sb(ph, "sim", [P, 4, GROUPS])
            ends = sb(ph, "ends", [P, 4])
            small = sb(ph, "small", [2, 4])
            spread = sb(ph, "spread", W)
            seen = sb(ph, "seen", W)
            t_ps = ps(ph, "ends_ps", [2, P])
            e_ps = ps(ph, "span_ps", [P, 2])
            key_ps = ps(ph, "key_ps", [P, GROUPS * S])
            n_step, n_root, n_pe = sem("n_step"), sem("n_root"), sem("n_pe")
            n_ends, n_small, n_spread = sem("n_ends"), sem("n_small"), sem("n_spread")
            block = ph.enter_context(nc.Block())

            @block.scalar
            def _(eng):
                act.activation(norm[:], lie[:, 1], ACT.Sqrt).then_inc(n_root, 1)

            @block.tensor
            def _(pe):
                pe.wait_ge(n_ends, 1)
                pe.transpose(t_ps[:], ends[:, 0:2], ident).then_inc(n_pe, 1)
                pe.wait_ge(n_small, 1)
                pe.matmul(e_ps[:], ones[0:2, :], small[:, 2:4], start=True, stop=True).then_inc(n_pe, 1)
                pe.wait_ge(n_spread, 1)
                for n in range(2):
                    ins_ = pe.matmul(key_ps[:, n * BLK:(n + 1) * BLK], c("same_seq"),
                                     spread[:, n * 16:(n + 1) * 16, :], start=True, stop=True)
                ins_.then_inc(n_pe, 1)

            @block.vector
            def _(eng):
                count = [0]

                def done(ins_):
                    count[0] += 1
                    ins_.then_inc(n_step, 1)
                    v.wait_ge(n_step, count[0])

                def over_k(a):
                    return a.unsqueeze(2).to_broadcast(W)

                def over_g(a):
                    return a.unsqueeze(1).to_broadcast(W)

                v.wait_ge(n_root, 1)
                done(v.reciprocal(inv[:], norm[:]))
                done(v.tensor_tensor(inv[:], inv[:], lie[:, 0], ALU.mult))
                done(v.tensor_reduce(sim[:, 0, :], inv[:], AX_X, ALU.add))
                done(v.tensor_scalar(sim[:, 0, :], sim[:, 0, :], 1.0 / H0, None, ALU.mult))
                done(v.tensor_scalar(ends[:, 2:3], c("is_reg_row"), -BIG, None, ALU.mult))
                v.tensor_scalar(sim[:, 1, :], sim[:, 0, :], ends[:, 2:3], None, ALU.add)
                done(v.tensor_scalar(sim[:, 2, :], sim[:, 0, :], -1.0, ends[:, 2:3], ALU.mult, ALU.add))
                v.tensor_reduce(ends[:, 0:2], sim[:, 1:3, :], AX_X, ALU.max).then_inc(n_ends, 1)
                v.wait_ge(n_pe, 1)
                done(v.tensor_reduce(small[:, 0:1], t_ps[:], AX_X, ALU.max))
                v.tensor_scalar(small[:, 2:4], ident[0:2, 0:2], small[:, 0:1], None, ALU.mult).then_inc(n_small, 1)
                v.wait_ge(n_pe, 2)
                done(v.tensor_copy(ends[:, 0:2], e_ps[:]))
                done(v.tensor_tensor(ends[:, 2:3], ends[:, 0:1], ends[:, 1:2], ALU.add))
                done(v.reciprocal(ends[:, 3:4], ends[:, 2:3]))
                done(v.tensor_scalar(sim[:, 1, :], sim[:, 0, :], ends[:, 1:2], ends[:, 3:4], ALU.add, ALU.mult))
                done(v.tensor_scalar(sim[:, 2, :], sim[:, 1, :], 0.9, None, ALU.is_gt))
                done(v.tensor_scalar(sim[:, 3, :], sim[:, 2, :], c("is_reg_row"), None, ALU.max))
                v.tensor_tensor(spread[:], over_k(sim[:, 3, :]), over_g(c("own")), ALU.mult).then_inc(n_spread, 1)
                v.wait_ge(n_pe, 3)
                keys = key_ps[:].rearrange("p (g k) -> p g k", k=S)
                v.tensor_scalar(spread[:], keys, -1.0, 1.0, ALU.mult, ALU.add)
                done(v.tensor_tensor(seen[:], keys, over_k(sim[:, 3, :]), ALU.is_equal))
                v.tensor_tensor(spread[:], spread[:], over_g(c("is_reg_key")), ALU.max)
                done(v.tensor_tensor(seen[:], seen[:], over_g(c("is_reg_key")), ALU.max))
                done(v.tensor_scalar(class_mask[:, :, HPG, :], spread[:], BIG, -BIG, ALU.mult, ALU.add))
                for h in range(HPG):
                    ins_ = v.tensor_scalar(class_mask[:, :, h, :], seen[:], BIG, -BIG, ALU.mult, ALU.add)
                done(ins_)
        pooling.close()
        similar.close()

        def block_of(i, j, lag):
            return 2 * i + (j - lag) // GPB

        def attention(ph, tag, parts, masked):
            cols = parts * S
            score_steps = 2 if masked else 1
            banks = 2 if cols > BLK else 1
            t = dict(
                s_ps=[ps(ph, f"{tag}_s_ps{r}", [P, banks, BLK]) for r in range(2)],
                o_ps=ps(ph, f"{tag}_o_ps", [P, 2, BLK]),
                rows=sb(ph, f"{tag}_rows", [P, 4, cols]),
                stat=sb(ph, f"{tag}_stat", [P, 4, 3, parts]),
                prob=sb(ph, f"{tag}_prob", [P, 2, cols]),
                o_sb=sb(ph, f"{tag}_o_sb", [P, 2, SPB, 4, S]),
                x_ps=ps(ph, f"{tag}_x_ps", [P, 2 if masked else 1, BLK]),
            )
            names = ("scored", "turned", "masked", "topped", "shifted", "exped", "summed", "inverted",
                     "shared", "scaled", "turned_back", "merged", "weighed_half", "weighed", "kept", "projected", "added")
            g = {n: sem(f"{tag}_{n}") for n in names}

            def half_cols(a):
                return a.rearrange("p (b c) -> p b c", b=banks)

            def turn(n, r):
                v.wait_ge(g["scored"], score_steps * (n + 1))
                after(v, g["turned_back"], n - 3)
                v.transpose(half_cols(t["rows"][:, r % 4, :]), t["s_ps"][r % 2][:, :, 0:cols // banks]).then_inc(g["turned"], 1)

            def mask(n, r):
                pool.wait_ge(g["turned"], n + 1)
                rows = t["rows"][:, r % 4, :].rearrange("p (g c) -> p g c", g=HG)
                pool.tensor_tensor(rows, rows, class_mask[:, n, :, :].rearrange("p s k -> p (s k)").unsqueeze(1)
                                   .to_broadcast([P, HG, QX]), ALU.add).then_inc(g["masked"], 1)

            def top(n, r):
                v.wait_ge(g["masked" if masked else "turned"], n + 1)
                v.tensor_reduce(t["stat"][:, r % 4, 0, :], t["rows"][:, r % 4, :].rearrange("p (s k) -> p s k", k=S),
                                AX_X, ALU.max).then_inc(g["topped"], 1)

            def per_row(n, r, which, op, after, signal):
                pool.wait_ge(g[after], n + 1)
                rows = t["rows"][:, r % 4, :].rearrange("p (s k) -> p s k", k=S)
                pool.tensor_tensor(rows, rows, t["stat"][:, r % 4, which, :].unsqueeze(2).to_broadcast([P, parts, S]),
                                   op).then_inc(g[signal], 1)

            def shift(n, r):
                per_row(n, r, 0, ALU.subtract, "topped", "shifted")

            def scale(n, r):
                per_row(n, r, 2, ALU.mult, "shared" if masked else "inverted", "scaled")

            def exp(n, r):
                act.wait_ge(g["shifted"], n + 1)
                act.activation(t["rows"][:, r % 4, :], t["rows"][:, r % 4, :], ACT.Exp).then_inc(g["exped"], 1)

            def total(n, r):
                st = t["stat"][:, r % 4]
                v.wait_ge(g["exped"], n + 1)
                v.tensor_reduce(st[:, 1, :], t["rows"][:, r % 4, :].rearrange("p (s k) -> p s k", k=S),
                                AX_X, ALU.add).then_inc(g["summed"], 1)
                v.wait_ge(g["summed"], n + 1)
                v.reciprocal(st[:, 2, :], st[:, 1, :]).then_inc(g["inverted"], 1)
                if masked:
                    v.wait_ge(g["inverted"], n + 1)
                    v.tensor_tensor(st[:, 2, :], st[:, 2, :], c("share"), ALU.mult).then_inc(g["shared"], 1)

            def turn_back(n, r):
                v.wait_ge(g["scaled"], n + 1)
                v.wait_ge(g["weighed"], 2 * n + 1)
                v.transpose(t["prob"][:, r % 2, :], t["rows"][:, r % 4, :]).then_inc(g["turned_back"], 1)
                if masked:
                    v.wait_ge(g["turned_back"], n + 1)
                    pr = t["prob"][:, r % 2, :].rearrange("p (g c) -> p g c", g=HG)
                    first = pr[:, :, 0:HPG * S].rearrange("p g (h q) -> p g h q", q=S)[:, :, :, 0:REG]
                    second = pr[:, :, HPG * S:HPG * S + HPG * REG].rearrange("p g (h q) -> p g h q", q=REG)
                    v.tensor_tensor(first, first, second, ALU.add).then_inc(g["merged"], 1)

            def weigh(pe, n, r, values, width):
                pe.wait_ge(g["merged" if masked else "turned_back"], n + 1)
                wait_apart(pe, g["kept"], n)
                for turn_, s in enumerate((0, 2, 1, 3)):
                    rows = slice(32 * s, 32 * s + 32)
                    if turn_ >= 2:
                        wait_apart(pe, g["weighed_half"], 2 * n + turn_ - 1)
                    for m in range(4):
                        ins_ = pe.matmul(t["o_ps"][32 * m:32 * m + 32, s // 2, (s % 2) * P:(s % 2) * P + P],
                                         values(rows, m), t["prob"][rows, r % 2, m * width:m * width + 4 * S],
                                         start=True, stop=True)
                    ins_.then_inc(g["weighed_half" if turn_ < 2 else "weighed"], 1)

            def keep(n, blk, r):
                act.wait_ge(g["weighed"], 2 * n + 5)
                act.wait_ge(g["projected"], blk + 1)
                dst = t["o_sb"][:, (r // GPB) % 2, 4 * (r % GPB):4 * (r % GPB) + 4, :, :].rearrange("p s h q -> p (s h q)")
                act.activation(dst.rearrange("p (b c) -> p b c", b=2), t["o_ps"][:, :, 0:2 * P], ACT.Copy).then_inc(g["kept"], 1)

            def project(pe, blk, r, weights):
                half = (r // GPB) % 2
                x_bank = t["x_ps"][:, half if masked else 0, :]
                pe.wait_ge(g["kept"], GPB * (blk + 1))
                pe.wait_ge(g["added"], blk + 1)
                for h in range(4):
                    ins_ = pe.matmul(x_bank, weights[:, h, :], t["o_sb"][:, half, :, h, :], start=(h == 0), stop=(h == 3))
                ins_.then_inc(g["projected"], 1)

            t.update(g)
            t.update(turn=turn, mask=mask, top=top, shift=shift, scale=scale, exp=exp, total=total,
                     turn_back=turn_back, weigh=weigh, keep=keep, project=project)
            return t

        L_SCORE, L_TOP, L_SUM, L_BACK, L_ADD = 4, 5, 6, 7, 8

        def softmax_on_vector(t, i, j, live):
            if live(L_SCORE):
                t["turn"](SLOTS * i + j - L_SCORE, j - L_SCORE)
            if live(L_BACK):
                t["turn_back"](SLOTS * i + j - L_BACK, j - L_BACK)
            if live(L_SUM):
                t["total"](SLOTS * i + j - L_SUM, j - L_SUM)
            if live(L_TOP):
                t["top"](SLOTS * i + j - L_TOP, j - L_TOP)

        def softmax_on_pool(t, i, j, live, masked):
            if masked and live(L_SCORE):
                t["mask"](SLOTS * i + j - L_SCORE, j - L_SCORE)
            if live(L_SUM):
                t["scale"](SLOTS * i + j - L_SUM, j - L_SUM)
            if live(L_TOP):
                t["shift"](SLOTS * i + j - L_TOP, j - L_TOP)

        def softmax_on_scalar(t, i, j, live):
            if live(L_TOP):
                t["exp"](SLOTS * i + j - L_TOP, j - L_TOP)
            if live(L_BACK):
                t["keep"](SLOTS * i + j - L_BACK, block_of(i, j, L_BACK), j - L_BACK)

        with ExitStack() as ph:
            k_st = sb(ph, "k_st", [P, 2, BLK])
            v_st = sb(ph, "v_st", [P, 2, GPB, C])
            q_x = sb(ph, "q_x", [P, 2, SPB, QX])
            head_scale = sb(ph, "head_scale", [P, HPG])
            t = attention(ph, "d", HG * (HPG + 1), masked=True)
            d_k, d_v = [sem("d_k0"), sem("d_k1")], [sem("d_v0"), sem("d_v1")]
            d_q, d_clear, d_half = sem("d_q"), sem("d_clear"), sem("d_half")
            block = ph.enter_context(nc.Block())

            @block.sync
            def _(sp):
                def stage(blk, half):
                    if not isinstance(blk, int):
                        sp.wait_ge(t["weighed"], 2 * GPB * (blk - 1) + 3)
                    sp.dma_start(k_st[:, half, :], k_f[:, bass.ds(blk * BLK, BLK)]).then_inc(d_k[half], 16)
                    sp.dma_start(v_st[:, half], v_t[:, bass.ds(blk * GPB, GPB), :]).then_inc(d_v[half], 16)

                for i, half in blocks(sp):
                    stage(2 * i + half, half)

            @block.tensor
            def _(pe):
                pe.sem_inc(t["projected"], 2)
                pe.sem_inc(t["weighed"], 3)
                for i, j, live in slots(pe, L_ADD):
                    if live(L_SCORE):
                        n, r = SLOTS * i + j - L_SCORE, (j - L_SCORE) % SLOTS
                        blk, half, g = block_of(i, j, L_SCORE), r // GPB, r % GPB
                        if g == 0:
                            pe.wait_ge(d_q, GPB * (blk + 1))
                            pe.wait_ge(d_k[half], 16 * (i if j >= L_SCORE else i - 1) + 16)
                        wait_apart(pe, t["turned"], n - 1)
                        for turn_, m in enumerate((0, 2, 1, 3)):
                            rows = slice(32 * m, 32 * m + 32)
                            if turn_ >= 2:
                                wait_apart(pe, d_half, 2 * n + turn_ - 1)
                            for s in range(SEQ):
                                ins_ = pe.matmul(t["s_ps"][r % 2][32 * s:32 * s + 32, m // 2, (m % 2) * QX:(m % 2) * QX + QX],
                                                 k_st[rows, half, g * P + 32 * s:g * P + 32 * s + 32],
                                                 q_x[rows, half, g * SEQ + s, :], start=True, stop=True)
                            ins_.then_inc(d_half if turn_ < 2 else t["scored"], 1)
                    if live(L_BACK):
                        n, r = SLOTS * i + j - L_BACK, (j - L_BACK) % SLOTS
                        if r % GPB == 0:
                            pe.wait_ge(d_v[r // GPB], 16 * (i if j >= L_BACK else i - 1) + 16)
                        t["weigh"](pe, n, r, lambda rows, m, r=r: v_st[rows, r // GPB, r % GPB, 32 * m:32 * m + 32], QX)
                    if live(L_ADD) and (j - L_ADD) % GPB == GPB - 1:
                        t["project"](pe, block_of(i, j, L_ADD), (j - L_ADD) % SLOTS, wproj_h)

            @block.gpsimd
            def _(eng):
                pool.memset(q_x[:], 0.0).then_inc(d_clear, 1)
                for i, j, live in slots(pool, L_ADD):
                    softmax_on_pool(t, i, j, live, True)

            @block.scalar
            def _(eng):
                for i, j, live in slots(act, L_ADD):
                    softmax_on_scalar(t, i, j, live)

            @block.vector
            def _(eng):
                v.tensor_scalar(head_scale[:], c("head_row"), float(D0) ** -0.5, None, ALU.mult).then_inc(d_clear, 1)
                v.wait_ge(d_clear, 2)
                v.sem_inc(t["added"], 2)
                for i, j, live in slots(v, L_ADD):
                    softmax_on_vector(t, i, j, live)
                    if live(0):
                        blk, half, h = 2 * i + j // GPB, j // GPB, j % GPB
                        if h == 0:
                            after(v, t["scored"], 2 * GPB * (blk - 1))
                        q = q_f[:, bass.ds(blk * BLK, BLK)].rearrange("p (s q) -> p s q", q=S)
                        v.tensor_scalar(q_x[:, half, :, h * S:(h + 1) * S], q, head_scale[:, h:h + 1], None, ALU.mult)
                        v.tensor_scalar(q_x[:, half, :, HPG * S + h * REG:HPG * S + (h + 1) * REG], q[:, :, 0:REG],
                                        head_scale[:, h:h + 1], None, ALU.mult).then_inc(d_q, 1)
                    if live(L_ADD) and (j - L_ADD) % GPB == GPB - 1:
                        blk = block_of(i, j, L_ADD)
                        v.wait_ge(t["projected"], blk + 3)
                        xs = x_f[:, bass.ds(blk * BLK, BLK)]
                        v.scalar_tensor_tensor(out=xs, in0=t["x_ps"][:, ((j - L_ADD) // GPB) % 2, :],
                                               scalar=bproj[:, 0:1], in1=xs, op0=ALU.add, op1=ALU.add).then_inc(t["added"], 1)
        layer0.close()

        layer1 = top.enter_context(ExitStack())
        y_f = sb(layer1, "y_f", [P, TOK])
        yn_f = sb(layer1, "yn_f", [P, TOK])

        with ExitStack() as ph:
            x_st = sb(ph, "x_st", [P, 2, BLK])
            w_st = sb(ph, "w_st", [P, 2, SEQ, C])
            subject = sb(ph, "subject", [1, B], I32)
            subject_w = sb(ph, "subject_w", [SUBJ, B], I32)
            subject_f = sb(ph, "subject_f", [SUBJ, B])
            is_subject = sb(ph, "is_subject", [SUBJ, B, S])
            is_st = sb(ph, "is_st", [SUBJ, 2, BLK])
            rank = sb(ph, "rank", [SUBJ, 1])
            bias = sb(ph, "bias", [SUBJ, C])
            y_t = sb(ph, "y_t", [P, 2, GPB, C])
            yn_t = sb(ph, "yn_t", [P, 2, GPB, C])
            junk = sb(ph, "junk", [P, C])
            sq = sb(ph, "sq", [P, 2, 3, GPB])
            y_ps = [ps(ph, f"y_ps{r}", [P, BLK]) for r in range(2)]
            yt_ps = [ps(ph, f"yt_ps{r}", [P, BLK]) for r in range(2)]
            nt_ps = [ps(ph, f"nt_ps{r}", [P, BLK]) for r in range(2)]
            e_ld, e_x, e_is = sem("e_ld"), [sem("e_x0"), sem("e_x1")], [sem("e_is0"), sem("e_is1")]
            e_ready, e_w, e_w2, e_y, e_yc, e_sq, e_ms, e_rt, e_inv, e_yn = (
                sem(n) for n in ("e_ready", "e_w", "e_w2", "e_y", "e_yc", "e_sq", "e_ms", "e_rt", "e_inv", "e_yn"))
            e_yt, e_nt, e_ytc, e_ntc, e_bias = (sem(n) for n in ("e_yt", "e_nt", "e_ytc", "e_ntc", "e_bias"))
            block = ph.enter_context(nc.Block())

            @block.sync
            def _(sp):
                sp.dma_start(subject[:], ins["itok_B_0_7"].rearrange("(a b) -> a b", a=1)).then_inc(e_ld, 16)
                sp.dma_start(subject_w[:], ins["itok_B_0_7"].partition_broadcast(SUBJ)).then_inc(e_ld, 16)
                sp.dma_start(bias[:], ins["L1_cond_bias"]).then_inc(e_ld, 16)
                sp.wait_ge(e_ready, 3)

                def stage(blk, half):
                    after(sp, e_y, GPB * (blk - 1))
                    sp.dma_start(x_st[:, half, :], x_f[:, bass.ds(blk * BLK, BLK)]).then_inc(e_x[half], 16)
                    sp.dma_start(is_st[:, half, :], is_subject[:].rearrange("p b s -> p (b s)")[:, bass.ds(blk * BLK, BLK)])\
                        .then_inc(e_is[half], 16)

                for i, half in blocks(sp):
                    stage(2 * i + half, half)

            def fetch(eng, copy, n, r, seqs, signal):
                for s in seqs:
                    which = eng.value_load(subject[0:1, bass.ds(n * SEQ + s, 1)], min_val=0, max_val=SUBJ - 1)
                    ins_ = copy(w_st[:, r % 2, s, :], w_subj_t[:, bass.ds(which, 1), :].rearrange("p a o -> p (a o)"))
                ins_.then_inc(signal, 1)

            @block.gpsimd
            def _(eng):
                pool.iota(rank[:], [[0, 1]], base=0, channel_multiplier=1, allow_small_or_imprecise_dtypes=True).then_inc(e_ready, 1)

            @block.tensor
            def _(pe):
                pe.wait_ge(e_ready, 3)
                for i, j, live in slots(pe, 4):
                    if live(0):
                        n, g, half = SLOTS * i + j, j % GPB, j // GPB
                        if g == 0:
                            pe.wait_ge(e_x[half], 16 * i + 16)
                            pe.wait_ge(e_is[half], 16 * i + 16)
                        after(pe, e_yc, n - 1)
                        after(pe, e_sq, n - 1)
                        y = y_ps[j % 2]
                        pe.matmul(y[:, 0:C], is_st[:, half, g * P:(g + 1) * P], bias[:], start=True, stop=False,
                                  skip_group_check=True).then_inc(e_bias, 1)
                        pe.wait_ge(e_w, n + 1)
                        pe.wait_ge(e_w2, n + 1)
                        pe.wait_ge(e_bias, n + 1)
                        for s in range(SEQ):
                            ins_ = pe.matmul(y[32 * s:32 * s + 32, 0:C], x_st[:, half, g * P + 32 * s:g * P + 32 * s + 32],
                                             w_st[:, j % 2, s, :], start=False, stop=True, skip_group_check=True)
                        ins_.then_inc(e_y, 1)
                    if live(4) and j % GPB == GPB - 1:
                        blk, half = block_of(i, j, 4), ((j - 4) // GPB) % 2
                        pe.wait_ge(e_yc, GPB * (blk + 1))
                        after(pe, e_ytc, blk)
                        after(pe, e_ntc, blk)
                        for g in range(GPB):
                            ins_ = pe.transpose(yt_ps[half][:, g * P:(g + 1) * P], y_t[:, half, g, :], ident)
                        ins_.then_inc(e_yt, 1)
                        pe.wait_ge(e_yn, blk + 1)
                        for g in range(GPB):
                            ins_ = pe.transpose(nt_ps[half][:, g * P:(g + 1) * P], yn_t[:, half, g, :], ident)
                        ins_.then_inc(e_nt, 1)

            @block.scalar
            def _(eng):
                act.wait_ge(e_ld, 48)
                for i, j, live in slots(act, 4):
                    if live(0):
                        n, g, half = SLOTS * i + j, j % GPB, j // GPB
                        after(act, e_y, n - 1)
                        fetch(act, lambda o, a: act.activation(o, a, ACT.Copy), n, j, (0, 1), e_w)
                        act.wait_ge(e_y, n + 1)
                        act.activation(junk[:], y_ps[j % 2][:, 0:C], ACT.Square, accum_out=sq[:, half, 0, g:g + 1]).then_inc(e_sq, 1)
                        if g == GPB - 1:
                            blk = block_of(i, j, 0)
                            act.wait_ge(e_ms, blk + 1)
                            act.activation(sq[:, half, 2, :], sq[:, half, 1, :], ACT.Sqrt).then_inc(e_rt, 1)
                    if live(4) and j % GPB == GPB - 1:
                        blk, half = block_of(i, j, 4), ((j - 4) // GPB) % 2
                        act.wait_ge(e_yt, blk + 1)
                        act.activation(y_f[:, bass.ds(blk * BLK, BLK)], yt_ps[half][:], ACT.Copy).then_inc(e_ytc, 1)

            @block.vector
            def _(eng):
                v.wait_ge(e_ld, 48)
                v.wait_ge(e_ready, 1)
                v.tensor_copy(subject_f[:], subject_w[:]).then_inc(e_ready, 1)
                v.wait_ge(e_ready, 2)
                v.tensor_scalar(is_subject[:], subject_f[:].unsqueeze(2).to_broadcast([SUBJ, B, S]), rank[:, 0:1], None,
                                ALU.is_equal).then_inc(e_ready, 1)
                for i, j, live in slots(v, 4):
                    if live(0):
                        n, g, half = SLOTS * i + j, j % GPB, j // GPB
                        after(v, e_y, n - 1)
                        fetch(v, v.tensor_copy, n, j, (2, 3), e_w2)
                        v.wait_ge(e_sq, n + 1)
                        if g == 0:
                            after(v, e_yt, block_of(i, j, 8) + 1)
                        v.tensor_copy(y_t[:, half, g, :], y_ps[j % 2][:, 0:C]).then_inc(e_yc, 1)
                        if g == GPB - 1:
                            blk = block_of(i, j, 0)
                            v.tensor_scalar(sq[:, half, 1, :], sq[:, half, 0, :], 1.0 / C, EPS, ALU.mult, ALU.add).then_inc(e_ms, 1)
                            v.wait_ge(e_rt, blk + 1)
                            v.reciprocal(sq[:, half, 1, :], sq[:, half, 2, :]).then_inc(e_inv, 1)
                            v.wait_ge(e_inv, blk + 1)
                            v.wait_ge(e_yc, GPB * (blk + 1))
                            after(v, e_nt, blk - 1)
                            v.tensor_tensor(yn_t[:, half], y_t[:, half], sq[:, half, 1, :].unsqueeze(2).to_broadcast([P, GPB, C]),
                                            ALU.mult).then_inc(e_yn, 1)
                    if live(4) and j % GPB == GPB - 1:
                        blk, half = block_of(i, j, 4), ((j - 4) // GPB) % 2
                        v.wait_ge(e_nt, blk + 1)
                        v.tensor_copy(yn_f[:, bass.ds(blk * BLK, BLK)], nt_ps[half][:]).then_inc(e_ntc, 1)

        with ExitStack() as ph:
            y_st = sb(ph, "y_st", [P, 2, BLK])
            q_h = sb(ph, "q_h", [P, 2, SPB, H1, S])
            k_h = sb(ph, "k_h", [P, 2, BLK])
            k_tmp = sb(ph, "k_tmp", [64, BLK])
            lat = sb(ph, "lat", [P, 2, GPB, S])
            q_ps = [ps(ph, f"q_ps{r}", [P, BLK]) for r in range(2)]
            kv_ps = ps(ph, "kv_ps", [P, BLK])
            t = attention(ph, "f", H1, masked=False)
            f_y = [sem("f_y0"), sem("f_y1")]
            f_const, f_q, f_qt, f_ka, f_kb, f_kl, f_kac, f_kt, f_kbc, f_klc = (
                sem(n) for n in ("f_const", "f_q", "f_qt", "f_ka", "f_kb", "f_kl", "f_kac", "f_kt", "f_kbc", "f_klc"))
            block = ph.enter_context(nc.Block())

            @block.sync
            def _(sp):
                def stage(blk, half):
                    after(sp, f_q, H1 * (blk - 1))
                    after(sp, f_kl, blk - 1)
                    sp.dma_start(y_st[:, half, :], yn_f[:, bass.ds(blk * BLK, BLK)]).then_inc(f_y[half], 16)

                for i, half in blocks(sp):
                    stage(2 * i + half, half)

            @block.tensor
            def _(pe):
                pe.sem_inc(t["projected"], 2)
                pe.sem_inc(t["weighed"], 3)
                for i, j, live in slots(pe, L_ADD):
                    if live(L_SCORE):
                        n, r = SLOTS * i + j - L_SCORE, (j - L_SCORE) % SLOTS
                        blk, half, g = block_of(i, j, L_SCORE), r // GPB, r % GPB
                        if g == 0:
                            pe.wait_ge(f_qt, H1 * (blk + 1))
                            pe.wait_ge(f_kbc, blk + 1)
                            pe.wait_ge(f_const, 2)
                        after(pe, t["turned"], n - 1)
                        for s in range(SEQ):
                            ins_ = pe.matmul(t["s_ps"][r % 2][32 * s:32 * s + 32, 0, :], k_h[:, half, g * P + 32 * s:g * P + 32 * s + 32],
                                             q_h[:, half, g * SEQ + s, :, :], start=True, stop=True)
                        ins_.then_inc(t["scored"], 1)
                    if live(L_BACK):
                        n, r = SLOTS * i + j - L_BACK, (j - L_BACK) % SLOTS
                        if r % GPB == 0:
                            pe.wait_ge(f_klc, block_of(i, j, L_BACK) + 1)
                        t["weigh"](pe, n, r, lambda rows, m, r=r: lat[rows, r // GPB, r % GPB, :], 4 * S)
                    if live(L_ADD) and (j - L_ADD) % GPB == GPB - 1:
                        t["project"](pe, block_of(i, j, L_ADD), (j - L_ADD) % SLOTS, w_o)
                    if live(0):
                        blk, half, g = block_of(i, j, 0), j // GPB, j % GPB
                        if g == 0:
                            pe.wait_ge(f_y[half], 16 * i + 16)
                            after(pe, f_klc, blk)
                            pe.matmul(kv_ps[0:96, :], wk_a[:], y_st[:, half, :], start=True, stop=True).then_inc(f_ka, 1)
                        if g == 1:
                            pe.wait_ge(f_kac, blk + 1)
                            pe.matmul(kv_ps[0:64, :], wk_b[:], y_st[:, half, :], start=True, stop=True).then_inc(f_kb, 1)
                        if g == 2:
                            pe.wait_ge(f_kt, blk + 1)
                            for m in range(GPB):
                                ins_ = pe.matmul(kv_ps[:, m * S:(m + 1) * S], y_st[:, half, m * P:(m + 1) * P], w_lat[:],
                                                 start=True, stop=True)
                            ins_.then_inc(f_kl, 1)
                        for h in range(4 * g, 4 * g + 4):
                            after(pe, f_qt, blk * H1 + h - 1)
                            pe.matmul(q_ps[h % 2][0:96, :], wq_heads[:, h, :], y_st[:, half, :], start=True, stop=True).then_inc(f_q, 1)

            @block.gpsimd
            def _(eng):
                for half in range(2):
                    ins_ = pool.tensor_copy(q_h[96:128, half].rearrange("p s h q -> p (s h) q"),
                                            c("causal")[96:128, :].unsqueeze(1).to_broadcast([S, SPB * H1, S]))
                ins_.then_inc(f_const, 1)
                ins_ = pool.tensor_copy(k_h[96:128].rearrange("p a (s k) -> p (a s) k", k=S),
                                        c("own")[96:128, :].unsqueeze(1).to_broadcast([S, 2 * SPB, S])).then_inc(f_const, 1)
                for i, j, live in slots(pool, L_ADD):
                    softmax_on_pool(t, i, j, live, False)

            @block.scalar
            def _(eng):
                for i, j, live in slots(act, L_ADD):
                    softmax_on_scalar(t, i, j, live)
                    if live(0) and j % GPB == 2:
                        blk, half = block_of(i, j, 0), j // GPB
                        act.wait_ge(f_kl, blk + 1)
                        if not isinstance(blk, int):
                            act.wait_ge(t["weighed"], 2 * GPB * (blk - 1) + 3)
                        act.activation(lat[:, half].rearrange("p g r -> p (g r)"), kv_ps[:, 0:GPB * S], ACT.Copy).then_inc(f_klc, 1)

            @block.vector
            def _(eng):
                def over_s(a):
                    return a.unsqueeze(1).to_broadcast([a.shape[0], SPB, S])

                def by_s(a):
                    return a.rearrange("p (s q) -> p s q", q=S)

                v.sem_inc(t["added"], 1)
                for i, j, live in slots(v, L_ADD):
                    softmax_on_vector(t, i, j, live)
                    if live(0):
                        blk, half, g = block_of(i, j, 0), j // GPB, j % GPB
                        if g == 0:
                            after(v, t["scored"], GPB * (blk - 1))
                            v.wait_ge(f_ka, blk + 1)
                            v.tensor_tensor(by_s(k_h[0:96, half, :]), by_s(kv_ps[0:96, :]), over_s(c("k_turn")[0:96, :]),
                                            ALU.mult).then_inc(f_kac, 1)
                        if g == 1:
                            v.wait_ge(f_kb, blk + 1)
                            after(v, f_kbc, blk)
                            v.tensor_tensor(by_s(k_tmp[:]), by_s(kv_ps[0:64, :]), over_s(c("k_cross")[0:64, :]), ALU.mult).then_inc(f_kt, 1)
                            v.wait_ge(f_kt, blk + 1)
                            v.wait_ge(f_kac, blk + 1)
                            v.tensor_tensor(k_h[0:64, half, :], k_h[0:64, half, :], k_tmp[:], ALU.add).then_inc(f_kbc, 1)
                        for h in range(4 * g, 4 * g + 4):
                            v.wait_ge(f_q, blk * H1 + h + 1)
                            v.tensor_tensor(q_h[0:96, half, :, h, :], by_s(q_ps[h % 2][0:96, :]), over_s(c("q_turn")[0:96, :]),
                                            ALU.mult).then_inc(f_qt, 1)
                    if live(L_ADD) and (j - L_ADD) % GPB == GPB - 1:
                        blk = block_of(i, j, L_ADD)
                        v.wait_ge(t["projected"], blk + 3)
                        ys = y_f[:, bass.ds(blk * BLK, BLK)]
                        v.tensor_tensor(ys, t["x_ps"][:, 0, :], ys, ALU.add).then_inc(t["added"], 1)

        moe = top.enter_context(ExitStack())
        logits = sb(moe, "logits", [P, GROUPS, E])
        comb_t = sb(moe, "comb_t", [3 * (E + 1), TOK], BF16)
        z_f = yn_f
        with ExitStack() as ph:
            z_st = sb(ph, "z_st", [P, 2, BLK])
            z2 = sb(ph, "z2", [P, BLK])
            ms = sb(ph, "ms", [P, 3, GPB])
            diag = sb(ph, "diag", [P, GPB, P])
            l_ps = ps(ph, "l_ps", [P, GPB, 16])
            r_ps = ps(ph, "r_ps", [P, BLK])
            g_z = [sem("g_z0"), sem("g_z1")]
            g_sq, g_l, g_ms, g_rt, g_inv, g_lm, g_lb, g_dg, g_r, g_zn, g_sum = (
                sem(n) for n in ("g_sq", "g_l", "g_ms", "g_rt", "g_inv", "g_lm", "g_lb", "g_dg", "g_r", "g_zn", "g_sum"))
            block = ph.enter_context(nc.Block())

            @block.sync
            def _(sp):
                def stage(blk, half):
                    after(sp, g_zn, blk - 1)
                    after(sp, g_sum, blk - 1)
                    sp.dma_start(z_st[:, half, :], y_f[:, bass.ds(blk * BLK, BLK)]).then_inc(g_z[half], 16)

                for i, half in blocks(sp):
                    stage(2 * i + half, half)

            @block.gpsimd
            def _(eng):
                for i, half in blocks(pool):
                    blk = 2 * i + half
                    pool.wait_ge(g_z[half], 16 * i + 16)
                    xs = x_f[:, bass.ds(blk * BLK, BLK)]
                    pool.tensor_tensor(xs, xs, z_st[:, half, :], ALU.add).then_inc(g_sum, 1)

            @block.scalar
            def _(eng):
                for i, half in blocks(act):
                    blk = 2 * i + half
                    act.wait_ge(g_z[half], 16 * i + 16)
                    after(act, g_l, blk)
                    act.activation(z2[:], z_st[:, half, :], ACT.Square).then_inc(g_sq, 1)
                    act.wait_ge(g_ms, blk + 1)
                    act.activation(ms[:, 1, :], ms[:, 0, :], ACT.Sqrt).then_inc(g_rt, 1)

            @block.tensor
            def _(pe):
                for i, half in blocks(pe):
                    blk = 2 * i + half
                    pe.wait_ge(g_z[half], 16 * i + 16)
                    after(pe, g_lm, blk)
                    after(pe, g_ms, blk)
                    for g in range(GPB):
                        pe.matmul(l_ps[:, g, 0:E], z_st[:, half, g * P:(g + 1) * P], wgate[:], start=True, stop=True)
                    pe.wait_ge(g_sq, blk + 1)
                    for g in range(GPB):
                        ins_ = pe.matmul(l_ps[:, g, E:E + 1], z2[:, g * P:(g + 1) * P], ones[:, 0:1], start=True, stop=True)
                    ins_.then_inc(g_l, 1)
                    pe.wait_ge(g_dg, blk + 1)
                    after(pe, g_zn, blk)
                    pe.matmul(r_ps[:], ones[:], diag[:].rearrange("p g t -> p (g t)"), start=True, stop=True).then_inc(g_r, 1)

            @block.vector
            def _(eng):
                for i, half in blocks(v):
                    blk = 2 * i + half
                    lg = logits[:, bass.ds(blk * GPB, GPB), :]
                    v.wait_ge(g_l, blk + 1)
                    after(v, g_rt, blk)
                    v.tensor_scalar(ms[:, 0, :], l_ps[:, :, E], 1.0 / C, EPS, ALU.mult, ALU.add).then_inc(g_ms, 1)
                    v.wait_ge(g_rt, blk + 1)
                    v.reciprocal(ms[:, 2, :], ms[:, 1, :]).then_inc(g_inv, 1)
                    v.wait_ge(g_inv, blk + 1)
                    v.tensor_tensor(lg, l_ps[:, :, 0:E], ms[:, 2, :].unsqueeze(2).to_broadcast([P, GPB, E]), ALU.mult).then_inc(g_lm, 1)
                    after(v, g_r, blk)
                    for g in range(GPB):
                        ins_ = v.tensor_scalar(diag[:, g, :], ident, ms[:, 2, g:g + 1], None, ALU.mult)
                    ins_.then_inc(g_dg, 1)
                    v.wait_ge(g_lm, blk + 1)
                    v.tensor_tensor(lg, lg, gate_b[:].unsqueeze(1).to_broadcast([P, GPB, E]), ALU.add).then_inc(g_lb, 1)
                    v.wait_ge(g_r, blk + 1)
                    v.tensor_tensor(z_f[:, bass.ds(blk * BLK, BLK)], z_st[:, half, :], r_ps[:], ALU.mult).then_inc(g_zn, 1)

        with ExitStack() as ph:
            W = [P, GROUPS, E]
            best = sb(ph, "best", W)
            chosen = sb(ph, "chosen", [P, 2, GROUPS, E])
            rest = sb(ph, "rest", W)
            ex = sb(ph, "ex", W)
            top_of = sb(ph, "top_of", [P, 4, GROUPS])
            comb = sb(ph, "comb", [P, GROUPS, E + 1])
            left = sb(ph, "left", [P, GROUPS, E + 1])
            parts = sb(ph, "parts", [P, GROUPS, 3, E + 1], BF16)
            ident_b = sb(ph, "ident_b", [P, P], BF16)
            c_ps = [ps(ph, f"c_ps{n}", [3 * (E + 1), 8, P], BF16) for n in range(4)]
            k_step, k_shift, k_exp, k_parts, k_t = (sem(n) for n in ("k_step", "k_shift", "k_exp", "k_parts", "k_t"))
            block = ph.enter_context(nc.Block())

            @block.scalar
            def _(eng):
                act.wait_ge(k_shift, 1)
                act.activation(ex[:], ex[:], ACT.Exp).then_inc(k_exp, 1)

            @block.tensor
            def _(pe):
                pe.wait_ge(k_parts, 1)
                for n in range(GROUPS):
                    ins_ = pe.transpose(c_ps[n // 8][:, n % 8, :], parts[:, n].rearrange("p a e -> p (a e)"), ident_b[:])
                    if n % 8 == 7:
                        ins_.then_inc(k_t, 1)

            @block.vector
            def _(eng):
                count = [0]

                def done(ins_):
                    count[0] += 1
                    ins_.then_inc(k_step, 1)
                    v.wait_ge(k_step, count[0])

                def over_e(a):
                    return a.unsqueeze(2).to_broadcast(W)

                def choose(src, rnd):
                    done(v.tensor_reduce(top_of[:, rnd, :], src, AX_X, ALU.max))
                    done(v.tensor_tensor(best[:], src, over_e(top_of[:, rnd, :]), ALU.is_equal))
                    done(v.tensor_tensor(best[:], best[:], c("first").unsqueeze(1).to_broadcast(W), ALU.mult))
                    done(v.tensor_reduce(top_of[:, 2, :], best[:], AX_X, ALU.max))
                    done(v.tensor_tensor(chosen[:, rnd], best[:], over_e(top_of[:, 2, :]), ALU.is_equal))

                v.tensor_copy(ident_b[:], ident)
                v.memset(comb[:, :, E:E + 1], 1.0)
                choose(logits[:], 0)
                v.tensor_tensor(ex[:], logits[:], over_e(top_of[:, 0, :]), ALU.subtract).then_inc(k_shift, 1)
                done(v.tensor_scalar(rest[:], chosen[:, 0], -BIG, None, ALU.mult))
                done(v.tensor_tensor(rest[:], rest[:], logits[:], ALU.add))
                choose(rest[:], 1)
                done(v.tensor_tensor(rest[:], chosen[:, 0], chosen[:, 1], ALU.add))
                v.wait_ge(k_exp, 1)
                done(v.tensor_tensor(ex[:], ex[:], rest[:], ALU.mult))
                done(v.tensor_reduce(top_of[:, 2, :], ex[:], AX_X, ALU.add))
                done(v.reciprocal(top_of[:, 3, :], top_of[:, 2, :]))
                done(v.tensor_tensor(comb[:, :, 0:E], ex[:], over_e(top_of[:, 3, :]), ALU.mult))
                done(v.tensor_copy(parts[:, :, 0, :], comb[:]))
                done(v.tensor_tensor(left[:], comb[:], parts[:, :, 0, :], ALU.subtract))
                done(v.tensor_copy(parts[:, :, 1, :], left[:]))
                done(v.tensor_tensor(left[:], left[:], parts[:, :, 1, :], ALU.subtract))
                v.tensor_copy(parts[:, :, 2, :], left[:]).then_inc(k_parts, 1)
                for n in range(4):
                    v.wait_ge(k_t, n + 1)
                    ins_ = v.tensor_copy(comb_t[:, n * 8 * P:(n + 1) * 8 * P], c_ps[n][:].rearrange("p a t -> p (a t)"))
                done(ins_)

        with ExitStack() as ph:
            tanh = sb(ph, "tanh", [P, 2, BLK])
            gated = sb(ph, "gated", [P, 2, BLK])
            hidden = sb(ph, "hidden", [P, 2, BLK])
            total_f = sb(ph, "total_f", [P, 2, BLK])
            total_t = sb(ph, "total_t", [P, 2, GPB, C])
            g_ps, u_ps = ([ps(ph, f"{n}_ps{r}", [P, BLK]) for r in range(2)] for n in ("g", "u"))
            m_ps = ps(ph, "mix_ps", [P, BLK])
            dn_ps = [ps(ph, f"dn_ps{r}", [P, BLK]) for r in range(2)]
            ot_ps = ps(ph, "ot_ps", [P, BLK])
            h_g, h_u, h_m, h_th, h_a, h_b, h_h, h_d, h_dn, h_sum, h_t, h_tc = (
                sem(n) for n in ("h_g", "h_u", "h_m", "h_th", "h_a", "h_b", "h_h", "h_d", "h_dn", "h_sum", "h_t", "h_tc"))
            h_out = [sem("h_out0"), sem("h_out1")]
            block = ph.enter_context(nc.Block())
            SPAN = [P] * (PAIRS - 1) + [I]

            @block.sync
            def _(sp):
                for i, half in blocks(sp):
                    blk = 2 * i + half
                    sp.wait_ge(h_tc, blk + 1)
                    sp.dma_start(out_groups[:, bass.ds(blk * GPB, GPB), :], total_t[:, half]).then_inc(h_out[half], 16)
                for half in range(2):
                    sp.wait_ge(h_out[half], 16 * NBLK // 2)

            @block.tensor
            def _(pe):
                for i in pairs_of_blocks(pe):
                    for k in range(2 * PAIRS + 1):
                        if k < 2 * PAIRS:
                            half, p = k // PAIRS, k % PAIRS
                            m = i * 2 * PAIRS + k
                            w = SPAN[p]
                            z = z_f[:, bass.ds((2 * i + half) * BLK, BLK)]
                            def before(sem_, lag):
                                wait_apart(pe, sem_, m - lag + 1 if k >= lag else i * 2 * PAIRS)
                            before(h_a, 2)
                            pe.matmul(g_ps[k % 2][0:w, :], wg[:, 2 * p:2 * p + w // I, :], z, start=True, stop=True).then_inc(h_g, 1)
                            before(h_b, 2)
                            pe.matmul(u_ps[k % 2][0:w, :], wu[:, 2 * p:2 * p + w // I, :], z, start=True, stop=True).then_inc(h_u, 1)
                            before(h_h, 1)
                            pe.matmul(m_ps[:], pick[:, p, :], comb_t[:, bass.ds((2 * i + half) * BLK, BLK)],
                                      start=True, stop=True).then_inc(h_m, 1)
                        if k >= 1:
                            q, half, p = k - 1, (k - 1) // PAIRS, (k - 1) % PAIRS
                            w = SPAN[p]
                            wait_apart(pe, h_h, i * 2 * PAIRS + q + 1)
                            if p == 0:
                                after(pe, h_sum, 2 * i)
                            pe.matmul(dn_ps[half][:], wd[0:w, p, :], hidden[0:w, q % 2, :], start=(p == 0), stop=(p == PAIRS - 1),
                                      skip_group_check=True).then_inc(h_d, 1)
                            if p == PAIRS - 1:
                                pe.wait_ge(h_sum, 2 * i + half + 1)
                                after(pe, h_tc, 2 * i + half)
                                for g in range(GPB):
                                    ins_ = pe.transpose(ot_ps[:, g * P:(g + 1) * P], total_f[:, half, g * P:(g + 1) * P], ident)
                                ins_.then_inc(h_t, 1)

            @block.scalar
            def _(eng):
                for i in pairs_of_blocks(act):
                    for k in range(2 * PAIRS):
                        half, p = k // PAIRS, k % PAIRS
                        w = SPAN[p]
                        act.wait_ge(h_g, i * 2 * PAIRS + k + 1)
                        if k >= 2:
                            act.wait_ge(h_a, i * 2 * PAIRS + k - 1)
                        act.activation(tanh[0:w, k % 2, :], g_ps[k % 2][0:w, :], ACT.Tanh, scale=0.5).then_inc(h_th, 1)
                        if p == PAIRS - 1:
                            act.wait_ge(h_t, 2 * i + half + 1)
                            after(act, h_out[half], 16 * i)
                            act.activation(total_t[:, half].rearrange("p g c -> p (g c)"), ot_ps[:], ACT.Copy).then_inc(h_tc, 1)

            @block.vector
            def _(eng):
                for i in pairs_of_blocks(v):
                    for k in range(2 * PAIRS):
                        half, p = k // PAIRS, k % PAIRS
                        w = SPAN[p]
                        m = i * 2 * PAIRS + k
                        v.wait_ge(h_th, m + 1)
                        after(v, h_b, m)
                        v.scalar_tensor_tensor(out=gated[0:w, 0, :], in0=tanh[0:w, k % 2, :], scalar=1.0, in1=g_ps[k % 2][0:w, :],
                                               op0=ALU.add, op1=ALU.mult).then_inc(h_a, 1)
                        v.wait_ge(h_u, m + 1)
                        v.wait_ge(h_a, m + 1)
                        after(v, h_h, m)
                        v.tensor_tensor(gated[0:w, 1, :], gated[0:w, 0, :], u_ps[k % 2][0:w, :], ALU.mult).then_inc(h_b, 1)
                        v.wait_ge(h_m, m + 1)
                        v.wait_ge(h_b, m + 1)
                        if k >= 2:
                            v.wait_ge(h_d, m - 1)
                        v.tensor_tensor(hidden[0:w, k % 2, :], gated[0:w, 1, :], m_ps[0:w, :], ALU.mult).then_inc(h_h, 1)
                        if p == PAIRS - 1:
                            v.wait_ge(h_d, m + 1)
                            after(v, h_t, 2 * i)
                            v.tensor_tensor(total_f[:, half, :], dn_ps[half][:], x_f[:, bass.ds((2 * i + half) * BLK, BLK)],
                                            ALU.add).then_inc(h_sum, 1)


_INS = ["x", "itok_B_0_2", "itok_B_0_7", "L0_cond_W1", "L0_cond_b1", "L0_cond_v", "L0_ffn_g_info", "L0_ffn_W_qkv",
        "L0_ffn_W_proj", "L0_ffn_b_proj", "L1_cond_weight", "L1_cond_bias", "L1_ffn_w_ln1", "L1_ffn_Wq", "L1_ffn_Wkva",
        "L1_ffn_Wkvb", "L1_ffn_Wo", "L1_ffn_w_ln2", "L1_ffn_Wgate", "L1_ffn_expert_bias", "L1_ffn_Wg", "L1_ffn_Wu",
        "L1_ffn_Wd", "L1_ffn_sWg", "L1_ffn_sWu", "L1_ffn_sWd"]


def kernel(**inputs):
    import concourse.bacc as _bacc
    from concourse.bass_utils import run_bass_kernel_spmd as _run

    nc = _bacc.Bacc("TRN2", target_bir_lowering=False, num_devices=1)
    arrays, aps = {}, {}
    for name in _INS:
        a = np.ascontiguousarray(inputs[name])
        arrays[f"in_{name}_dram"] = a
        aps[name] = nc.dram_tensor(f"in_{name}_dram", a.shape, mybir.dt.from_np(a.dtype), kind="ExternalInput").ap()
    at, table = shape_constants()
    arrays["shape_constants_dram"] = table
    const = nc.dram_tensor("shape_constants_dram", table.shape, F32, kind="ExternalInput").ap()
    out = nc.dram_tensor("out_dram", (B, S, C), F32, kind="ExternalOutput").ap()
    build(nc, aps, const, at, out)
    r = _run(nc, [arrays], core_ids=[0])
    return r.results[0]["out_dram"]
```

```python
from contextlib import ExitStack

import concourse.bass as bass
import numpy as np
from concourse import mybir

ALU = mybir.AluOpType
ACT = mybir.ActivationFunctionType
AX_X = mybir.AxisListType.X
F32 = mybir.dt.float32
BF16 = mybir.dt.bfloat16
I32 = mybir.dt.int32

P = 128
B, S, C = 128, 32, 128
TOK = B * S
SEQ = P // S
GROUPS = TOK // P
GPB = 4
BLK = GPB * P
NBLK = TOK // BLK
SPB = BLK // S
A = 32
H0, D0, REG = 16, 8, 5
HG = 4
HPG = H0 // HG
H1, D1, ROPE, R = 16, 64, 32, 16
NOPE = D1 - ROPE
E, K_TOP, I = 8, 2, 64
PAIRS = (E + 2) // 2
SUBJ = 8
EPS = 1e-5
THETA = 100000.0
QX = HPG * S + S
BIG = 1e30
MASK = -float(2 ** 100)


def shape_constants():
    p = np.arange(P)
    f = np.float32
    q, k = p % S, np.arange(S)
    cols = {}
    cols["ident"] = np.eye(P)
    cols["prefix"] = k[None] <= q[:, None]
    cols["postfix"] = k[None] >= q[:, None]
    cols["cloze"] = k[None] != q[:, None]
    cols["own"] = k[None] == q[:, None]
    cols["same_seq"] = (p[:, None] // S) == (p[None] // S)
    cols["is_reg_key"] = np.broadcast_to(k[None] < REG, (P, S))
    cols["is_reg_row"] = (q < REG)[:, None]
    head = (p // D0) % HPG
    cols["head_row"] = head[:, None] == np.arange(HPG)[None]
    share = np.where((q < REG)[:, None, None] | (np.arange(HPG + 1) == HPG)[None, None], 0.5, 1.0)
    cols["share"] = np.broadcast_to(share, (P, HG, HPG + 1)).reshape(P, -1)
    t = np.arange(S, dtype=f)
    freqs = (f(1.0) / f(THETA) ** (np.arange(0, ROPE, 2, dtype=f) / f(ROPE))).astype(f)
    angle = np.outer(t, freqs).astype(f)
    cos = np.repeat(np.cos(angle).T, 2, axis=0)
    sin = np.repeat(np.sin(angle).T, 2, axis=0)
    one, zero = np.ones((S, S)), np.zeros((S, S))
    causal = np.where(k[:, None] > k[None], MASK, 0.0)
    cols["q_turn"] = np.concatenate([cos, sin, one, zero]) * f(D1) ** f(-0.5)
    cols["k_turn"] = np.concatenate([cos, cos, one, zero])
    cols["k_cross"] = np.concatenate([sin, sin, zero, zero])
    cols["causal"] = np.concatenate([zero, zero, zero, causal])
    pick = np.zeros((P, PAIRS, P))
    for part in range(3):
        for e in range(E + 1):
            pick[part * (E + 1) + e, e // 2, (e % 2) * I:(e % 2) * I + I] = 0.5
    cols["pick"] = pick.reshape(P, -1)
    cols["first"] = np.broadcast_to(E - np.arange(E)[None], (P, E))
    at, n = {}, 0
    for name, v in cols.items():
        at[name] = (n, n + v.shape[1])
        n += v.shape[1]
    return at, np.concatenate([np.asarray(v, f) for v in cols.values()], axis=1).astype(f)


def pairs_of_blocks(eng):
    yield 0
    with eng.Fori(1, NBLK // 2) as i:
        yield i


def blocks(eng):
    for i in pairs_of_blocks(eng):
        for half in range(2):
            yield i, half


def after(eng, signal, count):
    if not isinstance(count, int) or count > 0:
        eng.wait_ge(signal, count)


def wait_apart(pe, signal, count):
    if not isinstance(count, int) or count > 0:
        pe.wait_ge(signal, count)
        pe.nop(nofuse=True)


SLOTS = 2 * GPB


def slots(eng, most, ring=SLOTS, total=GROUPS):
    for j in range(ring):
        yield 0, j, lambda lag, j=j: j >= lag
    with eng.Fori(1, total // ring) as i:
        for j in range(ring):
            yield i, j, lambda lag: True
    for j in range(most):
        yield total // ring, j, lambda lag, j=j: lag > j


def skewed_blocks(eng, most):
    return slots(eng, most, 2, NBLK)


def build(nc, ins, const, const_at, out):
    v, act, pool = nc.vector, nc.scalar, nc.gpsimd
    x_d = ins["x"].rearrange("b s c -> (b s) c")
    x_groups = x_d.rearrange("(g p) c -> p g c", p=P)
    out_groups = out.rearrange("b s c -> (b s) c").rearrange("(g p) c -> p g c", p=P)

    top = ExitStack()
    with top:
        def sem(name):
            return top.enter_context(nc.semaphore(name))

        def sb(ctx, name, shape, dt=F32):
            return ctx.enter_context(nc.sbuf_tensor(name, shape, dt))

        def ps(ctx, name, shape, dt=F32):
            return ctx.enter_context(nc.psum_tensor(name, shape, dt))

        con = sb(top, "con", [P, const.shape[1]])

        def c(name):
            a, b = const_at[name]
            return con[:, a:b]

        ident = c("ident")
        x_f = sb(top, "x_f", [P, TOK])
        ones = sb(top, "ones", [P, P])
        w1 = sb(top, "w1", [P, A])
        b1 = sb(top, "b1", [A, 1])
        v_col = sb(top, "v_col", [A, 1])
        v_wide = sb(top, "v_wide", [A, S])
        prompt = sb(top, "prompt", [P, B], I32)
        wqkv = sb(top, "wqkv", [P, 3 * C])
        g_row = sb(top, "g_row", [P, C])
        wproj = sb(top, "wproj", [P, C])
        wproj_h = sb(top, "wproj_h", [P, HPG, C])
        bproj = sb(top, "bproj", [P, 1])
        w_subj = sb(top, "w_subj", [P, SUBJ, C])
        w_subj_t = sb(top, "w_subj_t", [P, SUBJ, C])
        ln1 = sb(top, "ln1", [P, 1])
        ln2 = sb(top, "ln2", [P, 1])
        wq_heads = sb(top, "wq_heads", [P, H1, 96])
        wk_a = sb(top, "wk_a", [P, 96])
        wk_b = sb(top, "wk_b", [P, 64])
        w_lat = sb(top, "w_lat", [P, S])
        w_o = sb(top, "w_o", [P, H1 // 4, C])
        wgate = sb(top, "wgate", [P, E])
        gate_b = sb(top, "gate_b", [P, E])
        wg = sb(top, "wg", [P, 2 * PAIRS, I])
        wu = sb(top, "wu", [P, 2 * PAIRS, I])
        wd = sb(top, "wd", [P, PAIRS, C])
        pick = sb(top, "pick", [3 * (E + 1), PAIRS, P], BF16)

        layer0 = top.enter_context(ExitStack())
        q_f = sb(layer0, "q_f", [P, TOK])
        k_f = sb(layer0, "k_f", [P, TOK])
        v_t = sb(layer0, "v_t", [P, GROUPS, C])
        class_mask = sb(layer0, "class_mask", [P, GROUPS, HPG + 1, S])

        similar = top.enter_context(ExitStack())
        lie = sb(similar, "lie", [P, 2, GROUPS, H0])
        guide = sb(similar, "guide", [P, C])

        pooling = top.enter_context(ExitStack())
        pooled_p = sb(pooling, "pooled_p", [P, GROUPS, P])

        between = top.enter_context(ExitStack())
        W = [P, GROUPS, S]
        seen_by = sb(between, "seen_by", W)
        row = sb(between, "row", [P, 4, GROUPS])
        wq = sb(between, "wq", [P, H1 * D1])
        wka = sb(between, "wka", [P, R + ROPE])
        wkvb = sb(between, "wkvb", [R, H1 * NOPE])
        wkvb_t = sb(between, "wkvb_t", [NOPE, H1, S])
        wo = sb(between, "wo", [NOPE, H1, C])
        score_ps = ps(between, "score_ps", [P, GROUPS * S])
        cleared, ld_late = sem("cleared"), sem("ld_late")
        late_loads = [
            (wkvb[:], ins["L1_ffn_Wkvb"]), (w_subj[:], ins["L1_cond_weight"].rearrange("s o h -> o s h")),
            (wo[:], ins["L1_ffn_Wo"].rearrange("(h d) c -> d h c", d=D1)[0:NOPE, :, :]),
            (wd[0:I, 0:E // 2, :], ins["L1_ffn_Wd"].rearrange("(p t) i c -> t i p c", t=2)[0]),
            (wd[I:P, 0:E // 2, :], ins["L1_ffn_Wd"].rearrange("(p t) i c -> t i p c", t=2)[1]),
            (wd[0:I, E // 2, :], ins["L1_ffn_sWd"][0]),
        ]

        with ExitStack() as ph:
            x_in = sb(ph, "x_in", [P, 2, GPB, C])
            hid = sb(ph, "hid", [A, TOK])
            types = sb(ph, "types", [P, GROUPS])
            kind = sb(ph, "kind", [P, 3, GROUPS])
            allow = sb(ph, "allow", W)
            part = sb(ph, "part", W)
            x_ps = ps(ph, "x_ps", [P, 2, BLK])
            h_ps = ps(ph, "h_ps", [A, 2, BLK])
            ld_ident, ld_first, ld_con, ld_prompt = sem("ld_ident"), sem("ld_first"), sem("ld_con"), sem("ld_prompt")
            ld_q, ld_mix = sem("ld_q"), sem("ld_mix")
            a_in = [sem("a_in0"), sem("a_in1")]
            a_x, a_xc, a_h, a_hc, a_sc, a_wide = (sem(n) for n in ("a_x", "a_xc", "a_h", "a_hc", "a_sc", "a_wide"))
            a_step = sem("a_step")
            first_loads = [
                (w1[:], ins["L0_cond_W1"]), (b1[:], ins["L0_cond_b1"].rearrange("(p a) -> p a", a=1)),
                (v_col[:], ins["L0_cond_v"].rearrange("(p a) -> p a", a=1)),
            ]
            q_loads = [
                (ln1[:], ins["L1_ffn_w_ln1"].rearrange("(p a) -> p a", a=1)),
                (ln2[:], ins["L1_ffn_w_ln2"].rearrange("(p a) -> p a", a=1)),
                (wka[:], ins["L1_ffn_Wkva"]), (wproj[:], ins["L0_ffn_W_proj"]), (wq[:], ins["L1_ffn_Wq"]),
            ]
            mix_loads = [
                (wgate[:], ins["L1_ffn_Wgate"]), (gate_b[:], ins["L1_ffn_expert_bias"].partition_broadcast(P)),
                (wg[:, 0:E, :], ins["L1_ffn_Wg"].rearrange("e c i -> c e i")),
                (wg[:, E, :], ins["L1_ffn_sWg"][0]),
                (wu[:, 0:E, :], ins["L1_ffn_Wu"].rearrange("e c i -> c e i")),
                (wu[:, E, :], ins["L1_ffn_sWu"][0]),
                (wqkv[:], ins["L0_ffn_W_qkv"]),
                (g_row[:], ins["L0_ffn_g_info"][0, 0].partition_broadcast(P)),
                (bproj[:], ins["L0_ffn_b_proj"].rearrange("(p a) -> p a", a=1)),
            ]
            block = ph.enter_context(nc.Block())
            ident_end = const_at["ident"][1]

            @block.sync
            def _(sp):
                sp.dma_start(con[:, 0:ident_end], const[:, 0:ident_end]).then_inc(ld_ident, 16)
                for i, half in blocks(sp):
                    blk = 2 * i + half
                    after(sp, a_x, blk - 1)
                    sp.dma_start(x_in[:, half], x_groups[:, bass.ds(blk * GPB, GPB), :]).then_inc(a_in[half], 16)
                for dst, src in mix_loads:
                    sp.dma_start(dst, src).then_inc(ld_mix, 16)
                for dst, src in late_loads:
                    sp.dma_start(dst, src).then_inc(ld_late, 16)

            @block.gpsimd
            def _(eng):
                pool.memset(wkvb_t[:], 0.0).then_inc(cleared, 1)
                pool.memset(wq_heads[:], 0.0).then_inc(cleared, 1)
                pool.memset(wk_a[:], 0.0).then_inc(cleared, 1)
                pool.memset(w_lat[:], 0.0).then_inc(cleared, 1)
                pool.memset(ones[:], 1.0).then_inc(cleared, 1)
                pool.memset(pooled_p[:], 0.0).then_inc(cleared, 1)

            @block.tensor
            def _(pe):
                pe.wait_ge(ld_ident, 16)
                pe.wait_ge(ld_first, 16 * len(first_loads))
                for i, j, live in skewed_blocks(pe, 1):
                    if live(0):
                        blk = 2 * i + j
                        pe.wait_ge(a_in[j], 16 * i + 16)
                        after(pe, a_xc, blk - 1)
                        for g in range(GPB):
                            ins_ = pe.transpose(x_ps[:, j, g * P:(g + 1) * P], x_in[:, j, g, :], ident)
                        ins_.then_inc(a_x, 1)
                    if live(1):
                        blk, half = 2 * i + j - 1, (j - 1) % 2
                        pe.wait_ge(a_xc, blk + 1)
                        after(pe, a_hc, blk - 1)
                        pe.matmul(h_ps[:, half, :], w1[:], x_f[:, bass.ds(blk * BLK, BLK)], start=True, stop=True).then_inc(a_h, 1)
                pe.wait_ge(a_hc, NBLK)
                pe.wait_ge(a_wide, 1)
                hid_v = hid[:].rearrange("a (g s l) -> a g s l", s=SEQ, l=S)
                for n in range(2):
                    for s in range(SEQ):
                        ins_ = pe.matmul(score_ps[32 * s:32 * s + 32, n * BLK:(n + 1) * BLK], v_wide[:],
                                         hid_v[:, n * 16:(n + 1) * 16, s, :], start=True, stop=True)
                ins_.then_inc(a_sc, 1)

            @block.scalar
            def _(eng):
                for dst, src in first_loads:
                    act.dma_start(dst, src).then_inc(ld_first, 16)
                act.dma_start(prompt[:], ins["itok_B_0_2"].partition_broadcast(P)).then_inc(ld_prompt, 16)
                act.dma_start(con[:, ident_end:], const[:, ident_end:]).then_inc(ld_con, 16)
                for dst, src in q_loads:
                    act.dma_start(dst, src).then_inc(ld_q, 16)
                act.wait_ge(ld_first, 16 * len(first_loads))
                for i, j, live in skewed_blocks(act, 1):
                    if live(0):
                        blk = 2 * i + j
                        act.wait_ge(a_x, blk + 1)
                        act.activation(x_f[:, bass.ds(blk * BLK, BLK)], x_ps[:, j, :], ACT.Copy).then_inc(a_xc, 1)
                    if live(1):
                        blk, half = 2 * i + j - 1, (j - 1) % 2
                        act.wait_ge(a_h, blk + 1)
                        act.activation(hid[:, bass.ds(blk * BLK, BLK)], h_ps[:, half, :], ACT.Tanh, bias=b1[:, 0:1]).then_inc(a_hc, 1)
                act.wait_ge(a_sc, 1)

            @block.vector
            def _(eng):
                count = [0]

                def done(ins_):
                    count[0] += 1
                    ins_.then_inc(a_step, 1)
                    v.wait_ge(a_step, count[0])

                def over_l(a):
                    return a.unsqueeze(2).to_broadcast(W)

                def over_g(a):
                    return a.unsqueeze(1).to_broadcast(W)

                v.wait_ge(ld_first, 16 * len(first_loads))
                v.tensor_copy(v_wide[:], v_col[:, 0:1].to_broadcast([A, S])).then_inc(a_wide, 1)
                v.wait_ge(ld_prompt, 16)
                for s in range(SEQ):
                    r = slice(32 * s, 32 * s + 32)
                    ins_ = v.tensor_copy(types[r, :], prompt[r, :].rearrange("p (g s) -> p g s", s=SEQ)[:, :, s])
                done(ins_)
                v.tensor_scalar(kind[:, 0, :], types[:], 0.0, None, ALU.is_equal)
                done(v.tensor_scalar(kind[:, 1, :], types[:], 1.0, None, ALU.is_equal))
                done(v.tensor_tensor(kind[:, 2, :], kind[:, 0, :], kind[:, 1, :], ALU.add))
                done(v.tensor_scalar(kind[:, 2, :], kind[:, 2, :], -1.0, 1.0, ALU.mult, ALU.add))
                v.wait_ge(ld_con, 16)
                v.tensor_tensor(part[:], over_l(kind[:, 0, :]), over_g(c("prefix")), ALU.mult)
                v.tensor_tensor(seen_by[:], over_l(kind[:, 1, :]), over_g(c("postfix")), ALU.mult)
                done(v.tensor_tensor(allow[:], over_l(kind[:, 2, :]), over_g(c("cloze")), ALU.mult))
                done(v.tensor_tensor(allow[:], allow[:], part[:], ALU.add))
                done(v.tensor_tensor(allow[:], allow[:], seen_by[:], ALU.add))
                v.tensor_reduce(row[:, 0, :], allow[:], AX_X, ALU.add)
                v.tensor_scalar(seen_by[:], allow[:], BIG, -BIG, ALU.mult, ALU.add)
                v.wait_ge(cleared, 5)
                v.wait_ge(ld_q, 16 * len(q_loads))
                v.tensor_scalar(wq[:], wq[:], ln1[:, 0:1], None, ALU.mult)
                done(v.tensor_scalar(wka[:], wka[:], ln1[:, 0:1], None, ALU.mult))
                for h in range(HPG):
                    v.tensor_scalar(wproj_h[:, h, :], wproj[:], c("head_row")[:, h:h + 1], None, ALU.mult)
                pairs = wq[:].rearrange("p (h a f t) -> p h a f t", h=H1, a=2, t=2)[:, :, 1, :, :]
                crossed = wq_heads[:, :, ROPE:2 * ROPE].rearrange("p h (f t) -> p h f t", t=2)
                v.tensor_copy(wq_heads[:, :, 0:ROPE], wq[:].rearrange("p (h a f) -> p h a f", h=H1, a=2)[:, :, 1, :])
                v.tensor_scalar(crossed[:, :, :, 0], pairs[:, :, :, 1], -1.0, None, ALU.mult)
                v.tensor_copy(crossed[:, :, :, 1], pairs[:, :, :, 0])
                rope = wka[:, R:R + ROPE]
                rope_pairs = rope.rearrange("p (f t) -> p f t", t=2)
                v.tensor_copy(wk_a[:, 0:ROPE], rope)
                v.tensor_copy(wk_a[:, ROPE:2 * ROPE], rope)
                v.tensor_copy(wk_a[:, 2 * ROPE:2 * ROPE + R], wka[:, 0:R])
                v.tensor_copy(w_lat[:, 0:R], wka[:, 0:R])
                for n in range(2):
                    cross = wk_b[:, n * ROPE:(n + 1) * ROPE].rearrange("p (f t) -> p f t", t=2)
                    v.tensor_scalar(cross[:, :, 0], rope_pairs[:, :, 1], -1.0, None, ALU.mult)
                    v.tensor_copy(cross[:, :, 1], rope_pairs[:, :, 0])
                v.tensor_copy(pick[:], c("pick")[0:3 * (E + 1), :].rearrange("p (a b) -> p a b", a=PAIRS))
                v.wait_ge(ld_mix, 16 * len(mix_loads))
                v.tensor_scalar(wgate[:], wgate[:], ln2[:, 0:1], None, ALU.mult)
                v.tensor_scalar(wg[:, 0:E + 1, :], wg[:, 0:E + 1, :], ln2[:, 0:1], None, ALU.mult)
                v.tensor_scalar(wu[:, 0:E + 1, :], wu[:, 0:E + 1, :], ln2[:, 0:1], None, ALU.mult)
                v.wait_ge(cleared, 6)

        with ExitStack() as ph:
            sc = sb(ph, "sc", W)
            wq_nt = sb(ph, "wq_nt", [NOPE, H1, C])
            t_ps = [ps(ph, f"t_ps{n}", [P, BLK]) for n in range(4)]
            small_ps = ps(ph, "small_ps", [P, BLK])
            m_ps = ps(ph, "m_ps", [P, BLK])
            k_ps = small_ps[:, 0:4 * R].rearrange("p (n r) -> p n r", r=R)
            a_ps = small_ps[:, 4 * R:4 * R + H1 * R].rearrange("p (h r) -> p h r", r=R)
            turned = sem("turned")
            untangled = sem("untangled")
            absorbed = sem("absorbed")
            b_step, b_shift, b_exp = sem("b_step"), sem("b_shift"), sem("b_exp")
            block = ph.enter_context(nc.Block())

            @block.tensor
            def _(pe):
                pe.wait_ge(ld_late, 16 * len(late_loads))
                for n in range(4):
                    ins_ = pe.transpose(k_ps[:, n, :], wkvb[:, n * P:(n + 1) * P], ident[0:R, 0:R])
                ins_.then_inc(turned, 1)
                for n in range(8):
                    ins_ = pe.transpose(t_ps[2 + n // 4][:, (n % 4) * P:(n % 4 + 1) * P], wq[:, n * P:(n + 1) * P], ident)
                    if n % 4 == 3:
                        ins_.then_inc(turned, 1)
                for s in range(SUBJ):
                    ins_ = pe.transpose(t_ps[s // 4][:, (s % 4) * P:(s % 4 + 1) * P], w_subj[:, s, :], ident)
                    if s % 4 == 3:
                        ins_.then_inc(turned, 1)
                pe.wait_ge(untangled, 5)
                for h in range(H1):
                    pe.matmul(a_ps[:, h, :], wq_nt[:, h, :], wkvb_t[:, h, 0:R], start=True, stop=True)
                for h in range(H1):
                    ins_ = pe.matmul(m_ps[32 * (h // 4):32 * (h // 4) + 32, (h % 4) * C:(h % 4 + 1) * C],
                                     wkvb_t[:, h, :], wo[:, h, :], start=True, stop=True)
                ins_.then_inc(absorbed, 1)

            @block.scalar
            def _(eng):
                act.wait_ge(b_shift, 1)
                act.activation(sc[:], sc[:], ACT.Exp).then_inc(b_exp, 1)
                act.wait_ge(turned, 1)
                for m in range(4):
                    ins_ = act.activation(wkvb_t[:, :, 0:R].rearrange("p (n m) r -> p n m r", m=4)[:, :, m, :],
                                          k_ps[32 * m:32 * m + 32, :, :], ACT.Copy)
                ins_.then_inc(untangled, 1)
                for n in range(2):
                    act.wait_ge(turned, 2 + n)
                    for m in range(2):
                        act.activation(wq_nt[:, 8 * n:8 * n + 8, :].rearrange("p (j m) c -> p j m c", m=2)[:, :, m, :],
                                       t_ps[2 + n][64 * m:64 * m + NOPE, :].rearrange("p (j c) -> p j c", j=4),
                                       ACT.Copy).then_inc(untangled, 1)
                for n in range(2):
                    act.wait_ge(turned, n + 4)
                    act.activation(w_subj_t[:, 4 * n:4 * n + 4, :].rearrange("p s o -> p (s o)"), t_ps[n][:], ACT.Copy)
                act.wait_ge(absorbed, 1)
                act.activation(wq_heads[:, :, 64:64 + R], a_ps, ACT.Copy)
                act.activation(w_o[:].rearrange("p h c -> p (h c)"), m_ps[:], ACT.Copy)

            @block.vector
            def _(eng):
                count = [0]

                def done(ins_):
                    count[0] += 1
                    ins_.then_inc(b_step, 1)
                    v.wait_ge(b_step, count[0])

                def over_l(a):
                    return a.unsqueeze(2).to_broadcast(W)

                done(v.tensor_tensor(sc[:], seen_by[:], score_ps[:].rearrange("p (g l) -> p g l", l=S), ALU.add))
                done(v.tensor_reduce(row[:, 1, :], sc[:], AX_X, ALU.max))
                v.tensor_tensor(sc[:], sc[:], over_l(row[:, 1, :]), ALU.subtract).then_inc(b_shift, 1)
                v.wait_ge(b_exp, 1)
                done(v.tensor_reduce(row[:, 2, :], sc[:], AX_X, ALU.add))
                done(v.tensor_tensor(row[:, 2, :], row[:, 2, :], row[:, 0, :], ALU.mult))
                done(v.reciprocal(row[:, 3, :], row[:, 2, :]))
                done(v.tensor_tensor(sc[:], sc[:], over_l(row[:, 3, :]), ALU.mult))
                for s in range(SEQ):
                    r = slice(32 * s, 32 * s + 32)
                    ins_ = v.transpose(pooled_p[r, :, r], sc[r, :, :])
                done(ins_)
        between.close()

        with ExitStack() as ph:
            xc = sb(ph, "xc", [P, 2, BLK])
            q2 = sb(ph, "q2", [P, GPB, C])
            qg = sb(ph, "qg", [P, GPB, C])
            gh = sb(ph, "gh", [P, 2, H0])
            xc_ps = ps(ph, "xc_ps", [P, 2, BLK])
            qf_ps, kf_ps, qt_ps, vt_ps = (ps(ph, n, [P, BLK]) for n in ("qf_ps", "kf_ps", "qt_ps", "vt_ps"))
            c_xc, c_xcc = sem("c_xc"), sem("c_xcc")
            c_qf, c_kf, c_qt, c_vt = (sem(n) for n in ("c_qf", "c_kf", "c_qt", "c_vt"))
            c_qfc, c_kfc, c_sq, c_vtc, c_qg, c_red, c_g, c_g2 = (
                sem(n) for n in ("c_qfc", "c_kfc", "c_sq", "c_vtc", "c_qg", "c_red", "c_g", "c_g2"))
            x_st = sb(ph, "x_st2", [P, 2, GPB, C])
            c_x = [sem("c_x0"), sem("c_x1")]
            block = ph.enter_context(nc.Block())

            @block.sync
            def _(sp):
                for i, half in blocks(sp):
                    blk = 2 * i + half
                    after(sp, c_xc, blk - 1)
                    sp.dma_start(x_st[:, half], x_groups[:, bass.ds(blk * GPB, GPB), :]).then_inc(c_x[half], 16)

            @block.tensor
            def _(pe):
                for i, j, live in skewed_blocks(pe, 1):
                    if live(0):
                        blk = 2 * i + j
                        pe.wait_ge(c_x[j], 16 * i + 16)
                        after(pe, c_xcc, blk - 1)
                        for g in range(GPB):
                            ins_ = pe.matmul(xc_ps[:, j, g * P:(g + 1) * P], x_st[:, j, g, :],
                                             pooled_p[:, blk * GPB + g, :], start=True, stop=True)
                        ins_.then_inc(c_xc, 1)
                    if live(1):
                        blk, half = 2 * i + j - 1, (j - 1) % 2
                        pe.wait_ge(c_xcc, blk + 1)
                        after(pe, c_qg, blk)
                        after(pe, c_sq, blk)
                        for g in range(GPB):
                            ins_ = pe.matmul(qt_ps[:, g * P:(g + 1) * P], xc[:, half, g * P:(g + 1) * P],
                                             wqkv[:, 0:C], start=True, stop=True)
                        ins_.then_inc(c_qt, 1)
                        after(pe, c_qfc, blk)
                        pe.matmul(qf_ps[:], wqkv[:, 0:C], xc[:, half, :], start=True, stop=True).then_inc(c_qf, 1)
                        after(pe, c_kfc, blk)
                        pe.matmul(kf_ps[:], wqkv[:, C:2 * C], xc[:, half, :], start=True, stop=True).then_inc(c_kf, 1)
                        after(pe, c_vtc, blk)
                        for g in range(GPB):
                            ins_ = pe.matmul(vt_ps[:, g * P:(g + 1) * P], xc[:, half, g * P:(g + 1) * P],
                                             wqkv[:, 2 * C:3 * C], start=True, stop=True)
                        ins_.then_inc(c_vt, 1)

            @block.scalar
            def _(eng):
                act.wait_ge(c_g, 1)
                act.activation(gh[:, 1, :], gh[:, 0, :], ACT.Sqrt).then_inc(c_g, 1)
                for i, j, live in skewed_blocks(act, 1):
                    if live(0):
                        blk = 2 * i + j
                        act.wait_ge(c_xc, blk + 1)
                        after(act, c_vt, blk - 1)
                        act.activation(xc[:, j, :], xc_ps[:, j, :], ACT.Copy).then_inc(c_xcc, 1)
                    if live(1):
                        blk = 2 * i + j - 1
                        act.wait_ge(c_qt, blk + 1)
                        after(act, c_red, 2 * blk)
                        act.activation(q2[:].rearrange("p g c -> p (g c)"), qt_ps[:], ACT.Square).then_inc(c_sq, 1)
                        act.wait_ge(c_kf, blk + 1)
                        act.activation(k_f[:, bass.ds(blk * BLK, BLK)], kf_ps[:], ACT.Copy).then_inc(c_kfc, 1)
                        act.wait_ge(c_vt, blk + 1)
                        act.activation(v_t[:, bass.ds(blk * GPB, GPB), :], vt_ps[:].rearrange("p (g c) -> p g c", g=GPB),
                                       ACT.Copy).then_inc(c_vtc, 1)

            @block.vector
            def _(eng):
                def heads(a):
                    return a.rearrange("p (h d) -> p h d", d=D0)

                v.tensor_tensor(qg[:, 0, :], g_row[:], g_row[:], ALU.mult).then_inc(c_g2, 1)
                v.wait_ge(c_g2, 1)
                v.tensor_reduce(gh[:, 0, :], heads(qg[:, 0, :]), AX_X, ALU.add).then_inc(c_g, 1)
                v.wait_ge(c_g, 2)
                v.reciprocal(gh[:, 0, :], gh[:, 1, :]).then_inc(c_g, 1)
                v.wait_ge(c_g, 3)
                v.tensor_tensor(heads(guide[:]), heads(g_row[:]), gh[:, 0, :].unsqueeze(2).to_broadcast([P, H0, D0]),
                                ALU.mult).then_inc(c_g, 1)
                v.wait_ge(c_g, 4)
                for i, half in blocks(v):
                    blk = 2 * i + half
                    v.wait_ge(c_sq, blk + 1)
                    after(v, c_red, 2 * blk)
                    v.tensor_tensor(qg[:], qt_ps[:].rearrange("p (g c) -> p g c", g=GPB),
                                    guide[:].unsqueeze(1).to_broadcast([P, GPB, C]), ALU.mult).then_inc(c_qg, 1)
                    v.wait_ge(c_qf, blk + 1)
                    v.tensor_copy(q_f[:, bass.ds(blk * BLK, BLK)], qf_ps[:]).then_inc(c_qfc, 1)
                    v.wait_ge(c_qg, blk + 1)
                    v.tensor_reduce(lie[:, 0, bass.ds(blk * GPB, GPB), :], qg[:].rearrange("p g (h d) -> p g h d", d=D0),
                                    AX_X, ALU.add).then_inc(c_red, 1)
                    v.wait_ge(c_sq, blk + 1)
                    v.tensor_reduce(lie[:, 1, bass.ds(blk * GPB, GPB), :], q2[:].rearrange("p g (h d) -> p g h d", d=D0),
                                    AX_X, ALU.add).then_inc(c_red, 1)

        with ExitStack() as ph:
            W = [P, GROUPS, S]
            norm = sb(ph, "norm", [P, GROUPS, H0])
            inv = sb(ph, "inv", [P, GROUPS, H0])
            sim = sb(ph, "sim", [P, 4, GROUPS])
            ends = sb(ph, "ends", [P, 4])
            small = sb(ph, "small", [2, 4])
            spread = sb(ph, "spread", W)
            seen = sb(ph, "seen", W)
            t_ps = ps(ph, "ends_ps", [2, P])
            e_ps = ps(ph, "span_ps", [P, 2])
            key_ps = ps(ph, "key_ps", [P, GROUPS * S])
            n_step, n_root, n_pe = sem("n_step"), sem("n_root"), sem("n_pe")
            n_ends, n_small, n_spread = sem("n_ends"), sem("n_small"), sem("n_spread")
            block = ph.enter_context(nc.Block())

            @block.scalar
            def _(eng):
                act.activation(norm[:], lie[:, 1], ACT.Sqrt).then_inc(n_root, 1)

            @block.tensor
            def _(pe):
                pe.wait_ge(n_ends, 1)
                pe.transpose(t_ps[:], ends[:, 0:2], ident).then_inc(n_pe, 1)
                pe.wait_ge(n_small, 1)
                pe.matmul(e_ps[:], ones[0:2, :], small[:, 2:4], start=True, stop=True).then_inc(n_pe, 1)
                pe.wait_ge(n_spread, 1)
                for n in range(2):
                    ins_ = pe.matmul(key_ps[:, n * BLK:(n + 1) * BLK], c("same_seq"),
                                     spread[:, n * 16:(n + 1) * 16, :], start=True, stop=True)
                ins_.then_inc(n_pe, 1)

            @block.vector
            def _(eng):
                count = [0]

                def done(ins_):
                    count[0] += 1
                    ins_.then_inc(n_step, 1)
                    v.wait_ge(n_step, count[0])

                def over_k(a):
                    return a.unsqueeze(2).to_broadcast(W)

                def over_g(a):
                    return a.unsqueeze(1).to_broadcast(W)

                v.wait_ge(n_root, 1)
                done(v.reciprocal(inv[:], norm[:]))
                done(v.tensor_tensor(inv[:], inv[:], lie[:, 0], ALU.mult))
                done(v.tensor_reduce(sim[:, 0, :], inv[:], AX_X, ALU.add))
                done(v.tensor_scalar(sim[:, 0, :], sim[:, 0, :], 1.0 / H0, None, ALU.mult))
                done(v.tensor_scalar(ends[:, 2:3], c("is_reg_row"), -BIG, None, ALU.mult))
                v.tensor_scalar(sim[:, 1, :], sim[:, 0, :], ends[:, 2:3], None, ALU.add)
                done(v.tensor_scalar(sim[:, 2, :], sim[:, 0, :], -1.0, ends[:, 2:3], ALU.mult, ALU.add))
                v.tensor_reduce(ends[:, 0:2], sim[:, 1:3, :], AX_X, ALU.max).then_inc(n_ends, 1)
                v.wait_ge(n_pe, 1)
                done(v.tensor_reduce(small[:, 0:1], t_ps[:], AX_X, ALU.max))
                v.tensor_scalar(small[:, 2:4], ident[0:2, 0:2], small[:, 0:1], None, ALU.mult).then_inc(n_small, 1)
                v.wait_ge(n_pe, 2)
                done(v.tensor_copy(ends[:, 0:2], e_ps[:]))
                done(v.tensor_tensor(ends[:, 2:3], ends[:, 0:1], ends[:, 1:2], ALU.add))
                done(v.reciprocal(ends[:, 3:4], ends[:, 2:3]))
                done(v.tensor_scalar(sim[:, 1, :], sim[:, 0, :], ends[:, 1:2], ends[:, 3:4], ALU.add, ALU.mult))
                done(v.tensor_scalar(sim[:, 2, :], sim[:, 1, :], 0.9, None, ALU.is_gt))
                done(v.tensor_scalar(sim[:, 3, :], sim[:, 2, :], c("is_reg_row"), None, ALU.max))
                v.tensor_tensor(spread[:], over_k(sim[:, 3, :]), over_g(c("own")), ALU.mult).then_inc(n_spread, 1)
                v.wait_ge(n_pe, 3)
                keys = key_ps[:].rearrange("p (g k) -> p g k", k=S)
                v.tensor_scalar(spread[:], keys, -1.0, 1.0, ALU.mult, ALU.add)
                done(v.tensor_tensor(seen[:], keys, over_k(sim[:, 3, :]), ALU.is_equal))
                v.tensor_tensor(spread[:], spread[:], over_g(c("is_reg_key")), ALU.max)
                done(v.tensor_tensor(seen[:], seen[:], over_g(c("is_reg_key")), ALU.max))
                done(v.tensor_scalar(class_mask[:, :, HPG, :], spread[:], BIG, -BIG, ALU.mult, ALU.add))
                for h in range(HPG):
                    ins_ = v.tensor_scalar(class_mask[:, :, h, :], seen[:], BIG, -BIG, ALU.mult, ALU.add)
                done(ins_)
        pooling.close()
        similar.close()

        def block_of(i, j, lag):
            return 2 * i + (j - lag) // GPB

        def attention(ph, tag, parts, masked):
            cols = parts * S
            score_steps = 2 if masked else 1
            banks = 2 if cols > BLK else 1
            t = dict(
                s_ps=[ps(ph, f"{tag}_s_ps{r}", [P, banks, BLK]) for r in range(2)],
                o_ps=ps(ph, f"{tag}_o_ps", [P, 2, BLK]),
                rows=sb(ph, f"{tag}_rows", [P, 4, cols]),
                stat=sb(ph, f"{tag}_stat", [P, 4, 3, parts]),
                prob=sb(ph, f"{tag}_prob", [P, 2, cols]),
                o_sb=sb(ph, f"{tag}_o_sb", [P, 2, SPB, 4, S]),
                x_ps=ps(ph, f"{tag}_x_ps", [P, 2 if masked else 1, BLK]),
            )
            names = ("scored", "turned", "masked", "topped", "shifted", "exped", "summed", "inverted",
                     "shared", "scaled", "turned_back", "merged", "weighed_half", "weighed", "kept", "projected", "added")
            g = {n: sem(f"{tag}_{n}") for n in names}

            def half_cols(a):
                return a.rearrange("p (b c) -> p b c", b=banks)

            def turn(n, r):
                v.wait_ge(g["scored"], score_steps * (n + 1))
                after(v, g["turned_back"], n - 3)
                v.transpose(half_cols(t["rows"][:, r % 4, :]), t["s_ps"][r % 2][:, :, 0:cols // banks]).then_inc(g["turned"], 1)

            def mask(n, r):
                pool.wait_ge(g["turned"], n + 1)
                rows = t["rows"][:, r % 4, :].rearrange("p (g c) -> p g c", g=HG)
                pool.tensor_tensor(rows, rows, class_mask[:, n, :, :].rearrange("p s k -> p (s k)").unsqueeze(1)
                                   .to_broadcast([P, HG, QX]), ALU.add).then_inc(g["masked"], 1)

            def top(n, r):
                v.wait_ge(g["masked" if masked else "turned"], n + 1)
                v.tensor_reduce(t["stat"][:, r % 4, 0, :], t["rows"][:, r % 4, :].rearrange("p (s k) -> p s k", k=S),
                                AX_X, ALU.max).then_inc(g["topped"], 1)

            def per_row(n, r, which, op, after, signal):
                pool.wait_ge(g[after], n + 1)
                rows = t["rows"][:, r % 4, :].rearrange("p (s k) -> p s k", k=S)
                pool.tensor_tensor(rows, rows, t["stat"][:, r % 4, which, :].unsqueeze(2).to_broadcast([P, parts, S]),
                                   op).then_inc(g[signal], 1)

            def shift(n, r):
                per_row(n, r, 0, ALU.subtract, "topped", "shifted")

            def scale(n, r):
                per_row(n, r, 2, ALU.mult, "shared" if masked else "inverted", "scaled")

            def exp(n, r):
                act.wait_ge(g["shifted"], n + 1)
                act.activation(t["rows"][:, r % 4, :], t["rows"][:, r % 4, :], ACT.Exp).then_inc(g["exped"], 1)

            def total(n, r):
                st = t["stat"][:, r % 4]
                v.wait_ge(g["exped"], n + 1)
                v.tensor_reduce(st[:, 1, :], t["rows"][:, r % 4, :].rearrange("p (s k) -> p s k", k=S),
                                AX_X, ALU.add).then_inc(g["summed"], 1)
                v.wait_ge(g["summed"], n + 1)
                v.reciprocal(st[:, 2, :], st[:, 1, :]).then_inc(g["inverted"], 1)
                if masked:
                    v.wait_ge(g["inverted"], n + 1)
                    v.tensor_tensor(st[:, 2, :], st[:, 2, :], c("share"), ALU.mult).then_inc(g["shared"], 1)

            def turn_back(n, r):
                v.wait_ge(g["scaled"], n + 1)
                v.wait_ge(g["weighed"], 2 * n + 1)
                v.transpose(t["prob"][:, r % 2, :], t["rows"][:, r % 4, :]).then_inc(g["turned_back"], 1)
                if masked:
                    v.wait_ge(g["turned_back"], n + 1)
                    pr = t["prob"][:, r % 2, :].rearrange("p (g c) -> p g c", g=HG)
                    first = pr[:, :, 0:HPG * S].rearrange("p g (h q) -> p g h q", q=S)[:, :, :, 0:REG]
                    second = pr[:, :, HPG * S:HPG * S + HPG * REG].rearrange("p g (h q) -> p g h q", q=REG)
                    v.tensor_tensor(first, first, second, ALU.add).then_inc(g["merged"], 1)

            def weigh(pe, n, r, values, width):
                pe.wait_ge(g["merged" if masked else "turned_back"], n + 1)
                wait_apart(pe, g["kept"], n)
                for turn_, s in enumerate((0, 2, 1, 3)):
                    rows = slice(32 * s, 32 * s + 32)
                    if turn_ >= 2:
                        wait_apart(pe, g["weighed_half"], 2 * n + turn_ - 1)
                    for m in range(4):
                        ins_ = pe.matmul(t["o_ps"][32 * m:32 * m + 32, s // 2, (s % 2) * P:(s % 2) * P + P],
                                         values(rows, m), t["prob"][rows, r % 2, m * width:m * width + 4 * S],
                                         start=True, stop=True)
                    ins_.then_inc(g["weighed_half" if turn_ < 2 else "weighed"], 1)

            def keep(n, blk, r):
                act.wait_ge(g["weighed"], 2 * n + 5)
                act.wait_ge(g["projected"], blk + 1)
                dst = t["o_sb"][:, (r // GPB) % 2, 4 * (r % GPB):4 * (r % GPB) + 4, :, :].rearrange("p s h q -> p (s h q)")
                act.activation(dst.rearrange("p (b c) -> p b c", b=2), t["o_ps"][:, :, 0:2 * P], ACT.Copy).then_inc(g["kept"], 1)

            def project(pe, blk, r, weights):
                half = (r // GPB) % 2
                x_bank = t["x_ps"][:, half if masked else 0, :]
                pe.wait_ge(g["kept"], GPB * (blk + 1))
                pe.wait_ge(g["added"], blk + 1)
                for h in range(4):
                    ins_ = pe.matmul(x_bank, weights[:, h, :], t["o_sb"][:, half, :, h, :], start=(h == 0), stop=(h == 3))
                ins_.then_inc(g["projected"], 1)

            t.update(g)
            t.update(turn=turn, mask=mask, top=top, shift=shift, scale=scale, exp=exp, total=total,
                     turn_back=turn_back, weigh=weigh, keep=keep, project=project)
            return t

        L_SCORE, L_TOP, L_SUM, L_BACK, L_ADD = 4, 5, 6, 7, 8

        def softmax_on_vector(t, i, j, live):
            if live(L_BACK):
                t["turn_back"](SLOTS * i + j - L_BACK, j - L_BACK)
            if live(L_SUM):
                t["total"](SLOTS * i + j - L_SUM, j - L_SUM)
            if live(L_TOP):
                t["top"](SLOTS * i + j - L_TOP, j - L_TOP)
            if live(L_SCORE):
                t["turn"](SLOTS * i + j - L_SCORE, j - L_SCORE)

        def softmax_on_pool(t, i, j, live, masked):
            if live(L_SUM):
                t["scale"](SLOTS * i + j - L_SUM, j - L_SUM)
            if live(L_TOP):
                t["shift"](SLOTS * i + j - L_TOP, j - L_TOP)
            if masked and live(L_SCORE):
                t["mask"](SLOTS * i + j - L_SCORE, j - L_SCORE)

        def softmax_on_scalar(t, i, j, live):
            if live(L_TOP):
                t["exp"](SLOTS * i + j - L_TOP, j - L_TOP)
            if live(L_BACK):
                t["keep"](SLOTS * i + j - L_BACK, block_of(i, j, L_BACK), j - L_BACK)

        with ExitStack() as ph:
            k_st = sb(ph, "k_st", [P, 2, BLK])
            v_st = sb(ph, "v_st", [P, 2, GPB, C])
            q_x = sb(ph, "q_x", [P, 2, SPB, QX])
            head_scale = sb(ph, "head_scale", [P, HPG])
            t = attention(ph, "d", HG * (HPG + 1), masked=True)
            d_k, d_v = [sem("d_k0"), sem("d_k1")], [sem("d_v0"), sem("d_v1")]
            d_q, d_clear, d_half = sem("d_q"), sem("d_clear"), sem("d_half")
            block = ph.enter_context(nc.Block())

            @block.sync
            def _(sp):
                def stage(blk, half):
                    if not isinstance(blk, int):
                        sp.wait_ge(t["weighed"], 2 * GPB * (blk - 1) + 3)
                    sp.dma_start(k_st[:, half, :], k_f[:, bass.ds(blk * BLK, BLK)]).then_inc(d_k[half], 16)
                    sp.dma_start(v_st[:, half], v_t[:, bass.ds(blk * GPB, GPB), :]).then_inc(d_v[half], 16)

                for i, half in blocks(sp):
                    stage(2 * i + half, half)

            @block.tensor
            def _(pe):
                pe.sem_inc(t["projected"], 2)
                pe.sem_inc(t["weighed"], 3)
                for i, j, live in slots(pe, L_ADD):
                    if live(L_SCORE):
                        n, r = SLOTS * i + j - L_SCORE, (j - L_SCORE) % SLOTS
                        blk, half, g = block_of(i, j, L_SCORE), r // GPB, r % GPB
                        if g == 0:
                            pe.wait_ge(d_q, GPB * (blk + 1))
                            pe.wait_ge(d_k[half], 16 * (i if j >= L_SCORE else i - 1) + 16)
                        wait_apart(pe, t["turned"], n - 1)
                        for turn_, m in enumerate((0, 2, 1, 3)):
                            rows = slice(32 * m, 32 * m + 32)
                            if turn_ >= 2:
                                wait_apart(pe, d_half, 2 * n + turn_ - 1)
                            for s in range(SEQ):
                                ins_ = pe.matmul(t["s_ps"][r % 2][32 * s:32 * s + 32, m // 2, (m % 2) * QX:(m % 2) * QX + QX],
                                                 k_st[rows, half, g * P + 32 * s:g * P + 32 * s + 32],
                                                 q_x[rows, half, g * SEQ + s, :], start=True, stop=True)
                            ins_.then_inc(d_half if turn_ < 2 else t["scored"], 1)
                    if live(L_BACK):
                        n, r = SLOTS * i + j - L_BACK, (j - L_BACK) % SLOTS
                        if r % GPB == 0:
                            pe.wait_ge(d_v[r // GPB], 16 * (i if j >= L_BACK else i - 1) + 16)
                        t["weigh"](pe, n, r, lambda rows, m, r=r: v_st[rows, r // GPB, r % GPB, 32 * m:32 * m + 32], QX)
                    if live(L_ADD) and (j - L_ADD) % GPB == GPB - 1:
                        t["project"](pe, block_of(i, j, L_ADD), (j - L_ADD) % SLOTS, wproj_h)

            @block.gpsimd
            def _(eng):
                pool.memset(q_x[:], 0.0).then_inc(d_clear, 1)
                for i, j, live in slots(pool, L_ADD):
                    softmax_on_pool(t, i, j, live, True)

            @block.scalar
            def _(eng):
                for i, j, live in slots(act, L_ADD):
                    softmax_on_scalar(t, i, j, live)

            @block.vector
            def _(eng):
                v.tensor_scalar(head_scale[:], c("head_row"), float(D0) ** -0.5, None, ALU.mult).then_inc(d_clear, 1)
                v.wait_ge(d_clear, 2)
                v.sem_inc(t["added"], 2)
                for i, j, live in slots(v, L_ADD):
                    softmax_on_vector(t, i, j, live)
                    if live(0):
                        blk, half, h = 2 * i + j // GPB, j // GPB, j % GPB
                        if h == 0:
                            after(v, t["scored"], 2 * GPB * (blk - 1))
                        q = q_f[:, bass.ds(blk * BLK, BLK)].rearrange("p (s q) -> p s q", q=S)
                        v.tensor_scalar(q_x[:, half, :, h * S:(h + 1) * S], q, head_scale[:, h:h + 1], None, ALU.mult)
                        v.tensor_scalar(q_x[:, half, :, HPG * S + h * REG:HPG * S + (h + 1) * REG], q[:, :, 0:REG],
                                        head_scale[:, h:h + 1], None, ALU.mult).then_inc(d_q, 1)
                    if live(L_ADD) and (j - L_ADD) % GPB == GPB - 1:
                        blk = block_of(i, j, L_ADD)
                        v.wait_ge(t["projected"], blk + 3)
                        xs = x_f[:, bass.ds(blk * BLK, BLK)]
                        v.scalar_tensor_tensor(out=xs, in0=t["x_ps"][:, ((j - L_ADD) // GPB) % 2, :],
                                               scalar=bproj[:, 0:1], in1=xs, op0=ALU.add, op1=ALU.add).then_inc(t["added"], 1)
        layer0.close()

        layer1 = top.enter_context(ExitStack())
        y_f = sb(layer1, "y_f", [P, TOK])
        yn_f = sb(layer1, "yn_f", [P, TOK])

        q_h = sb(layer1, "q_h", [P, 2, SPB, H1, S])
        k_h = sb(layer1, "k_h", [P, 2, BLK])

        E_MAP, E_NORM, E_TURN, E_OUT = 1, 2, 3, 4

        with ExitStack() as ph:
            x_st = sb(ph, "x_st", [P, 2, BLK])
            w_st = sb(ph, "w_st", [P, 4, SEQ, C])
            subject = sb(ph, "subject", [1, B], I32)
            subject_w = sb(ph, "subject_w", [SUBJ, B], I32)
            subject_f = sb(ph, "subject_f", [SUBJ, B])
            is_subject = sb(ph, "is_subject", [SUBJ, B, S])
            is_st = sb(ph, "is_st", [SUBJ, 2, BLK])
            rank = sb(ph, "rank", [SUBJ, 1])
            bias = sb(ph, "bias", [SUBJ, C])
            y_t = sb(ph, "y_t", [P, 2, GPB, C])
            yn_t = sb(ph, "yn_t", [P, 2, GPB, C])
            junk = sb(ph, "junk", [P, 4, C])
            sq = sb(ph, "sq", [P, 2, 3, GPB])
            y_ps = [ps(ph, f"y_ps{r}", [P, BLK]) for r in range(4)]
            yt_ps = [ps(ph, f"yt_ps{r}", [P, BLK]) for r in range(2)]
            nt_ps = [ps(ph, f"nt_ps{r}", [P, BLK]) for r in range(2)]
            e_ld, e_x, e_is = sem("e_ld"), [sem("e_x0"), sem("e_x1")], [sem("e_is0"), sem("e_is1")]
            e_ready, e_w, e_w2, e_y, e_yc, e_sq, e_ms, e_rt, e_inv, e_yn = (
                sem(n) for n in ("e_ready", "e_w", "e_w2", "e_y", "e_yc", "e_sq", "e_ms", "e_rt", "e_inv", "e_yn"))
            f_const = sem("f_const")
            e_yt, e_nt, e_ytc, e_ntc, e_bias = (sem(n) for n in ("e_yt", "e_nt", "e_ytc", "e_ntc", "e_bias"))
            block = ph.enter_context(nc.Block())

            @block.sync
            def _(sp):
                sp.dma_start(subject[:], ins["itok_B_0_7"].rearrange("(a b) -> a b", a=1)).then_inc(e_ld, 16)
                sp.dma_start(subject_w[:], ins["itok_B_0_7"].partition_broadcast(SUBJ)).then_inc(e_ld, 16)
                sp.dma_start(bias[:], ins["L1_cond_bias"]).then_inc(e_ld, 16)
                sp.wait_ge(e_ready, 3)

                def stage(blk, half):
                    after(sp, e_y, GPB * (blk - 1))
                    sp.dma_start(x_st[:, half, :], x_f[:, bass.ds(blk * BLK, BLK)]).then_inc(e_x[half], 16)
                    sp.dma_start(is_st[:, half, :], is_subject[:].rearrange("p b s -> p (b s)")[:, bass.ds(blk * BLK, BLK)])\
                        .then_inc(e_is[half], 16)

                for i, half in blocks(sp):
                    stage(2 * i + half, half)

            def fetch(eng, copy, n, r, seqs, signal):
                for s in seqs:
                    which = eng.value_load(subject[0:1, bass.ds(n * SEQ + s, 1)], min_val=0, max_val=SUBJ - 1)
                    ins_ = copy(w_st[:, r % 4, s, :], w_subj_t[:, bass.ds(which, 1), :].rearrange("p a o -> p (a o)"))
                ins_.then_inc(signal, 1)

            @block.gpsimd
            def _(eng):
                pool.iota(rank[:], [[0, 1]], base=0, channel_multiplier=1, allow_small_or_imprecise_dtypes=True).then_inc(e_ready, 1)
                for half in range(2):
                    ins_ = pool.tensor_copy(q_h[96:128, half].rearrange("p s h q -> p (s h) q"),
                                            c("causal")[96:128, :].unsqueeze(1).to_broadcast([S, SPB * H1, S]))
                ins_.then_inc(f_const, 1)
                ins_ = pool.tensor_copy(k_h[96:128].rearrange("p a (s k) -> p (a s) k", k=S),
                                        c("own")[96:128, :].unsqueeze(1).to_broadcast([S, 2 * SPB, S])).then_inc(f_const, 1)

            @block.tensor
            def _(pe):
                pe.wait_ge(e_ready, 3)
                for i, j, live in slots(pe, E_OUT):
                    if live(E_MAP):
                        n, r = SLOTS * i + j - E_MAP, (j - E_MAP) % SLOTS
                        g, half = r % GPB, r // GPB
                        if g == 0:
                            block_i = i if j >= E_MAP else i - 1
                            pe.wait_ge(e_x[half], 16 * block_i + 16)
                            pe.wait_ge(e_is[half], 16 * block_i + 16)
                        after(pe, e_yc, n - 3)
                        after(pe, e_sq, n - 3)
                        y = y_ps[r % 4]
                        pe.matmul(y[:, 0:C], is_st[:, half, g * P:(g + 1) * P], bias[:], start=True, stop=False,
                                  skip_group_check=True).then_inc(e_bias, 1)
                        pe.wait_ge(e_w, n + 1)
                        pe.wait_ge(e_w2, n + 1)
                        pe.wait_ge(e_bias, n + 1)
                        for s in range(SEQ):
                            ins_ = pe.matmul(y[32 * s:32 * s + 32, 0:C], x_st[:, half, g * P + 32 * s:g * P + 32 * s + 32],
                                             w_st[:, r % 4, s, :], start=False, stop=True, skip_group_check=True)
                        ins_.then_inc(e_y, 1)
                    if live(E_TURN) and (j - E_TURN) % GPB == GPB - 1:
                        blk, half = block_of(i, j, E_TURN), ((j - E_TURN) // GPB) % 2
                        pe.wait_ge(e_yc, GPB * (blk + 1))
                        after(pe, e_ytc, blk - 1)
                        after(pe, e_ntc, blk - 1)
                        for g in range(GPB):
                            ins_ = pe.transpose(yt_ps[half][:, g * P:(g + 1) * P], y_t[:, half, g, :], ident)
                        ins_.then_inc(e_yt, 1)
                        pe.wait_ge(e_yn, blk + 1)
                        for g in range(GPB):
                            ins_ = pe.transpose(nt_ps[half][:, g * P:(g + 1) * P], yn_t[:, half, g, :], ident)
                        ins_.then_inc(e_nt, 1)

            @block.scalar
            def _(eng):
                act.wait_ge(e_ld, 48)
                for i, j, live in slots(act, E_OUT):
                    if live(0):
                        n = SLOTS * i + j
                        after(act, e_y, n - 3)
                        fetch(act, lambda o, a: act.activation(o, a, ACT.Copy), n, j, (0, 1), e_w)
                    if live(E_NORM) and (j - E_NORM) % GPB == GPB - 1:
                        blk, half = block_of(i, j, E_NORM), ((j - E_NORM) // GPB) % 2
                        act.wait_ge(e_ms, blk + 1)
                        act.activation(sq[:, half, 2, :], sq[:, half, 1, :], ACT.Sqrt).then_inc(e_rt, 1)
                    if live(E_MAP):
                        n, r = SLOTS * i + j - E_MAP, (j - E_MAP) % SLOTS
                        act.wait_ge(e_y, n + 1)
                        after(act, e_sq, n - 3)
                        act.activation(junk[:, r % 4, :], y_ps[r % 4][:, 0:C], ACT.Square,
                                       accum_out=sq[:, r // GPB, 0, r % GPB:r % GPB + 1]).then_inc(e_sq, 1)
                    if live(E_OUT) and (j - E_OUT) % GPB == GPB - 1:
                        blk, half = block_of(i, j, E_OUT), ((j - E_OUT) // GPB) % 2
                        act.wait_ge(e_yt, blk + 1)
                        act.activation(y_f[:, bass.ds(blk * BLK, BLK)], yt_ps[half][:], ACT.Copy).then_inc(e_ytc, 1)

            @block.vector
            def _(eng):
                v.wait_ge(e_ld, 48)
                v.wait_ge(e_ready, 1)
                v.tensor_copy(subject_f[:], subject_w[:]).then_inc(e_ready, 1)
                v.wait_ge(e_ready, 2)
                v.tensor_scalar(is_subject[:], subject_f[:].unsqueeze(2).to_broadcast([SUBJ, B, S]), rank[:, 0:1], None,
                                ALU.is_equal).then_inc(e_ready, 1)
                for i, j, live in slots(v, E_OUT):
                    if live(0):
                        n = SLOTS * i + j
                        after(v, e_y, n - 3)
                        fetch(v, v.tensor_copy, n, j, (2, 3), e_w2)
                    if live(E_NORM) and (j - E_NORM) % GPB == GPB - 1:
                        blk, half = block_of(i, j, E_NORM), ((j - E_NORM) // GPB) % 2
                        v.wait_ge(e_rt, blk + 1)
                        v.reciprocal(sq[:, half, 1, :], sq[:, half, 2, :]).then_inc(e_inv, 1)
                        v.wait_ge(e_inv, blk + 1)
                        v.wait_ge(e_yc, GPB * (blk + 1))
                        after(v, e_nt, blk - 1)
                        v.tensor_tensor(yn_t[:, half], y_t[:, half], sq[:, half, 1, :].unsqueeze(2).to_broadcast([P, GPB, C]),
                                        ALU.mult).then_inc(e_yn, 1)
                    if live(E_MAP):
                        n, r = SLOTS * i + j - E_MAP, (j - E_MAP) % SLOTS
                        g, half = r % GPB, r // GPB
                        v.wait_ge(e_sq, n + 1)
                        if g == 0:
                            after(v, e_yt, block_of(i, j, E_MAP) - 1)
                        v.tensor_copy(y_t[:, half, g, :], y_ps[r % 4][:, 0:C]).then_inc(e_yc, 1)
                        if g == GPB - 1:
                            v.tensor_scalar(sq[:, half, 1, :], sq[:, half, 0, :], 1.0 / C, EPS, ALU.mult, ALU.add).then_inc(e_ms, 1)
                    if live(E_OUT) and (j - E_OUT) % GPB == GPB - 1:
                        blk, half = block_of(i, j, E_OUT), ((j - E_OUT) // GPB) % 2
                        v.wait_ge(e_nt, blk + 1)
                        v.tensor_copy(yn_f[:, bass.ds(blk * BLK, BLK)], nt_ps[half][:]).then_inc(e_ntc, 1)

        with ExitStack() as ph:
            y_st = sb(ph, "y_st", [P, 2, BLK])
            k_tmp = sb(ph, "k_tmp", [64, BLK])
            lat = sb(ph, "lat", [P, 2, GPB, S])
            q_ps = [ps(ph, f"q_ps{r}", [P, BLK]) for r in range(2)]
            kv_ps = ps(ph, "kv_ps", [P, BLK])
            t = attention(ph, "f", H1, masked=False)
            f_y = [sem("f_y0"), sem("f_y1")]
            f_q, f_qt, f_ka, f_kb, f_kl, f_kac, f_kt, f_kbc, f_klc = (
                sem(n) for n in ("f_q", "f_qt", "f_ka", "f_kb", "f_kl", "f_kac", "f_kt", "f_kbc", "f_klc"))
            block = ph.enter_context(nc.Block())

            @block.sync
            def _(sp):
                def stage(blk, half):
                    after(sp, f_q, H1 * (blk - 1))
                    after(sp, f_kl, blk - 1)
                    sp.dma_start(y_st[:, half, :], yn_f[:, bass.ds(blk * BLK, BLK)]).then_inc(f_y[half], 16)

                for i, half in blocks(sp):
                    stage(2 * i + half, half)

            @block.tensor
            def _(pe):
                pe.sem_inc(t["projected"], 2)
                pe.sem_inc(t["weighed"], 3)
                for i, j, live in slots(pe, L_ADD):
                    if live(L_SCORE):
                        n, r = SLOTS * i + j - L_SCORE, (j - L_SCORE) % SLOTS
                        blk, half, g = block_of(i, j, L_SCORE), r // GPB, r % GPB
                        if g == 0:
                            pe.wait_ge(f_qt, H1 * (blk + 1))
                            pe.wait_ge(f_kbc, blk + 1)
                        after(pe, t["turned"], n - 1)
                        for s in range(SEQ):
                            ins_ = pe.matmul(t["s_ps"][r % 2][32 * s:32 * s + 32, 0, :], k_h[:, half, g * P + 32 * s:g * P + 32 * s + 32],
                                             q_h[:, half, g * SEQ + s, :, :], start=True, stop=True)
                        ins_.then_inc(t["scored"], 1)
                    if live(L_BACK):
                        n, r = SLOTS * i + j - L_BACK, (j - L_BACK) % SLOTS
                        if r % GPB == 0:
                            pe.wait_ge(f_klc, block_of(i, j, L_BACK) + 1)
                        t["weigh"](pe, n, r, lambda rows, m, r=r: lat[rows, r // GPB, r % GPB, :], 4 * S)
                    if live(L_ADD) and (j - L_ADD) % GPB == GPB - 1:
                        t["project"](pe, block_of(i, j, L_ADD), (j - L_ADD) % SLOTS, w_o)
                    if live(0):
                        blk, half, g = block_of(i, j, 0), j // GPB, j % GPB
                        if g == 0:
                            pe.wait_ge(f_y[half], 16 * i + 16)
                            after(pe, f_klc, blk)
                            pe.matmul(kv_ps[0:96, :], wk_a[:], y_st[:, half, :], start=True, stop=True).then_inc(f_ka, 1)
                        if g == 1:
                            pe.wait_ge(f_kac, blk + 1)
                            pe.matmul(kv_ps[0:64, :], wk_b[:], y_st[:, half, :], start=True, stop=True).then_inc(f_kb, 1)
                        if g == 2:
                            pe.wait_ge(f_kt, blk + 1)
                            for m in range(GPB):
                                ins_ = pe.matmul(kv_ps[:, m * S:(m + 1) * S], y_st[:, half, m * P:(m + 1) * P], w_lat[:],
                                                 start=True, stop=True)
                            ins_.then_inc(f_kl, 1)
                        for h in range(4 * g, 4 * g + 4):
                            after(pe, f_qt, blk * H1 + h - 1)
                            pe.matmul(q_ps[h % 2][0:96, :], wq_heads[:, h, :], y_st[:, half, :], start=True, stop=True).then_inc(f_q, 1)

            @block.gpsimd
            def _(eng):
                for i, j, live in slots(pool, L_ADD):
                    softmax_on_pool(t, i, j, live, False)

            @block.scalar
            def _(eng):
                for i, j, live in slots(act, L_ADD):
                    softmax_on_scalar(t, i, j, live)
                    if live(0) and j % GPB == 2:
                        blk, half = block_of(i, j, 0), j // GPB
                        act.wait_ge(f_kl, blk + 1)
                        if not isinstance(blk, int):
                            act.wait_ge(t["weighed"], 2 * GPB * (blk - 1) + 3)
                        act.activation(lat[:, half].rearrange("p g r -> p (g r)"), kv_ps[:, 0:GPB * S], ACT.Copy).then_inc(f_klc, 1)

            @block.vector
            def _(eng):
                def over_s(a):
                    return a.unsqueeze(1).to_broadcast([a.shape[0], SPB, S])

                def by_s(a):
                    return a.rearrange("p (s q) -> p s q", q=S)

                v.sem_inc(t["added"], 1)
                for i, j, live in slots(v, L_ADD):
                    softmax_on_vector(t, i, j, live)
                    if live(0):
                        blk, half, g = block_of(i, j, 0), j // GPB, j % GPB
                        if g == 0:
                            after(v, t["scored"], GPB * (blk - 1))
                            v.wait_ge(f_ka, blk + 1)
                            v.tensor_tensor(by_s(k_h[0:96, half, :]), by_s(kv_ps[0:96, :]), over_s(c("k_turn")[0:96, :]),
                                            ALU.mult).then_inc(f_kac, 1)
                        if g == 1:
                            v.wait_ge(f_kb, blk + 1)
                            after(v, f_kbc, blk)
                            v.tensor_tensor(by_s(k_tmp[:]), by_s(kv_ps[0:64, :]), over_s(c("k_cross")[0:64, :]), ALU.mult).then_inc(f_kt, 1)
                            v.wait_ge(f_kt, blk + 1)
                            v.wait_ge(f_kac, blk + 1)
                            v.tensor_tensor(k_h[0:64, half, :], k_h[0:64, half, :], k_tmp[:], ALU.add).then_inc(f_kbc, 1)
                        for h in range(4 * g, 4 * g + 4):
                            v.wait_ge(f_q, blk * H1 + h + 1)
                            v.tensor_tensor(q_h[0:96, half, :, h, :], by_s(q_ps[h % 2][0:96, :]), over_s(c("q_turn")[0:96, :]),
                                            ALU.mult).then_inc(f_qt, 1)
                    if live(L_ADD) and (j - L_ADD) % GPB == GPB - 1:
                        blk = block_of(i, j, L_ADD)
                        v.wait_ge(t["projected"], blk + 3)
                        ys = y_f[:, bass.ds(blk * BLK, BLK)]
                        v.tensor_tensor(ys, t["x_ps"][:, 0, :], ys, ALU.add).then_inc(t["added"], 1)

        moe = top.enter_context(ExitStack())
        logits = sb(moe, "logits", [P, GROUPS, E])
        comb_t = sb(moe, "comb_t", [3 * (E + 1), TOK], BF16)
        z_f = yn_f
        with ExitStack() as ph:
            z_st = sb(ph, "z_st", [P, 2, BLK])
            z2 = sb(ph, "z2", [P, 2, BLK])
            ms = sb(ph, "ms", [P, 2, 3, GPB])
            diag = sb(ph, "diag", [P, 2, GPB, P])
            l_ps = [ps(ph, f"l_ps{r}", [P, GPB, 16]) for r in range(2)]
            r_ps = [ps(ph, f"r_ps{r}", [P, BLK]) for r in range(2)]
            g_z = [sem("g_z0"), sem("g_z1")]
            g_sq, g_l, g_ms, g_rt, g_inv, g_lm, g_lb, g_dg, g_r, g_zn, g_sum = (
                sem(n) for n in ("g_sq", "g_l", "g_ms", "g_rt", "g_inv", "g_lm", "g_lb", "g_dg", "g_r", "g_zn", "g_sum"))
            block = ph.enter_context(nc.Block())

            @block.sync
            def _(sp):
                for i, half in blocks(sp):
                    blk = 2 * i + half
                    after(sp, g_l, blk - 1)
                    sp.dma_start(z_st[:, half, :], y_f[:, bass.ds(blk * BLK, BLK)]).then_inc(g_z[half], 16)

            @block.gpsimd
            def _(eng):
                for i in pairs_of_blocks(pool):
                    pair = bass.ds(i * 2 * BLK, 2 * BLK)
                    pool.tensor_tensor(x_f[:, pair], x_f[:, pair], y_f[:, pair], ALU.add).then_inc(g_sum, 1)

            @block.scalar
            def _(eng):
                for i, j, live in skewed_blocks(act, 1):
                    if live(0):
                        blk = 2 * i + j
                        after(act, g_l, blk - 1)
                        act.activation(z2[:, j, :], y_f[:, bass.ds(blk * BLK, BLK)], ACT.Square).then_inc(g_sq, 1)
                    if live(1):
                        blk, half = 2 * i + j - 1, (j - 1) % 2
                        act.wait_ge(g_ms, blk + 1)
                        act.activation(ms[:, half, 1, :], ms[:, half, 0, :], ACT.Sqrt).then_inc(g_rt, 1)

            @block.tensor
            def _(pe):
                for i, j, live in skewed_blocks(pe, 1):
                    if live(0):
                        blk = 2 * i + j
                        pe.wait_ge(g_z[j], 16 * i + 16)
                        after(pe, g_lm, blk - 1)
                        after(pe, g_ms, blk - 1)
                        for g in range(GPB):
                            pe.matmul(l_ps[j][:, g, 0:E], z_st[:, j, g * P:(g + 1) * P], wgate[:], start=True, stop=True)
                        pe.wait_ge(g_sq, blk + 1)
                        for g in range(GPB):
                            ins_ = pe.matmul(l_ps[j][:, g, E:E + 1], z2[:, j, g * P:(g + 1) * P], ones[:, 0:1], start=True, stop=True)
                        ins_.then_inc(g_l, 1)
                    if live(1):
                        blk, half = 2 * i + j - 1, (j - 1) % 2
                        pe.wait_ge(g_dg, blk + 1)
                        after(pe, g_zn, blk - 1)
                        pe.matmul(r_ps[half][:], ones[:], diag[:, half].rearrange("p g t -> p (g t)"), start=True, stop=True)\
                            .then_inc(g_r, 1)

            @block.vector
            def _(eng):
                for i, j, live in skewed_blocks(v, 2):
                    if live(1):
                        blk, half = 2 * i + j - 1, (j - 1) % 2
                        lg = logits[:, bass.ds(blk * GPB, GPB), :]
                        v.wait_ge(g_rt, blk + 1)
                        v.reciprocal(ms[:, half, 2, :], ms[:, half, 1, :]).then_inc(g_inv, 1)
                        v.wait_ge(g_inv, blk + 1)
                        after(v, g_r, blk - 1)
                        for g in range(GPB):
                            ins_ = v.tensor_scalar(diag[:, half, g, :], ident, ms[:, half, 2, g:g + 1], None, ALU.mult)
                        ins_.then_inc(g_dg, 1)
                        v.tensor_tensor(lg, l_ps[half][:, :, 0:E], ms[:, half, 2, :].unsqueeze(2).to_broadcast([P, GPB, E]),
                                        ALU.mult).then_inc(g_lm, 1)
                        v.wait_ge(g_lm, blk + 1)
                        v.tensor_tensor(lg, lg, gate_b[:].unsqueeze(1).to_broadcast([P, GPB, E]), ALU.add).then_inc(g_lb, 1)
                    if live(0):
                        blk = 2 * i + j
                        v.wait_ge(g_l, blk + 1)
                        after(v, g_rt, blk - 1)
                        v.tensor_scalar(ms[:, j, 0, :], l_ps[j][:, :, E], 1.0 / C, EPS, ALU.mult, ALU.add).then_inc(g_ms, 1)
                    if live(2):
                        blk, half = 2 * i + j - 2, j
                        v.wait_ge(g_r, blk + 1)
                        at = bass.ds(blk * BLK, BLK)
                        v.tensor_tensor(z_f[:, at], y_f[:, at], r_ps[half][:], ALU.mult).then_inc(g_zn, 1)

        with ExitStack() as ph:
            W = [P, GROUPS, E]
            best = sb(ph, "best", W)
            chosen = sb(ph, "chosen", [P, 2, GROUPS, E])
            rest = sb(ph, "rest", W)
            ex = sb(ph, "ex", W)
            top_of = sb(ph, "top_of", [P, 4, GROUPS])
            comb = sb(ph, "comb", [P, GROUPS, E + 1])
            left = sb(ph, "left", [P, GROUPS, E + 1])
            parts = sb(ph, "parts", [P, GROUPS, 3, E + 1], BF16)
            ident_b = sb(ph, "ident_b", [P, P], BF16)
            c_ps = [ps(ph, f"c_ps{n}", [3 * (E + 1), 8, P], BF16) for n in range(4)]
            k_step, k_shift, k_exp, k_parts, k_t = (sem(n) for n in ("k_step", "k_shift", "k_exp", "k_parts", "k_t"))
            block = ph.enter_context(nc.Block())

            @block.scalar
            def _(eng):
                act.wait_ge(k_shift, 1)
                act.activation(ex[:], ex[:], ACT.Exp).then_inc(k_exp, 1)

            @block.tensor
            def _(pe):
                pe.wait_ge(k_parts, 1)
                for n in range(GROUPS):
                    ins_ = pe.transpose(c_ps[n // 8][:, n % 8, :], parts[:, n].rearrange("p a e -> p (a e)"), ident_b[:])
                    if n % 8 == 7:
                        ins_.then_inc(k_t, 1)

            @block.vector
            def _(eng):
                count = [0]

                def done(ins_):
                    count[0] += 1
                    ins_.then_inc(k_step, 1)
                    v.wait_ge(k_step, count[0])

                def over_e(a):
                    return a.unsqueeze(2).to_broadcast(W)

                def choose(src, rnd):
                    done(v.tensor_reduce(top_of[:, rnd, :], src, AX_X, ALU.max))
                    done(v.tensor_tensor(best[:], src, over_e(top_of[:, rnd, :]), ALU.is_equal))
                    done(v.tensor_tensor(best[:], best[:], c("first").unsqueeze(1).to_broadcast(W), ALU.mult))
                    done(v.tensor_reduce(top_of[:, 2, :], best[:], AX_X, ALU.max))
                    done(v.tensor_tensor(chosen[:, rnd], best[:], over_e(top_of[:, 2, :]), ALU.is_equal))

                v.tensor_copy(ident_b[:], ident)
                v.memset(comb[:, :, E:E + 1], 1.0)
                choose(logits[:], 0)
                v.tensor_tensor(ex[:], logits[:], over_e(top_of[:, 0, :]), ALU.subtract).then_inc(k_shift, 1)
                done(v.tensor_scalar(rest[:], chosen[:, 0], -BIG, None, ALU.mult))
                done(v.tensor_tensor(rest[:], rest[:], logits[:], ALU.add))
                choose(rest[:], 1)
                done(v.tensor_tensor(rest[:], chosen[:, 0], chosen[:, 1], ALU.add))
                v.wait_ge(k_exp, 1)
                done(v.tensor_tensor(ex[:], ex[:], rest[:], ALU.mult))
                done(v.tensor_reduce(top_of[:, 2, :], ex[:], AX_X, ALU.add))
                done(v.reciprocal(top_of[:, 3, :], top_of[:, 2, :]))
                done(v.tensor_tensor(comb[:, :, 0:E], ex[:], over_e(top_of[:, 3, :]), ALU.mult))
                done(v.tensor_copy(parts[:, :, 0, :], comb[:]))
                done(v.tensor_tensor(left[:], comb[:], parts[:, :, 0, :], ALU.subtract))
                done(v.tensor_copy(parts[:, :, 1, :], left[:]))
                done(v.tensor_tensor(left[:], left[:], parts[:, :, 1, :], ALU.subtract))
                v.tensor_copy(parts[:, :, 2, :], left[:]).then_inc(k_parts, 1)
                for n in range(4):
                    v.wait_ge(k_t, n + 1)
                    ins_ = v.tensor_copy(comb_t[:, n * 8 * P:(n + 1) * 8 * P], c_ps[n][:].rearrange("p a t -> p (a t)"))
                done(ins_)

        with ExitStack() as ph:
            tanh = sb(ph, "tanh", [P, 2, BLK])
            gated = sb(ph, "gated", [P, 2, BLK])
            hidden = sb(ph, "hidden", [P, 2, BLK])
            total_f = sb(ph, "total_f", [P, 2, BLK])
            total_t = sb(ph, "total_t", [P, 2, GPB, C])
            g_ps, u_ps = ([ps(ph, f"{n}_ps{r}", [P, BLK]) for r in range(2)] for n in ("g", "u"))
            m_ps = ps(ph, "mix_ps", [P, BLK])
            dn_ps = [ps(ph, f"dn_ps{r}", [P, BLK]) for r in range(2)]
            ot_ps = ps(ph, "ot_ps", [P, BLK])
            h_g, h_u, h_m, h_th, h_a, h_b, h_h, h_d, h_dn, h_sum, h_t, h_tc = (
                sem(n) for n in ("h_g", "h_u", "h_m", "h_th", "h_a", "h_b", "h_h", "h_d", "h_dn", "h_sum", "h_t", "h_tc"))
            h_out = [sem("h_out0"), sem("h_out1")]
            block = ph.enter_context(nc.Block())
            SPAN = [P] * (PAIRS - 1) + [I]

            @block.sync
            def _(sp):
                for i, half in blocks(sp):
                    blk = 2 * i + half
                    sp.wait_ge(h_tc, blk + 1)
                    sp.dma_start(out_groups[:, bass.ds(blk * GPB, GPB), :], total_t[:, half]).then_inc(h_out[half], 16)
                for half in range(2):
                    sp.wait_ge(h_out[half], 16 * NBLK // 2)

            @block.tensor
            def _(pe):
                for i in pairs_of_blocks(pe):
                    for k in range(2 * PAIRS + 1):
                        if k < 2 * PAIRS:
                            half, p = k // PAIRS, k % PAIRS
                            m = i * 2 * PAIRS + k
                            w = SPAN[p]
                            z = z_f[:, bass.ds((2 * i + half) * BLK, BLK)]
                            def before(sem_, lag):
                                wait_apart(pe, sem_, m - lag + 1 if k >= lag else i * 2 * PAIRS)
                            before(h_a, 2)
                            pe.matmul(g_ps[k % 2][0:w, :], wg[:, 2 * p:2 * p + w // I, :], z, start=True, stop=True).then_inc(h_g, 1)
                            before(h_b, 2)
                            pe.matmul(u_ps[k % 2][0:w, :], wu[:, 2 * p:2 * p + w // I, :], z, start=True, stop=True).then_inc(h_u, 1)
                            before(h_h, 1)
                            pe.matmul(m_ps[:], pick[:, p, :], comb_t[:, bass.ds((2 * i + half) * BLK, BLK)],
                                      start=True, stop=True).then_inc(h_m, 1)
                        if k >= 1:
                            q, half, p = k - 1, (k - 1) // PAIRS, (k - 1) % PAIRS
                            w = SPAN[p]
                            wait_apart(pe, h_h, i * 2 * PAIRS + q + 1)
                            if p == 0:
                                after(pe, h_sum, 2 * i)
                            pe.matmul(dn_ps[half][:], wd[0:w, p, :], hidden[0:w, q % 2, :], start=(p == 0), stop=(p == PAIRS - 1),
                                      skip_group_check=True).then_inc(h_d, 1)
                            if p == PAIRS - 1:
                                pe.wait_ge(h_sum, 2 * i + half + 1)
                                after(pe, h_tc, 2 * i + half)
                                for g in range(GPB):
                                    ins_ = pe.transpose(ot_ps[:, g * P:(g + 1) * P], total_f[:, half, g * P:(g + 1) * P], ident)
                                ins_.then_inc(h_t, 1)

            @block.scalar
            def _(eng):
                for i in pairs_of_blocks(act):
                    for k in range(2 * PAIRS):
                        half, p = k // PAIRS, k % PAIRS
                        w = SPAN[p]
                        act.wait_ge(h_g, i * 2 * PAIRS + k + 1)
                        if k >= 2:
                            act.wait_ge(h_a, i * 2 * PAIRS + k - 1)
                        act.activation(tanh[0:w, k % 2, :], g_ps[k % 2][0:w, :], ACT.Tanh, scale=0.5).then_inc(h_th, 1)
                        if p == PAIRS - 1:
                            act.wait_ge(h_t, 2 * i + half + 1)
                            after(act, h_out[half], 16 * i)
                            act.activation(total_t[:, half].rearrange("p g c -> p (g c)"), ot_ps[:], ACT.Copy).then_inc(h_tc, 1)

            @block.vector
            def _(eng):
                for i in pairs_of_blocks(v):
                    for k in range(2 * PAIRS):
                        half, p = k // PAIRS, k % PAIRS
                        w = SPAN[p]
                        m = i * 2 * PAIRS + k
                        v.wait_ge(h_th, m + 1)
                        after(v, h_b, m)
                        v.scalar_tensor_tensor(out=gated[0:w, 0, :], in0=tanh[0:w, k % 2, :], scalar=1.0, in1=g_ps[k % 2][0:w, :],
                                               op0=ALU.add, op1=ALU.mult).then_inc(h_a, 1)
                        v.wait_ge(h_u, m + 1)
                        v.wait_ge(h_a, m + 1)
                        after(v, h_h, m)
                        v.tensor_tensor(gated[0:w, 1, :], gated[0:w, 0, :], u_ps[k % 2][0:w, :], ALU.mult).then_inc(h_b, 1)
                        v.wait_ge(h_m, m + 1)
                        v.wait_ge(h_b, m + 1)
                        if k >= 2:
                            v.wait_ge(h_d, m - 1)
                        v.tensor_tensor(hidden[0:w, k % 2, :], gated[0:w, 1, :], m_ps[0:w, :], ALU.mult).then_inc(h_h, 1)
                        if p == PAIRS - 1:
                            v.wait_ge(h_d, m + 1)
                            after(v, h_t, 2 * i)
                            v.tensor_tensor(total_f[:, half, :], dn_ps[half][:], x_f[:, bass.ds((2 * i + half) * BLK, BLK)],
                                            ALU.add).then_inc(h_sum, 1)


_INS = ["x", "itok_B_0_2", "itok_B_0_7", "L0_cond_W1", "L0_cond_b1", "L0_cond_v", "L0_ffn_g_info", "L0_ffn_W_qkv",
        "L0_ffn_W_proj", "L0_ffn_b_proj", "L1_cond_weight", "L1_cond_bias", "L1_ffn_w_ln1", "L1_ffn_Wq", "L1_ffn_Wkva",
        "L1_ffn_Wkvb", "L1_ffn_Wo", "L1_ffn_w_ln2", "L1_ffn_Wgate", "L1_ffn_expert_bias", "L1_ffn_Wg", "L1_ffn_Wu",
        "L1_ffn_Wd", "L1_ffn_sWg", "L1_ffn_sWu", "L1_ffn_sWd"]


def kernel(**inputs):
    import concourse.bacc as _bacc
    from concourse.bass_utils import run_bass_kernel_spmd as _run

    nc = _bacc.Bacc("TRN2", target_bir_lowering=False, num_devices=1)
    arrays, aps = {}, {}
    for name in _INS:
        a = np.ascontiguousarray(inputs[name])
        arrays[f"in_{name}_dram"] = a
        aps[name] = nc.dram_tensor(f"in_{name}_dram", a.shape, mybir.dt.from_np(a.dtype), kind="ExternalInput").ap()
    at, table = shape_constants()
    arrays["shape_constants_dram"] = table
    const = nc.dram_tensor("shape_constants_dram", table.shape, F32, kind="ExternalInput").ap()
    out = nc.dram_tensor("out_dram", (B, S, C), F32, kind="ExternalOutput").ap()
    build(nc, aps, const, at, out)
    r = _run(nc, [arrays], core_ids=[0])
    return r.results[0]["out_dram"]
```

```python
from collections import namedtuple
from contextlib import ExitStack

import concourse.bass as bass
import numpy as np
from concourse import mybir

ALU = mybir.AluOpType
ACT = mybir.ActivationFunctionType
AX_X = mybir.AxisListType.X
F32 = mybir.dt.float32
BF16 = mybir.dt.bfloat16
I32 = mybir.dt.int32

P = 128
B, S, C = 128, 32, 128
TOK = B * S
SEQ = P // S
GROUPS = TOK // P
GPB = 4
BLK = GPB * P
NBLK = TOK // BLK
SPB = BLK // S
A = 32
H0, D0, REG = 16, 8, 5
HG = 4
HPG = H0 // HG
H1, D1, ROPE, R = 16, 64, 32, 16
NOPE = D1 - ROPE
E, I = 8, 64
PAIRS = (E + 2) // 2
SUBJ = 8
EPS = 1e-5
THETA = 100000.0
QX = HPG * S + S
BIG = 1e30
MASK = -float(2 ** 100)


def shape_constants():
    p = np.arange(P)
    f = np.float32
    q, k = p % S, np.arange(S)
    cols = {}
    cols["ident"] = np.eye(P)
    cols["prefix"] = k[None] <= q[:, None]
    cols["postfix"] = k[None] >= q[:, None]
    cols["cloze"] = k[None] != q[:, None]
    cols["own"] = k[None] == q[:, None]
    cols["same_seq"] = (p[:, None] // S) == (p[None] // S)
    cols["is_reg_key"] = np.broadcast_to(k[None] < REG, (P, S))
    cols["is_reg_row"] = (q < REG)[:, None]
    head = (p // D0) % HPG
    cols["head_scale"] = (p[:, None] // D0 == np.arange(H0)[None]) * f(D0) ** f(-0.5)
    cols["head_row"] = head[:, None] == np.arange(HPG)[None]
    share = np.where((q < REG)[:, None, None] | (np.arange(HPG + 1) == HPG)[None, None], 0.5, 1.0)
    cols["share"] = np.broadcast_to(share, (P, HG, HPG + 1)).reshape(P, -1)
    t = np.arange(S, dtype=f)
    freqs = (f(1.0) / f(THETA) ** (np.arange(0, ROPE, 2, dtype=f) / f(ROPE))).astype(f)
    angle = np.outer(t, freqs).astype(f)
    cos = np.repeat(np.cos(angle).T, 2, axis=0)
    sin = np.repeat(np.sin(angle).T, 2, axis=0)
    zero = np.zeros((S, S))
    causal = np.where(k[:, None] > k[None], MASK, 0.0)
    cols["q_turn"] = np.concatenate([cos, sin, zero, zero]) * f(D1) ** f(-0.5)
    cols["k_turn"] = np.concatenate([cos, sin, zero, zero])
    cols["causal"] = np.concatenate([zero, zero, zero, causal])
    pick = np.zeros((P, PAIRS, P))
    for part in range(3):
        for e in range(E + 1):
            pick[part * (E + 1) + e, e // 2, (e % 2) * I:(e % 2) * I + I] = 0.5
    cols["pick"] = pick.reshape(P, -1)
    cols["first"] = np.broadcast_to(E - np.arange(E)[None], (P, E))
    at, n = {}, 0
    for name, v in cols.items():
        at[name] = (n, n + v.shape[1])
        n += v.shape[1]
    return at, np.concatenate([np.asarray(v, f) for v in cols.values()], axis=1).astype(f)


def pairs_of_blocks(eng):
    yield 0
    with eng.Fori(1, NBLK // 2) as i:
        yield i


def blocks(eng):
    for i in pairs_of_blocks(eng):
        for half in range(2):
            yield i, half


def after(eng, signal, count):
    if not isinstance(count, int) or count > 0:
        eng.wait_ge(signal, count)


def wait_apart(pe, signal, count):
    if not isinstance(count, int) or count > 0:
        pe.wait_ge(signal, count)
        pe.nop(nofuse=True)


SLOTS = 2 * GPB


def slots(eng, most, ring=SLOTS, total=GROUPS):
    for j in range(ring):
        yield 0, j, lambda lag, j=j: j >= lag
    with eng.Fori(1, total // ring) as i:
        for j in range(ring):
            yield i, j, lambda lag: True
    for j in range(most):
        yield total // ring, j, lambda lag, j=j: lag > j


def skewed_blocks(eng, most):
    return slots(eng, most, 2, NBLK)


def build(nc, ins, const, const_at, out):
    v, act, pool = nc.vector, nc.scalar, nc.gpsimd
    x_d = ins["x"].rearrange("b s c -> (b s) c")
    x_groups = x_d.rearrange("(g p) c -> p g c", p=P)
    out_groups = out.rearrange("b s c -> (b s) c").rearrange("(g p) c -> p g c", p=P)

    top = ExitStack()
    with top:
        def sem(name):
            return top.enter_context(nc.semaphore(name))

        def sb(ctx, name, shape, dt=F32):
            return ctx.enter_context(nc.sbuf_tensor(name, shape, dt))

        def ps(ctx, name, shape, dt=F32):
            return ctx.enter_context(nc.psum_tensor(name, shape, dt))

        con = sb(top, "con", [P, const.shape[1]])

        def c(name):
            a, b = const_at[name]
            return con[:, a:b]

        ident = c("ident")
        x_f = sb(top, "x_f", [P, TOK])
        ones = sb(top, "ones", [P, P])
        w1 = sb(top, "w1", [P, A])
        b1 = sb(top, "b1", [A, 1])
        v_col = sb(top, "v_col", [A, 1])
        v_wide = sb(top, "v_wide", [A, S])
        prompt = sb(top, "prompt", [P, B], I32)
        wqkv = sb(top, "wqkv", [P, 3 * C])
        g_row = sb(top, "g_row", [P, C])
        wproj = sb(top, "wproj", [P, C])
        wproj_h = sb(top, "wproj_h", [P, HPG, C])
        bproj = sb(top, "bproj", [P, 1])
        w_subj = sb(top, "w_subj", [P, SUBJ, C])
        w_subj_t = sb(top, "w_subj_t", [P, SUBJ, C])
        ln1 = sb(top, "ln1", [P, 1])
        ln2 = sb(top, "ln2", [P, 1])
        wq_rope = sb(top, "wq_rope", [P, H1, 2 * ROPE])
        wq_lat = sb(top, "wq_lat", [P, H1, S])
        wk = sb(top, "wk", [P, 96])
        w_lat = sb(top, "w_lat", [P, S])
        w_o = sb(top, "w_o", [P, H1 // 4, C])
        wgate = sb(top, "wgate", [P, S])
        gate_b = sb(top, "gate_b", [P, E])
        wg = sb(top, "wg", [P, 2 * PAIRS, I])
        wu = sb(top, "wu", [P, E, I])
        wd = sb(top, "wd", [P, PAIRS, C])
        pick = sb(top, "pick", [3 * (E + 1), PAIRS, P], BF16)

        layer0 = top.enter_context(ExitStack())
        q_f = sb(layer0, "q_f", [P, TOK])
        k_f = sb(layer0, "k_f", [P, TOK])
        v_t = sb(layer0, "v_t", [P, GROUPS, C])
        class_mask = sb(layer0, "class_mask", [P, GROUPS, HPG + 1, S])

        similar = top.enter_context(ExitStack())
        lie = sb(similar, "lie", [P, 2, GROUPS, H0])
        guide = sb(similar, "guide", [P, C])

        pooling = top.enter_context(ExitStack())
        pooled_p = sb(pooling, "pooled_p", [P, GROUPS, P])

        between = top.enter_context(ExitStack())
        W = [P, GROUPS, S]
        seen_by = sb(between, "seen_by", W)
        row = sb(between, "row", [P, 4, GROUPS])
        wq = sb(between, "wq", [P, H1 * D1])
        wka = sb(between, "wka", [P, R + ROPE])
        wkvb = sb(between, "wkvb", [R, H1 * NOPE])
        wkvb_t = sb(between, "wkvb_t", [NOPE, H1, S])
        wo = sb(between, "wo", [NOPE, H1, C])
        score_ps = ps(between, "score_ps", [P, GROUPS * S])
        cleared, ld_late = sem("cleared"), sem("ld_late")
        late_loads = [
            (wkvb[:], ins["L1_ffn_Wkvb"]), (w_subj[:], ins["L1_cond_weight"].rearrange("s o h -> o s h")),
            (wo[:], ins["L1_ffn_Wo"].rearrange("(h d) c -> d h c", d=D1)[0:NOPE, :, :]),
            (wd[0:I, 0:E // 2, :], ins["L1_ffn_Wd"].rearrange("(p t) i c -> t i p c", t=2)[0]),
            (wd[I:P, 0:E // 2, :], ins["L1_ffn_Wd"].rearrange("(p t) i c -> t i p c", t=2)[1]),
            (wd[0:I, E // 2, :], ins["L1_ffn_sWd"][0]),
        ]

        with ExitStack() as ph:
            x_in = sb(ph, "x_in", [P, 2, GPB, C])
            hid = sb(ph, "hid", [A, TOK])
            types = sb(ph, "types", [P, GROUPS])
            kind = sb(ph, "kind", [P, 3, GROUPS])
            allow = sb(ph, "allow", W)
            part = sb(ph, "part", W)
            x_ps = ps(ph, "x_ps", [P, 2, BLK])
            h_ps = ps(ph, "h_ps", [A, 2, BLK])
            ld_ident, ld_first, ld_con, ld_prompt = sem("ld_ident"), sem("ld_first"), sem("ld_con"), sem("ld_prompt")
            ld_q, ld_mix = sem("ld_q"), sem("ld_mix")
            a_in = [sem("a_in0"), sem("a_in1")]
            a_x, a_xc, a_h, a_hc, a_sc, a_wide = (sem(n) for n in ("a_x", "a_xc", "a_h", "a_hc", "a_sc", "a_wide"))
            a_step = sem("a_step")
            first_loads = [
                (w1[:], ins["L0_cond_W1"]), (b1[:], ins["L0_cond_b1"].rearrange("(p a) -> p a", a=1)),
                (v_col[:], ins["L0_cond_v"].rearrange("(p a) -> p a", a=1)),
            ]
            q_loads = [
                (ln1[:], ins["L1_ffn_w_ln1"].rearrange("(p a) -> p a", a=1)),
                (ln2[:], ins["L1_ffn_w_ln2"].rearrange("(p a) -> p a", a=1)),
                (wka[:], ins["L1_ffn_Wkva"]), (wproj[:], ins["L0_ffn_W_proj"]), (wq[:], ins["L1_ffn_Wq"]),
            ]
            mix_loads = [
                (wgate[:, 0:E], ins["L1_ffn_Wgate"]), (gate_b[:], ins["L1_ffn_expert_bias"].partition_broadcast(P)),
                (wg[:, 0:E, :], ins["L1_ffn_Wg"].rearrange("e c i -> c e i")),
                (wg[:, E, :], ins["L1_ffn_sWg"][0]),
                (wu[:], ins["L1_ffn_Wu"].rearrange("e c i -> c e i")),
                (wg[:, E + 1, :], ins["L1_ffn_sWu"][0]),
                (wqkv[:], ins["L0_ffn_W_qkv"]),
                (g_row[:], ins["L0_ffn_g_info"][0, 0].partition_broadcast(P)),
                (bproj[:], ins["L0_ffn_b_proj"].rearrange("(p a) -> p a", a=1)),
            ]
            block = ph.enter_context(nc.Block())
            ident_end = const_at["ident"][1]

            @block.sync
            def _(sp):
                sp.dma_start(con[:, 0:ident_end], const[:, 0:ident_end]).then_inc(ld_ident, 16)
                for i, half in blocks(sp):
                    blk = 2 * i + half
                    after(sp, a_x, blk - 1)
                    sp.dma_start(x_in[:, half], x_groups[:, bass.ds(blk * GPB, GPB), :]).then_inc(a_in[half], 16)
                for dst, src in mix_loads:
                    sp.dma_start(dst, src).then_inc(ld_mix, 16)
                for dst, src in late_loads:
                    sp.dma_start(dst, src).then_inc(ld_late, 16)

            @block.gpsimd
            def _(eng):
                pool.memset(wkvb_t[:], 0.0).then_inc(cleared, 1)
                pool.memset(wq_lat[:], 0.0).then_inc(cleared, 1)
                pool.memset(wk[:], 0.0).then_inc(cleared, 1)
                pool.memset(w_lat[:], 0.0).then_inc(cleared, 1)
                pool.memset(ones[:], 1.0).then_inc(cleared, 1)
                pool.memset(wgate[:, E:S], 0.0).then_inc(cleared, 1)
                pool.memset(pooled_p[:], 0.0).then_inc(cleared, 1)

            @block.tensor
            def _(pe):
                pe.sem_inc(a_hc, 2)
                pe.wait_ge(ld_ident, 16)
                pe.wait_ge(ld_first, 16 * len(first_loads))
                for i, j, live in skewed_blocks(pe, 1):
                    if live(0):
                        blk = 2 * i + j
                        pe.wait_ge(a_in[j], 16 * i + 16)
                        after(pe, a_xc, blk - 1)
                        for g in range(GPB):
                            ins_ = pe.transpose(x_ps[:, j, g * P:(g + 1) * P], x_in[:, j, g, :], ident)
                        ins_.then_inc(a_x, 1)
                    if live(1):
                        blk, half = 2 * i + j - 1, (j - 1) % 2
                        pe.wait_ge(a_xc, blk + 1)
                        pe.wait_ge(a_hc, blk + 1)
                        pe.matmul(h_ps[:, half, :], w1[:], x_f[:, bass.ds(blk * BLK, BLK)], start=True, stop=True).then_inc(a_h, 1)
                pe.wait_ge(a_hc, NBLK + 2)
                pe.wait_ge(a_wide, 1)
                hid_v = hid[:].rearrange("a (g s l) -> a g s l", s=SEQ, l=S)
                for n in range(2):
                    for s in range(SEQ):
                        ins_ = pe.matmul(score_ps[32 * s:32 * s + 32, n * BLK:(n + 1) * BLK], v_wide[:],
                                         hid_v[:, n * 16:(n + 1) * 16, s, :], start=True, stop=True)
                ins_.then_inc(a_sc, 1)

            @block.scalar
            def _(eng):
                for dst, src in first_loads:
                    act.dma_start(dst, src).then_inc(ld_first, 16)
                act.dma_start(prompt[:], ins["itok_B_0_2"].partition_broadcast(P)).then_inc(ld_prompt, 16)
                act.dma_start(con[:, ident_end:], const[:, ident_end:]).then_inc(ld_con, 16)
                for dst, src in q_loads:
                    act.dma_start(dst, src).then_inc(ld_q, 16)
                act.wait_ge(ld_first, 16 * len(first_loads))
                for i, j, live in skewed_blocks(act, 1):
                    if live(0):
                        blk = 2 * i + j
                        act.wait_ge(a_x, blk + 1)
                        act.activation(x_f[:, bass.ds(blk * BLK, BLK)], x_ps[:, j, :], ACT.Copy).then_inc(a_xc, 1)
                    if live(1):
                        blk, half = 2 * i + j - 1, (j - 1) % 2
                        act.wait_ge(a_h, blk + 1)
                        act.activation(hid[:, bass.ds(blk * BLK, BLK)], h_ps[:, half, :], ACT.Tanh, bias=b1[:, 0:1]).then_inc(a_hc, 1)

            @block.vector
            def _(eng):
                count = [0]

                def done(ins_):
                    count[0] += 1
                    ins_.then_inc(a_step, 1)
                    v.wait_ge(a_step, count[0])

                def over_l(a):
                    return a.unsqueeze(2).to_broadcast(W)

                def over_g(a):
                    return a.unsqueeze(1).to_broadcast(W)

                v.wait_ge(ld_first, 16 * len(first_loads))
                v.tensor_copy(v_wide[:], v_col[:, 0:1].to_broadcast([A, S])).then_inc(a_wide, 1)
                v.wait_ge(ld_prompt, 16)
                for s in range(SEQ):
                    r = slice(32 * s, 32 * s + 32)
                    ins_ = v.tensor_copy(types[r, :], prompt[r, :].rearrange("p (g s) -> p g s", s=SEQ)[:, :, s])
                done(ins_)
                v.tensor_scalar(kind[:, 0, :], types[:], 0.0, None, ALU.is_equal)
                done(v.tensor_scalar(kind[:, 1, :], types[:], 1.0, None, ALU.is_equal))
                done(v.tensor_tensor(kind[:, 2, :], kind[:, 0, :], kind[:, 1, :], ALU.add))
                done(v.tensor_scalar(kind[:, 2, :], kind[:, 2, :], -1.0, 1.0, ALU.mult, ALU.add))
                v.wait_ge(ld_con, 16)
                v.tensor_tensor(part[:], over_l(kind[:, 0, :]), over_g(c("prefix")), ALU.mult)
                v.tensor_tensor(seen_by[:], over_l(kind[:, 1, :]), over_g(c("postfix")), ALU.mult)
                done(v.tensor_tensor(allow[:], over_l(kind[:, 2, :]), over_g(c("cloze")), ALU.mult))
                done(v.tensor_tensor(allow[:], allow[:], part[:], ALU.add))
                done(v.tensor_tensor(allow[:], allow[:], seen_by[:], ALU.add))
                v.tensor_reduce(row[:, 0, :], allow[:], AX_X, ALU.add)
                v.tensor_scalar(seen_by[:], allow[:], BIG, -BIG, ALU.mult, ALU.add)
                v.wait_ge(cleared, 5)
                v.wait_ge(ld_q, 16 * len(q_loads))
                v.tensor_scalar(wq[:], wq[:], ln1[:, 0:1], None, ALU.mult)
                done(v.tensor_scalar(wka[:], wka[:], ln1[:, 0:1], None, ALU.mult))
                for h in range(HPG):
                    v.tensor_scalar(wproj_h[:, h, :], wproj[:], c("head_row")[:, h:h + 1], None, ALU.mult)
                pairs = wq[:].rearrange("p (h a f t) -> p h a f t", h=H1, a=2, t=2)[:, :, 1, :, :]
                crossed = wq_rope[:, :, ROPE:2 * ROPE].rearrange("p h (f t) -> p h f t", t=2)
                v.tensor_copy(wq_rope[:, :, 0:ROPE], wq[:].rearrange("p (h a f) -> p h a f", h=H1, a=2)[:, :, 1, :])
                v.tensor_scalar(crossed[:, :, :, 0], pairs[:, :, :, 1], -1.0, None, ALU.mult)
                v.tensor_copy(crossed[:, :, :, 1], pairs[:, :, :, 0])
                rope = wka[:, R:R + ROPE]
                rope_pairs = rope.rearrange("p (f t) -> p f t", t=2)
                cross = wk[:, ROPE:2 * ROPE].rearrange("p (f t) -> p f t", t=2)
                v.tensor_copy(wk[:, 0:ROPE], rope)
                v.tensor_scalar(cross[:, :, 0], rope_pairs[:, :, 1], -1.0, None, ALU.mult)
                v.tensor_copy(cross[:, :, 1], rope_pairs[:, :, 0])
                v.tensor_copy(wk[:, 2 * ROPE:2 * ROPE + R], wka[:, 0:R])
                v.tensor_copy(w_lat[:, 0:R], wka[:, 0:R])
                v.tensor_copy(pick[:], c("pick")[0:3 * (E + 1), :].rearrange("p (a b) -> p a b", a=PAIRS))
                v.wait_ge(ld_mix, 16 * len(mix_loads))
                v.tensor_scalar(wgate[:, 0:E], wgate[:, 0:E], ln2[:, 0:1], None, ALU.mult)
                v.tensor_scalar(wg[:], wg[:], ln2[:, 0:1], None, ALU.mult)
                v.tensor_scalar(wu[:], wu[:], ln2[:, 0:1], None, ALU.mult)
                v.wait_ge(cleared, 7)

        with ExitStack() as ph:
            sc = sb(ph, "sc", W)
            wq_nt = sb(ph, "wq_nt", [NOPE, H1, C])
            t_ps = [ps(ph, f"t_ps{n}", [P, BLK]) for n in range(4)]
            small_ps = ps(ph, "small_ps", [P, BLK])
            m_ps = ps(ph, "m_ps", [P, BLK])
            k_ps = small_ps[:, 0:4 * R].rearrange("p (n r) -> p n r", r=R)
            a_ps = small_ps[:, 4 * R:4 * R + H1 * R].rearrange("p (h r) -> p h r", r=R)
            turned = sem("turned")
            untangled = sem("untangled")
            absorbed = sem("absorbed")
            b_step, b_shift, b_exp = sem("b_step"), sem("b_shift"), sem("b_exp")
            block = ph.enter_context(nc.Block())

            @block.tensor
            def _(pe):
                pe.wait_ge(ld_late, 16 * len(late_loads))
                for n in range(4):
                    ins_ = pe.transpose(k_ps[:, n, :], wkvb[:, n * P:(n + 1) * P], ident[0:R, 0:R])
                ins_.then_inc(turned, 1)
                for n in range(8):
                    ins_ = pe.transpose(t_ps[2 + n // 4][:, (n % 4) * P:(n % 4 + 1) * P], wq[:, n * P:(n + 1) * P], ident)
                    if n % 4 == 3:
                        ins_.then_inc(turned, 1)
                for s in range(SUBJ):
                    ins_ = pe.transpose(t_ps[s // 4][:, (s % 4) * P:(s % 4 + 1) * P], w_subj[:, s, :], ident)
                    if s % 4 == 3:
                        ins_.then_inc(turned, 1)
                pe.wait_ge(untangled, 5)
                for h in range(H1):
                    pe.matmul(a_ps[:, h, :], wq_nt[:, h, :], wkvb_t[:, h, 0:R], start=True, stop=True)
                for h in range(H1):
                    ins_ = pe.matmul(m_ps[32 * (h // 4):32 * (h // 4) + 32, (h % 4) * C:(h % 4 + 1) * C],
                                     wkvb_t[:, h, :], wo[:, h, :], start=True, stop=True)
                ins_.then_inc(absorbed, 1)

            @block.scalar
            def _(eng):
                act.wait_ge(b_shift, 1)
                act.activation(sc[:], sc[:], ACT.Exp).then_inc(b_exp, 1)
                act.wait_ge(turned, 1)
                for m in range(4):
                    ins_ = act.activation(wkvb_t[:, :, 0:R].rearrange("p (n m) r -> p n m r", m=4)[:, :, m, :],
                                          k_ps[32 * m:32 * m + 32, :, :], ACT.Copy)
                ins_.then_inc(untangled, 1)
                for n in range(2):
                    act.wait_ge(turned, 2 + n)
                    for m in range(2):
                        act.activation(wq_nt[:, 8 * n:8 * n + 8, :].rearrange("p (j m) c -> p j m c", m=2)[:, :, m, :],
                                       t_ps[2 + n][64 * m:64 * m + NOPE, :].rearrange("p (j c) -> p j c", j=4),
                                       ACT.Copy).then_inc(untangled, 1)
                for n in range(2):
                    act.wait_ge(turned, n + 4)
                    act.activation(w_subj_t[:, 4 * n:4 * n + 4, :].rearrange("p s o -> p (s o)"), t_ps[n][:], ACT.Copy)
                act.wait_ge(absorbed, 1)
                act.activation(wq_lat[:, :, 0:R], a_ps, ACT.Copy)
                act.activation(w_o[:].rearrange("p h c -> p (h c)"), m_ps[:], ACT.Copy)

            @block.vector
            def _(eng):
                count = [0]

                def done(ins_):
                    count[0] += 1
                    ins_.then_inc(b_step, 1)
                    v.wait_ge(b_step, count[0])

                def over_l(a):
                    return a.unsqueeze(2).to_broadcast(W)

                done(v.tensor_tensor(sc[:], seen_by[:], score_ps[:].rearrange("p (g l) -> p g l", l=S), ALU.add))
                done(v.tensor_reduce(row[:, 1, :], sc[:], AX_X, ALU.max))
                v.tensor_tensor(sc[:], sc[:], over_l(row[:, 1, :]), ALU.subtract).then_inc(b_shift, 1)
                v.wait_ge(b_exp, 1)
                done(v.tensor_reduce(row[:, 2, :], sc[:], AX_X, ALU.add))
                done(v.tensor_tensor(row[:, 2, :], row[:, 2, :], row[:, 0, :], ALU.mult))
                done(v.reciprocal(row[:, 3, :], row[:, 2, :]))
                done(v.tensor_tensor(sc[:], sc[:], over_l(row[:, 3, :]), ALU.mult))
                for s in range(SEQ):
                    r = slice(32 * s, 32 * s + 32)
                    ins_ = v.transpose(pooled_p[r, :, r], sc[r, :, :])
                done(ins_)
        between.close()

        with ExitStack() as ph:
            xc = sb(ph, "xc", [P, 2, BLK])
            q2 = sb(ph, "q2", [P, GPB, C])
            qg = sb(ph, "qg", [P, GPB, C])
            gh = sb(ph, "gh", [P, 2, H0])
            xc_ps = ps(ph, "xc_ps", [P, 2, BLK])
            qf_ps, kf_ps, qt_ps, vt_ps = (ps(ph, n, [P, BLK]) for n in ("qf_ps", "kf_ps", "qt_ps", "vt_ps"))
            c_xc, c_xcc = sem("c_xc"), sem("c_xcc")
            c_qf, c_kf, c_qt, c_vt = (sem(n) for n in ("c_qf", "c_kf", "c_qt", "c_vt"))
            c_qfc, c_kfc, c_sq, c_vtc, c_qg, c_red, c_g, c_g2 = (
                sem(n) for n in ("c_qfc", "c_kfc", "c_sq", "c_vtc", "c_qg", "c_red", "c_g", "c_g2"))
            x_st = sb(ph, "x_st2", [P, 2, GPB, C])
            c_x = [sem("c_x0"), sem("c_x1")]
            block = ph.enter_context(nc.Block())

            @block.sync
            def _(sp):
                for i, half in blocks(sp):
                    blk = 2 * i + half
                    after(sp, c_xc, blk - 1)
                    sp.dma_start(x_st[:, half], x_groups[:, bass.ds(blk * GPB, GPB), :]).then_inc(c_x[half], 16)

            @block.tensor
            def _(pe):
                for i, j, live in skewed_blocks(pe, 1):
                    if live(0):
                        blk = 2 * i + j
                        pe.wait_ge(c_x[j], 16 * i + 16)
                        after(pe, c_xcc, blk - 1)
                        for g in range(GPB):
                            ins_ = pe.matmul(xc_ps[:, j, g * P:(g + 1) * P], x_st[:, j, g, :],
                                             pooled_p[:, blk * GPB + g, :], start=True, stop=True)
                        ins_.then_inc(c_xc, 1)
                    if live(1):
                        blk, half = 2 * i + j - 1, (j - 1) % 2
                        pe.wait_ge(c_xcc, blk + 1)
                        after(pe, c_qg, blk)
                        after(pe, c_sq, blk)
                        for g in range(GPB):
                            ins_ = pe.matmul(qt_ps[:, g * P:(g + 1) * P], xc[:, half, g * P:(g + 1) * P],
                                             wqkv[:, 0:C], start=True, stop=True)
                        ins_.then_inc(c_qt, 1)
                        after(pe, c_qfc, blk)
                        pe.matmul(qf_ps[:], wqkv[:, 0:C], xc[:, half, :], start=True, stop=True).then_inc(c_qf, 1)
                        after(pe, c_kfc, blk)
                        pe.matmul(kf_ps[:], wqkv[:, C:2 * C], xc[:, half, :], start=True, stop=True).then_inc(c_kf, 1)
                        after(pe, c_vtc, blk)
                        for g in range(GPB):
                            ins_ = pe.matmul(vt_ps[:, g * P:(g + 1) * P], xc[:, half, g * P:(g + 1) * P],
                                             wqkv[:, 2 * C:3 * C], start=True, stop=True)
                        ins_.then_inc(c_vt, 1)

            @block.scalar
            def _(eng):
                act.wait_ge(c_g, 1)
                act.activation(gh[:, 1, :], gh[:, 0, :], ACT.Sqrt).then_inc(c_g, 1)
                for i, j, live in skewed_blocks(act, 1):
                    if live(0):
                        blk = 2 * i + j
                        act.wait_ge(c_xc, blk + 1)
                        after(act, c_vt, blk - 1)
                        act.activation(xc[:, j, :], xc_ps[:, j, :], ACT.Copy).then_inc(c_xcc, 1)
                    if live(1):
                        blk = 2 * i + j - 1
                        act.wait_ge(c_qt, blk + 1)
                        after(act, c_red, 2 * blk)
                        act.activation(q2[:].rearrange("p g c -> p (g c)"), qt_ps[:], ACT.Square).then_inc(c_sq, 1)
                        act.wait_ge(c_kf, blk + 1)
                        act.activation(k_f[:, bass.ds(blk * BLK, BLK)], kf_ps[:], ACT.Copy).then_inc(c_kfc, 1)
                        act.wait_ge(c_vt, blk + 1)
                        act.activation(v_t[:, bass.ds(blk * GPB, GPB), :], vt_ps[:].rearrange("p (g c) -> p g c", g=GPB),
                                       ACT.Copy).then_inc(c_vtc, 1)

            @block.vector
            def _(eng):
                def heads(a):
                    return a.rearrange("p (h d) -> p h d", d=D0)

                v.tensor_tensor(qg[:, 0, :], g_row[:], g_row[:], ALU.mult).then_inc(c_g2, 1)
                v.wait_ge(c_g2, 1)
                v.tensor_reduce(gh[:, 0, :], heads(qg[:, 0, :]), AX_X, ALU.add).then_inc(c_g, 1)
                v.wait_ge(c_g, 2)
                v.reciprocal(gh[:, 0, :], gh[:, 1, :]).then_inc(c_g, 1)
                v.wait_ge(c_g, 3)
                v.tensor_tensor(heads(guide[:]), heads(g_row[:]), gh[:, 0, :].unsqueeze(2).to_broadcast([P, H0, D0]),
                                ALU.mult).then_inc(c_g, 1)
                v.wait_ge(c_g, 4)
                for i, half in blocks(v):
                    blk = 2 * i + half
                    v.wait_ge(c_sq, blk + 1)
                    after(v, c_red, 2 * blk)
                    v.tensor_tensor(qg[:], qt_ps[:].rearrange("p (g c) -> p g c", g=GPB),
                                    guide[:].unsqueeze(1).to_broadcast([P, GPB, C]), ALU.mult).then_inc(c_qg, 1)
                    v.wait_ge(c_qf, blk + 1)
                    v.tensor_copy(q_f[:, bass.ds(blk * BLK, BLK)], qf_ps[:]).then_inc(c_qfc, 1)
                    v.wait_ge(c_qg, blk + 1)
                    v.tensor_reduce(lie[:, 0, bass.ds(blk * GPB, GPB), :], qg[:].rearrange("p g (h d) -> p g h d", d=D0),
                                    AX_X, ALU.add).then_inc(c_red, 1)
                    v.wait_ge(c_sq, blk + 1)
                    v.tensor_reduce(lie[:, 1, bass.ds(blk * GPB, GPB), :], q2[:].rearrange("p g (h d) -> p g h d", d=D0),
                                    AX_X, ALU.add).then_inc(c_red, 1)

        with ExitStack() as ph:
            W = [P, GROUPS, S]
            norm = sb(ph, "norm", [P, GROUPS, H0])
            inv = sb(ph, "inv", [P, GROUPS, H0])
            sim = sb(ph, "sim", [P, 4, GROUPS])
            ends = sb(ph, "ends", [P, 4])
            small = sb(ph, "small", [2, 4])
            spread = sb(ph, "spread", W)
            seen = sb(ph, "seen", W)
            t_ps = ps(ph, "ends_ps", [2, P])
            e_ps = ps(ph, "span_ps", [P, 2])
            key_ps = ps(ph, "key_ps", [P, GROUPS * S])
            n_step, n_root, n_pe = sem("n_step"), sem("n_root"), sem("n_pe")
            n_ends, n_small, n_spread = sem("n_ends"), sem("n_small"), sem("n_spread")
            block = ph.enter_context(nc.Block())

            @block.scalar
            def _(eng):
                act.activation(norm[:], lie[:, 1], ACT.Sqrt).then_inc(n_root, 1)

            @block.tensor
            def _(pe):
                pe.wait_ge(n_ends, 1)
                pe.transpose(t_ps[:], ends[:, 0:2], ident).then_inc(n_pe, 1)
                pe.wait_ge(n_small, 1)
                pe.matmul(e_ps[:], ones[0:2, :], small[:, 2:4], start=True, stop=True).then_inc(n_pe, 1)
                pe.wait_ge(n_spread, 1)
                for n in range(2):
                    ins_ = pe.matmul(key_ps[:, n * BLK:(n + 1) * BLK], c("same_seq"),
                                     spread[:, n * 16:(n + 1) * 16, :], start=True, stop=True)
                ins_.then_inc(n_pe, 1)

            @block.vector
            def _(eng):
                count = [0]

                def done(ins_):
                    count[0] += 1
                    ins_.then_inc(n_step, 1)
                    v.wait_ge(n_step, count[0])

                def over_k(a):
                    return a.unsqueeze(2).to_broadcast(W)

                def over_g(a):
                    return a.unsqueeze(1).to_broadcast(W)

                v.wait_ge(n_root, 1)
                done(v.reciprocal(inv[:], norm[:]))
                done(v.tensor_tensor(inv[:], inv[:], lie[:, 0], ALU.mult))
                done(v.tensor_reduce(sim[:, 0, :], inv[:], AX_X, ALU.add))
                done(v.tensor_scalar(sim[:, 0, :], sim[:, 0, :], 1.0 / H0, None, ALU.mult))
                done(v.tensor_scalar(ends[:, 2:3], c("is_reg_row"), -BIG, None, ALU.mult))
                v.tensor_scalar(sim[:, 1, :], sim[:, 0, :], ends[:, 2:3], None, ALU.add)
                done(v.tensor_scalar(sim[:, 2, :], sim[:, 0, :], -1.0, ends[:, 2:3], ALU.mult, ALU.add))
                v.tensor_reduce(ends[:, 0:2], sim[:, 1:3, :], AX_X, ALU.max).then_inc(n_ends, 1)
                v.wait_ge(n_pe, 1)
                done(v.tensor_reduce(small[:, 0:1], t_ps[:], AX_X, ALU.max))
                v.tensor_scalar(small[:, 2:4], ident[0:2, 0:2], small[:, 0:1], None, ALU.mult).then_inc(n_small, 1)
                v.wait_ge(n_pe, 2)
                done(v.tensor_copy(ends[:, 0:2], e_ps[:]))
                done(v.tensor_tensor(ends[:, 2:3], ends[:, 0:1], ends[:, 1:2], ALU.add))
                done(v.reciprocal(ends[:, 3:4], ends[:, 2:3]))
                done(v.tensor_scalar(sim[:, 1, :], sim[:, 0, :], ends[:, 1:2], ends[:, 3:4], ALU.add, ALU.mult))
                done(v.tensor_scalar(sim[:, 2, :], sim[:, 1, :], 0.9, None, ALU.is_gt))
                done(v.tensor_scalar(sim[:, 3, :], sim[:, 2, :], c("is_reg_row"), None, ALU.max))
                v.tensor_tensor(spread[:], over_k(sim[:, 3, :]), over_g(c("own")), ALU.mult).then_inc(n_spread, 1)
                v.wait_ge(n_pe, 3)
                keys = key_ps[:].rearrange("p (g k) -> p g k", k=S)
                v.tensor_scalar(spread[:], keys, -1.0, 1.0, ALU.mult, ALU.add)
                done(v.tensor_tensor(seen[:], keys, over_k(sim[:, 3, :]), ALU.is_equal))
                v.tensor_tensor(spread[:], spread[:], over_g(c("is_reg_key")), ALU.max)
                done(v.tensor_tensor(seen[:], seen[:], over_g(c("is_reg_key")), ALU.max))
                done(v.tensor_scalar(class_mask[:, :, HPG, :], spread[:], BIG, -BIG, ALU.mult, ALU.add))
                for h in range(HPG):
                    ins_ = v.tensor_scalar(class_mask[:, :, h, :], seen[:], BIG, -BIG, ALU.mult, ALU.add)
                done(ins_)
        pooling.close()
        similar.close()

        def block_of(i, j, lag):
            return 2 * i + (j - lag) // GPB

        def attention(ph, tag, parts, masked):
            cols = parts * S
            banks = 2 if cols > BLK else 1
            t = dict(
                s_ps=[ps(ph, f"{tag}_s_ps{r}", [P, banks, BLK]) for r in range(2)],
                o_ps=ps(ph, f"{tag}_o_ps", [P, 2, BLK]),
                rows=sb(ph, f"{tag}_rows", [P, 4, cols]),
                stat=sb(ph, f"{tag}_stat", [P, 4, 3, parts]),
                prob=sb(ph, f"{tag}_prob", [P, 2, cols]),
                o_sb=sb(ph, f"{tag}_o_sb", [P, 2, SPB, 4, S]),
                x_ps=ps(ph, f"{tag}_x_ps", [P, 2 if masked else 1, BLK]),
            )
            names = ("scored", "turned", "topped", "shifted", "exped", "summed", "inverted",
                     "scaled", "turned_back", "weighed", "kept", "projected", "added")
            if masked:
                names += ("masked", "shared", "merged")
            g = {n: sem(f"{tag}_{n}") for n in names}

            def half_cols(a):
                return a.rearrange("p (b c) -> p b c", b=banks)

            def turn(n, r):
                v.wait_ge(g["scored"], n + 1)
                after(v, g["turned_back"], n - 3)
                v.transpose(half_cols(t["rows"][:, r % 4, :]), t["s_ps"][r % 2][:, :, 0:cols // banks]).then_inc(g["turned"], 1)

            def mask(n, r):
                pool.wait_ge(g["turned"], n + 1)
                rows = t["rows"][:, r % 4, :].rearrange("p (g c) -> p g c", g=HG)
                pool.tensor_tensor(rows, rows, class_mask[:, n, :, :].rearrange("p s k -> p (s k)").unsqueeze(1)
                                   .to_broadcast([P, HG, QX]), ALU.add).then_inc(g["masked"], 1)

            def top(n, r):
                v.wait_ge(g["masked" if masked else "turned"], n + 1)
                v.tensor_reduce(t["stat"][:, r % 4, 0, :], t["rows"][:, r % 4, :].rearrange("p (s k) -> p s k", k=S),
                                AX_X, ALU.max).then_inc(g["topped"], 1)

            def per_row(n, r, which, op, after, signal):
                pool.wait_ge(g[after], n + 1)
                rows = t["rows"][:, r % 4, :].rearrange("p (s k) -> p s k", k=S)
                pool.tensor_tensor(rows, rows, t["stat"][:, r % 4, which, :].unsqueeze(2).to_broadcast([P, parts, S]),
                                   op).then_inc(g[signal], 1)

            def shift(n, r):
                per_row(n, r, 0, ALU.subtract, "topped", "shifted")

            def scale(n, r):
                per_row(n, r, 2, ALU.mult, "shared" if masked else "inverted", "scaled")

            def exp(n, r):
                act.wait_ge(g["shifted"], n + 1)
                act.activation(t["rows"][:, r % 4, :], t["rows"][:, r % 4, :], ACT.Exp).then_inc(g["exped"], 1)

            def total(n, r):
                st = t["stat"][:, r % 4]
                v.wait_ge(g["exped"], n + 1)
                v.tensor_reduce(st[:, 1, :], t["rows"][:, r % 4, :].rearrange("p (s k) -> p s k", k=S),
                                AX_X, ALU.add).then_inc(g["summed"], 1)

            def invert(n, r):
                st = t["stat"][:, r % 4]
                v.wait_ge(g["summed"], n + 1)
                v.reciprocal(st[:, 2, :], st[:, 1, :]).then_inc(g["inverted"], 1)

            def share(n, r):
                st = t["stat"][:, r % 4]
                if masked:
                    v.wait_ge(g["inverted"], n + 1)
                    v.tensor_tensor(st[:, 2, :], st[:, 2, :], c("share"), ALU.mult).then_inc(g["shared"], 1)

            def turn_back(n, r):
                v.wait_ge(g["scaled"], n + 1)
                v.wait_ge(g["weighed"], n + 1)
                v.transpose(t["prob"][:, r % 2, :], t["rows"][:, r % 4, :]).then_inc(g["turned_back"], 1)

            def merge(n, r):
                if masked:
                    v.wait_ge(g["turned_back"], n + 1)
                    pr = t["prob"][:, r % 2, :].rearrange("p (g c) -> p g c", g=HG)
                    first = pr[:, :, 0:HPG * S].rearrange("p g (h q) -> p g h q", q=S)[:, :, :, 0:REG]
                    second = pr[:, :, HPG * S:HPG * S + HPG * REG].rearrange("p g (h q) -> p g h q", q=REG)
                    v.tensor_tensor(first, first, second, ALU.add).then_inc(g["merged"], 1)

            def weigh(pe, n, r, values, width):
                pe.wait_ge(g["merged" if masked else "turned_back"], n + 1)
                wait_apart(pe, g["kept"], n)
                for s in range(SEQ):
                    for m in range(4):
                        ins_ = pe.matmul(t["o_ps"][32 * m:32 * m + 32, s // 2, (s % 2) * P:(s % 2) * P + P],
                                         values(s, m), t["prob"][:, r % 2, m * width:m * width + 4 * S],
                                         start=True, stop=True)
                ins_.then_inc(g["weighed"], 1)

            def keep(n, r):
                act.wait_ge(g["weighed"], n + 3)
                act.wait_ge(g["projected"], n + 1)
                dst = t["o_sb"][:, (r // GPB) % 2, 4 * (r % GPB):4 * (r % GPB) + 4, :, :].rearrange("p s h q -> p (s h q)")
                act.activation(dst.rearrange("p (b c) -> p b c", b=2), t["o_ps"][:, :, 0:2 * P], ACT.Copy).then_inc(g["kept"], 1)

            def project(pe, n, blk, r, weights):
                half, g_ = (r // GPB) % 2, r % GPB
                x_bank = t["x_ps"][:, half if masked else 0, g_ * P:(g_ + 1) * P]
                pe.wait_ge(g["kept"], n + 1)
                pe.wait_ge(g["added"], blk + 1)
                for h in range(4):
                    ins_ = pe.matmul(x_bank, weights[:, h, :], t["o_sb"][:, half, SEQ * g_:SEQ * (g_ + 1), h, :],
                                     start=(h == 0), stop=(h == 3))
                ins_.then_inc(g["projected"], 1)

            t.update(g)
            t.update(turn=turn, mask=mask, top=top, shift=shift, scale=scale, exp=exp, total=total, invert=invert, share=share, merge=merge,
                     turn_back=turn_back, weigh=weigh, keep=keep, project=project)
            return t

        Lags = namedtuple("Lags", "score top sum back keep add")
        D_LAGS = Lags(score=2, top=3, sum=5, back=6, keep=7, add=7)
        F_LAGS = Lags(score=4, top=5, sum=6, back=7, keep=7, add=8)
        SPREAD_ON_SCALAR = 14

        def softmax_on_vector(t, lags, i, j, live, between=lambda step: None):
            steps = ((("turn_back", lags.back), ("merge", lags.back)), (("total", lags.sum), ("invert", lags.sum), ("share", lags.sum)),
                     (("top", lags.top),), (("turn", lags.score),))
            for step, stages in enumerate(steps):
                for stage, lag in stages:
                    if live(lag):
                        t[stage](SLOTS * i + j - lag, j - lag)
                between(step)

        def softmax_on_pool(t, lags, i, j, live, masked):
            if live(lags.sum):
                t["scale"](SLOTS * i + j - lags.sum, j - lags.sum)
            if live(lags.top):
                t["shift"](SLOTS * i + j - lags.top, j - lags.top)
            if masked and live(lags.score):
                t["mask"](SLOTS * i + j - lags.score, j - lags.score)

        def softmax_on_scalar(t, lags, i, j, live, between=lambda: None):
            if live(lags.keep):
                t["keep"](SLOTS * i + j - lags.keep, j - lags.keep)
            between()
            if live(lags.top):
                t["exp"](SLOTS * i + j - lags.top, j - lags.top)

        with ExitStack() as ph:
            k_st = sb(ph, "k_st", [P, 2, BLK])
            v_st = sb(ph, "v_st", [P, 2, GPB, SEQ, C])
            q_x = sb(ph, "q_x", [P, 2, 2 * SEQ, H0, S])
            t = attention(ph, "d", HG * (HPG + 1), masked=True)
            d_k, d_v = [sem("d_k0"), sem("d_k1")], [sem("d_v0"), sem("d_v1")]
            d_q, d_values_cleared = [sem("d_q_act"), sem("d_q_dve")], sem("d_values_cleared")
            d_scores_cleared = sem("d_scores_cleared")
            block = ph.enter_context(nc.Block())

            @block.sync
            def _(sp):
                for i, half in blocks(sp):
                    blk = 2 * i + half
                    after(sp, t["scored"], GPB * (blk - 1))
                    sp.dma_start(k_st[:, half, :], k_f[:, bass.ds(blk * BLK, BLK)]).then_inc(d_k[half], 16)
                    if isinstance(blk, int):
                        sp.wait_ge(d_values_cleared, 1)
                    else:
                        sp.wait_ge(t["weighed"], GPB * (blk - 1) + 2)
                    for s in range(SEQ):
                        rows = slice(32 * s, 32 * s + 32)
                        sp.dma_start(v_st[rows, half, :, s, :], v_t[rows, bass.ds(blk * GPB, GPB), :]).then_inc(d_v[half], 16)

            @block.tensor
            def _(pe):
                pe.sem_inc(t["projected"], 2 * GPB)
                pe.sem_inc(t["weighed"], 2)
                pe.wait_ge(d_scores_cleared, 1)
                for i, j, live in slots(pe, D_LAGS.add):
                    if live(D_LAGS.score):
                        n, r = SLOTS * i + j - D_LAGS.score, (j - D_LAGS.score) % SLOTS
                        half, g = r // GPB, r % GPB
                        if g == 0:
                            pe.wait_ge(d_k[half], 16 * (i if j >= D_LAGS.score else i - 1) + 16)
                        for q_ready in d_q:
                            pe.wait_ge(q_ready, n - r % 2 + 2)
                        after(pe, t["turned"], n - 1)
                        for bank in range(2):
                            heads = slice(bank * H0 // 2, (bank + 1) * H0 // 2)
                            for s in range(SEQ):
                                keys = k_st[:, half, g * P + 32 * s:g * P + 32 * s + 32]
                                dst = t["s_ps"][r % 2][32 * s:32 * s + 32, bank, 0:2 * QX].rearrange("p (m c) -> p m c", c=QX)
                                queries = q_x[:, r // 2 % 2, r % 2 * SEQ + s, heads, :].rearrange("p (m h) q -> p m (h q)", m=2)
                                pe.matmul(dst[:, :, 0:HPG * S], keys, queries, start=True, stop=True)
                            for s in range(SEQ):
                                keys = k_st[:, half, g * P + 32 * s:g * P + 32 * s + 32]
                                dst = t["s_ps"][r % 2][32 * s:32 * s + 32, bank, 0:2 * QX].rearrange("p (m c) -> p m c", c=QX)
                                dst = dst[:, :, HPG * S:HPG * S + HPG * REG].rearrange("p m (h q) -> p m h q", q=REG)
                                queries = q_x[:, r // 2 % 2, r % 2 * SEQ + s, heads, 0:REG].rearrange("p (m h) q -> p m h q", m=2)
                                ins_ = pe.matmul(dst, keys, queries, start=True, stop=True)
                        ins_.then_inc(t["scored"], 1)
                    if live(D_LAGS.add):
                        t["project"](pe, SLOTS * i + j - D_LAGS.add, block_of(i, j, D_LAGS.add), (j - D_LAGS.add) % SLOTS, wproj_h)
                    if live(D_LAGS.back):
                        n, r = SLOTS * i + j - D_LAGS.back, (j - D_LAGS.back) % SLOTS
                        if r % GPB == 0:
                            pe.wait_ge(d_v[r // GPB], 16 * SEQ * ((i if j >= D_LAGS.back else i - 1) + 1))
                        t["weigh"](pe, n, r, lambda s, m, r=r: v_st[:, r // GPB, r % GPB, s, 32 * m:32 * m + 32], QX)

            @block.gpsimd
            def _(eng):
                pool.memset(v_st[:], 0.0).then_inc(d_values_cleared, 1)
                for i, j, live in slots(pool, D_LAGS.add):
                    softmax_on_pool(t, D_LAGS, i, j, live, True)

            def spread(i, j, live, scaled_copy, heads, signal):
                eng, copy = scaled_copy
                if live(j % 2):
                    n, r = SLOTS * i + j - j % 2, (j - j % 2) % SLOTS
                    if j % 2 == 0:
                        after(eng, t["scored"], n - 2)
                    q = q_f[:, bass.ds(n * P, 2 * P)].rearrange("p (s q) -> p s q", q=S)
                    for h in heads[j % 2::2]:
                        ins_ = copy(q_x[:, r // 2 % 2, :, h, :], q, c("head_scale")[:, h:h + 1])
                    ins_.then_inc(signal, 1)

            @block.scalar
            def _(eng):
                scaled = act, lambda o, a, f: act.activation(o, a, ACT.Copy, scale=f)
                for i, j, live in slots(act, D_LAGS.add):
                    softmax_on_scalar(t, D_LAGS, i, j, live, lambda: spread(i, j, live, scaled, range(SPREAD_ON_SCALAR), d_q[0]))

            @block.vector
            def _(eng):
                scaled = v, lambda o, a, f: v.tensor_scalar(o, a, f, None, ALU.mult)
                for r in range(2):
                    ins_ = v.memset(t["s_ps"][r][:, :, 0:2 * QX], 0.0)
                ins_.then_inc(d_scores_cleared, 1)
                v.sem_inc(t["added"], 2)

                def beside(i, j, live, step):
                    if step == 2:
                        spread(i, j, live, scaled, range(SPREAD_ON_SCALAR, H0), d_q[1])
                    if step == 3 and live(D_LAGS.add) and (j - D_LAGS.add) % GPB == GPB - 1:
                        blk = block_of(i, j, D_LAGS.add)
                        v.wait_ge(t["projected"], GPB * (blk + 3))
                        xs = x_f[:, bass.ds(blk * BLK, BLK)]
                        v.scalar_tensor_tensor(out=xs, in0=t["x_ps"][:, ((j - D_LAGS.add) // GPB) % 2, :],
                                               scalar=bproj[:, 0:1], in1=xs, op0=ALU.add, op1=ALU.add).then_inc(t["added"], 1)

                for i, j, live in slots(v, D_LAGS.add):
                    softmax_on_vector(t, D_LAGS, i, j, live, lambda step: beside(i, j, live, step))
        layer0.close()

        layer1 = top.enter_context(ExitStack())
        y_f = sb(layer1, "y_f", [P, TOK])
        yn_f = sb(layer1, "yn_f", [P, TOK])

        E_FETCH, E_MAP, E_NORM, E_TURN, E_OUT = 2, 3, 4, 5, 6

        with ExitStack() as ph:
            x_st = sb(ph, "x_st", [P, 2, BLK])
            w_st = sb(ph, "w_st", [P, 4, SEQ, C])
            subject = sb(ph, "subject", [1, B], I32)
            subject_w = sb(ph, "subject_w", [SUBJ, B], I32)
            subject_f = sb(ph, "subject_f", [SUBJ, B])
            is_subject = sb(ph, "is_subject", [SUBJ, B, S])
            is_st = sb(ph, "is_st", [SUBJ, 2, BLK])
            rank = sb(ph, "rank", [SUBJ, 1])
            bias = sb(ph, "bias", [SUBJ, C])
            y_t = sb(ph, "y_t", [P, 2, GPB, C])
            yn_t = sb(ph, "yn_t", [P, 2, GPB, C])
            junk = sb(ph, "junk", [P, 4, C])
            sq = sb(ph, "sq", [P, 2, 3, GPB])
            y_ps = [ps(ph, f"y_ps{r}", [P, BLK]) for r in range(4)]
            yt_ps = [ps(ph, f"yt_ps{r}", [P, BLK]) for r in range(2)]
            nt_ps = [ps(ph, f"nt_ps{r}", [P, BLK]) for r in range(2)]
            e_ld, e_x, e_is = sem("e_ld"), [sem("e_x0"), sem("e_x1")], [sem("e_is0"), sem("e_is1")]
            e_ready, e_w_act, e_w_dve, e_w_pool, e_y, e_yc, e_sq, e_ms, e_rt, e_inv, e_yn = (
                sem(n) for n in ("e_ready", "e_w_act", "e_w_dve", "e_w_pool", "e_y", "e_yc", "e_sq", "e_ms", "e_rt", "e_inv", "e_yn"))
            e_w_dma = [sem(f"e_w_dma{r}") for r in range(4)]
            e_yt, e_nt, e_ytc, e_ntc, e_bias = (sem(n) for n in ("e_yt", "e_nt", "e_ytc", "e_ntc", "e_bias"))
            block = ph.enter_context(nc.Block())

            def fetch(eng, copy, n, r, s, signal, by=1):
                after(eng, e_y, n - 3)
                which = eng.value_load(subject[0:1, bass.ds(n * SEQ + s, 1)], min_val=0, max_val=SUBJ - 1)
                copy(w_st[:, r % 4, s, :], w_subj_t[:, bass.ds(which, 1), :].rearrange("p a o -> p (a o)")).then_inc(signal, by)

            @block.sync
            def _(sp):
                sp.dma_start(subject[:], ins["itok_B_0_7"].rearrange("(a b) -> a b", a=1)).then_inc(e_ld, 16)
                sp.dma_start(subject_w[:], ins["itok_B_0_7"].partition_broadcast(SUBJ)).then_inc(e_ld, 16)
                sp.dma_start(bias[:], ins["L1_cond_bias"]).then_inc(e_ld, 16)
                sp.wait_ge(e_ready, 3)

                for i, j, live in slots(sp, E_FETCH):
                    if live(0) and j % GPB == 0:
                        blk, half = block_of(i, j, 0), j // GPB
                        after(sp, e_y, GPB * (blk - 1))
                        sp.dma_start(x_st[:, half, :], x_f[:, bass.ds(blk * BLK, BLK)]).then_inc(e_x[half], 16)
                        sp.dma_start(is_st[:, half, :], is_subject[:].rearrange("p b s -> p (b s)")[:, bass.ds(blk * BLK, BLK)])\
                            .then_inc(e_is[half], 16)
                    if live(E_FETCH):
                        r = (j - E_FETCH) % SLOTS
                        fetch(sp, sp.dma_start, SLOTS * i + j - E_FETCH, r, 3, e_w_dma[r % 4], 16)

            @block.gpsimd
            def _(eng):
                pool.iota(rank[:], [[0, 1]], base=0, channel_multiplier=1, allow_small_or_imprecise_dtypes=True).then_inc(e_ready, 1)
                pool.wait_ge(e_ld, 48)
                for i, j, live in slots(pool, E_FETCH):
                    if live(E_FETCH):
                        fetch(pool, pool.tensor_copy, SLOTS * i + j - E_FETCH, (j - E_FETCH) % SLOTS, 2, e_w_pool)

            @block.tensor
            def _(pe):
                for credited in (e_ytc, e_ntc, e_nt):
                    pe.sem_inc(credited, 2)
                pe.wait_ge(e_ready, 3)
                for i, j, live in slots(pe, E_OUT):
                    if live(E_FETCH):
                        n, r = SLOTS * i + j - E_FETCH, (j - E_FETCH) % SLOTS
                        g, half = r % GPB, r // GPB
                        if g == 0:
                            block_i = i if j >= E_FETCH else i - 1
                            pe.wait_ge(e_x[half], 16 * block_i + 16)
                            pe.wait_ge(e_is[half], 16 * block_i + 16)
                        after(pe, e_yc, n - 3)
                        after(pe, e_sq, n - 3)
                        pe.matmul(y_ps[r % 4][:, 0:C], is_st[:, half, g * P:(g + 1) * P], bias[:], start=True, stop=False,
                                  skip_group_check=True).then_inc(e_bias, 1)
                    if live(E_MAP):
                        n, r = SLOTS * i + j - E_MAP, (j - E_MAP) % SLOTS
                        g, half = r % GPB, r // GPB
                        for fetched in (e_w_act, e_w_dve, e_w_pool):
                            pe.wait_ge(fetched, n + 1)
                        uses = 2 * (i if j >= E_MAP else i - 1) + r // 4 + 1
                        pe.wait_ge(e_w_dma[r % 4], 16 * uses)
                        pe.wait_ge(e_bias, n + 1)
                        for s in range(SEQ):
                            ins_ = pe.matmul(y_ps[r % 4][32 * s:32 * s + 32, 0:C], x_st[:, half, g * P + 32 * s:g * P + 32 * s + 32],
                                             w_st[:, r % 4, s, :], start=False, stop=True, skip_group_check=True)
                        ins_.then_inc(e_y, 1)
                    if live(E_TURN) and (j - E_TURN) % GPB == GPB - 1:
                        blk, half = block_of(i, j, E_TURN), ((j - E_TURN) // GPB) % 2
                        pe.wait_ge(e_yc, GPB * (blk + 1))
                        pe.wait_ge(e_ytc, blk + 1)
                        pe.wait_ge(e_ntc, blk + 1)
                        for g in range(GPB):
                            ins_ = pe.transpose(yt_ps[half][:, g * P:(g + 1) * P], y_t[:, half, g, :], ident)
                        ins_.then_inc(e_yt, 1)
                        pe.wait_ge(e_yn, blk + 1)
                        for g in range(GPB):
                            ins_ = pe.transpose(nt_ps[half][:, g * P:(g + 1) * P], yn_t[:, half, g, :], ident)
                        ins_.then_inc(e_nt, 1)

            @block.scalar
            def _(eng):
                act.wait_ge(e_ld, 48)
                for i, j, live in slots(act, E_OUT):
                    if live(E_FETCH):
                        fetch(act, lambda o, a: act.activation(o, a, ACT.Copy), SLOTS * i + j - E_FETCH,
                              (j - E_FETCH) % SLOTS, 0, e_w_act)
                    if live(E_NORM) and (j - E_NORM) % GPB == GPB - 1:
                        blk, half = block_of(i, j, E_NORM), ((j - E_NORM) // GPB) % 2
                        act.wait_ge(e_ms, blk + 1)
                        act.activation(sq[:, half, 2, :], sq[:, half, 1, :], ACT.Sqrt).then_inc(e_rt, 1)
                    if live(E_MAP):
                        n, r = SLOTS * i + j - E_MAP, (j - E_MAP) % SLOTS
                        act.wait_ge(e_y, n + 1)
                        after(act, e_sq, n - 3)
                        act.activation(junk[:, r % 4, :], y_ps[r % 4][:, 0:C], ACT.Square,
                                       accum_out=sq[:, r // GPB, 0, r % GPB:r % GPB + 1]).then_inc(e_sq, 1)
                    if live(E_OUT) and (j - E_OUT) % GPB == GPB - 1:
                        blk, half = block_of(i, j, E_OUT), ((j - E_OUT) // GPB) % 2
                        act.wait_ge(e_yt, blk + 1)
                        act.activation(y_f[:, bass.ds(blk * BLK, BLK)], yt_ps[half][:], ACT.Copy).then_inc(e_ytc, 1)

            @block.vector
            def _(eng):
                v.wait_ge(e_ld, 48)
                v.wait_ge(e_ready, 1)
                v.tensor_copy(subject_f[:], subject_w[:]).then_inc(e_ready, 1)
                v.wait_ge(e_ready, 2)
                v.tensor_scalar(is_subject[:], subject_f[:].unsqueeze(2).to_broadcast([SUBJ, B, S]), rank[:, 0:1], None,
                                ALU.is_equal).then_inc(e_ready, 1)
                for i, j, live in slots(v, E_OUT):
                    if live(E_FETCH):
                        fetch(v, v.tensor_copy, SLOTS * i + j - E_FETCH, (j - E_FETCH) % SLOTS, 1, e_w_dve)
                    if live(E_NORM) and (j - E_NORM) % GPB == GPB - 1:
                        blk, half = block_of(i, j, E_NORM), ((j - E_NORM) // GPB) % 2
                        v.wait_ge(e_rt, blk + 1)
                        v.reciprocal(sq[:, half, 1, :], sq[:, half, 2, :]).then_inc(e_inv, 1)
                        v.wait_ge(e_inv, blk + 1)
                        v.wait_ge(e_yc, GPB * (blk + 1))
                        v.wait_ge(e_nt, blk + 1)
                        v.tensor_tensor(yn_t[:, half], y_t[:, half], sq[:, half, 1, :].unsqueeze(2).to_broadcast([P, GPB, C]),
                                        ALU.mult).then_inc(e_yn, 1)
                    if live(E_MAP):
                        n, r = SLOTS * i + j - E_MAP, (j - E_MAP) % SLOTS
                        g, half = r % GPB, r // GPB
                        v.wait_ge(e_sq, n + 1)
                        if g == 0:
                            after(v, e_yt, block_of(i, j, E_MAP) - 1)
                        v.tensor_copy(y_t[:, half, g, :], y_ps[r % 4][:, 0:C]).then_inc(e_yc, 1)
                        if g == GPB - 1:
                            v.tensor_scalar(sq[:, half, 1, :], sq[:, half, 0, :], 1.0 / C, EPS, ALU.mult, ALU.add).then_inc(e_ms, 1)
                    if live(E_OUT) and (j - E_OUT) % GPB == GPB - 1:
                        blk, half = block_of(i, j, E_OUT), ((j - E_OUT) // GPB) % 2
                        v.wait_ge(e_nt, blk + 3)
                        v.tensor_copy(yn_f[:, bass.ds(blk * BLK, BLK)], nt_ps[half][:]).then_inc(e_ntc, 1)

        with ExitStack() as ph:
            y_st = sb(ph, "y_st", [P, 2, BLK])
            q_h = sb(ph, "q_h", [P, 2, SPB, H1, S])
            k_h = sb(ph, "k_h", [P, 2, BLK])
            k_tmp = sb(ph, "k_tmp", [64, BLK])
            lat = sb(ph, "lat", [P, 2, GPB, SEQ, S])
            q_ps = [ps(ph, f"q_ps{r}", [P, BLK]) for r in range(2)]
            kv_ps = ps(ph, "kv_ps", [P, BLK])
            t = attention(ph, "f", H1, masked=False)
            f_y = [sem("f_y0"), sem("f_y1")]
            f_lat_cleared, f_const, f_q, f_qt, f_lt, f_ka, f_kl, f_kac, f_kt, f_kbc, f_klc = (
                sem(n) for n in ("f_lat_cleared", "f_const", "f_q", "f_qt", "f_lt", "f_ka", "f_kl", "f_kac", "f_kt", "f_kbc", "f_klc"))
            block = ph.enter_context(nc.Block())

            @block.sync
            def _(sp):
                def stage(blk, half):
                    after(sp, f_q, 3 * GPB * (blk - 1))
                    after(sp, f_kl, blk - 1)
                    sp.dma_start(y_st[:, half, :], yn_f[:, bass.ds(blk * BLK, BLK)]).then_inc(f_y[half], 16)

                for i, half in blocks(sp):
                    stage(2 * i + half, half)

            @block.tensor
            def _(pe):
                pe.sem_inc(t["projected"], 2 * GPB)
                pe.sem_inc(t["weighed"], 2)

                def queries(i, j, live, part):
                    if not live(0):
                        return
                    blk, half, g = block_of(i, j, 0), j // GPB, j % GPB
                    if part == 0:
                        if g == 0:
                            pe.wait_ge(f_y[half], 16 * i + 16)
                            after(pe, f_klc, blk)
                            pe.matmul(kv_ps[0:96, :], wk[:], y_st[:, half, :], start=True, stop=True).then_inc(f_ka, 1)
                        if g == 2:
                            pe.wait_ge(f_kt, blk + 1)
                            pe.wait_ge(f_kac, blk + 1)
                            for m in range(GPB):
                                ins_ = pe.matmul(kv_ps[:, m * S:(m + 1) * S], y_st[:, half, m * P:(m + 1) * P], w_lat[:],
                                                 start=True, stop=True)
                            ins_.then_inc(f_kl, 1)
                    slot = SLOTS * i + j
                    h = 4 * g + 2 * part
                    if part == 0:
                        after(pe, f_qt, 4 * slot)
                    else:
                        after(pe, f_lt, slot)
                    pe.matmul(q_ps[(j + part) % 2][:], wq_rope[:, h:h + 2, :], y_st[:, half, :], start=True, stop=True).then_inc(f_q, 1)
                    if part == 1:
                        pe.wait_ge(f_qt, 4 * slot + 2)
                        pe.matmul(q_ps[j % 2][:], wq_lat[:, 4 * g:4 * g + 4, :], y_st[:, half, :], start=True, stop=True).then_inc(f_q, 1)

                for i, j, live in slots(pe, F_LAGS.add):
                    if live(F_LAGS.score):
                        n, r = SLOTS * i + j - F_LAGS.score, (j - F_LAGS.score) % SLOTS
                        blk, half, g = block_of(i, j, F_LAGS.score), r // GPB, r % GPB
                        if g == 0:
                            pe.wait_ge(f_const, 2)
                            pe.wait_ge(f_qt, H1 * (blk + 1))
                            pe.wait_ge(f_lt, GPB * (blk + 1))
                            pe.wait_ge(f_kbc, blk + 1)
                            pe.wait_ge(f_kac, blk + 1)
                        after(pe, t["turned"], n - 1)
                        for s in range(SEQ):
                            ins_ = pe.matmul(t["s_ps"][r % 2][32 * s:32 * s + 32, 0, :], k_h[:, half, g * P + 32 * s:g * P + 32 * s + 32],
                                             q_h[:, half, g * SEQ + s, :, :], start=True, stop=True)
                        ins_.then_inc(t["scored"], 1)
                    if live(F_LAGS.add):
                        t["project"](pe, SLOTS * i + j - F_LAGS.add, block_of(i, j, F_LAGS.add), (j - F_LAGS.add) % SLOTS, w_o)
                    queries(i, j, live, 0)
                    if live(F_LAGS.back):
                        n, r = SLOTS * i + j - F_LAGS.back, (j - F_LAGS.back) % SLOTS
                        if r % GPB == 0:
                            pe.wait_ge(f_klc, block_of(i, j, F_LAGS.back) + 1)
                        t["weigh"](pe, n, r, lambda s, m, r=r: lat[:, r // GPB, r % GPB, s, :], 4 * S)
                    queries(i, j, live, 1)

            @block.gpsimd
            def _(eng):
                for half in range(2):
                    ins_ = pool.tensor_scalar(q_h[96:128, half].rearrange("p s h q -> p (s h) q"),
                                              c("causal")[96:128, :].unsqueeze(1).to_broadcast([S, SPB * H1, S]),
                                              1.0, 0.0, ALU.mult, ALU.add)
                ins_.then_inc(f_const, 1)
                ins_ = pool.tensor_copy(k_h[96:128].rearrange("p a (s k) -> p (a s) k", k=S),
                                        c("own")[96:128, :].unsqueeze(1).to_broadcast([S, 2 * SPB, S])).then_inc(f_const, 1)
                for i, j, live in slots(pool, F_LAGS.add):
                    softmax_on_pool(t, F_LAGS, i, j, live, False)

            @block.scalar
            def _(eng):
                for i, j, live in slots(act, F_LAGS.add):
                    softmax_on_scalar(t, F_LAGS, i, j, live)
                    if live(0) and j % GPB == 0:
                        blk, half = block_of(i, j, 0), j // GPB
                        act.wait_ge(f_ka, blk + 1)
                        after(act, t["scored"], GPB * (blk - 1))
                        act.activation(k_h[64:96, half, :], kv_ps[64:96, :], ACT.Copy).then_inc(f_kac, 1)
                    if live(0) and j % GPB == 2:
                        blk, half = block_of(i, j, 0), j // GPB
                        act.wait_ge(f_kl, blk + 1)
                        if isinstance(blk, int):
                            act.wait_ge(f_lat_cleared, 1)
                        else:
                            act.wait_ge(t["weighed"], GPB * (blk - 1) + 2)
                        for s in range(SEQ):
                            rows = slice(32 * s, 32 * s + 32)
                            ins_ = act.activation(lat[rows, half, :, s, :], kv_ps[rows, 0:GPB * S].rearrange("p (g r) -> p g r", r=S),
                                                  ACT.Copy)
                        ins_.then_inc(f_klc, 1)
                    if live(0):
                        blk, half, g = block_of(i, j, 0), j // GPB, j % GPB
                        act.wait_ge(f_q, 3 * (SLOTS * i + j) + 3)
                        after(act, t["scored"], GPB * (blk - 1))
                        for h in range(4):
                            ins_ = act.activation(q_h[64:96, half, :, 4 * g + h, :],
                                                  q_ps[j % 2][32 * h:32 * h + 32, :].rearrange("p (s q) -> p s q", q=S),
                                                  ACT.Copy, scale=float(D1) ** -0.5)
                        ins_.then_inc(f_lt, 1)

            @block.vector
            def _(eng):
                def over_s(a):
                    return a.unsqueeze(1).to_broadcast([a.shape[0], SPB, S])

                def by_s(a):
                    return a.rearrange("p (s q) -> p s q", q=S)

                v.memset(lat[:], 0.0).then_inc(f_lat_cleared, 1)
                v.sem_inc(t["added"], 1)
                def queries(i, j, live, step):
                    if step == 1 and live(F_LAGS.add) and (j - F_LAGS.add) % GPB == GPB - 1:
                        blk = block_of(i, j, F_LAGS.add)
                        v.wait_ge(t["projected"], GPB * (blk + 3))
                        ys = y_f[:, bass.ds(blk * BLK, BLK)]
                        v.tensor_tensor(ys, t["x_ps"][:, 0, :], ys, ALU.add).then_inc(t["added"], 1)
                    if not live(0) or step == 0:
                        return
                    blk, half, g = block_of(i, j, 0), j // GPB, j % GPB
                    if g == 0 and step == 1:
                        after(v, t["scored"], GPB * (blk - 1))
                    for h in {1: (0,), 2: (1,), 3: (2, 3)}[step]:
                        part, rows = h // 2, slice(64 * (h % 2), 64 * (h % 2) + 64)
                        v.wait_ge(f_q, 3 * (SLOTS * i + j) + part + 1)
                        v.tensor_tensor(q_h[0:64, half, :, 4 * g + h, :], by_s(q_ps[(j + part) % 2][rows, :]), over_s(c("q_turn")[0:64, :]),
                                        ALU.mult).then_inc(f_qt, 1)

                for i, j, live in slots(v, F_LAGS.add):
                    softmax_on_vector(t, F_LAGS, i, j, live, lambda step: queries(i, j, live, step))
                    if live(0):
                        blk, half, g = block_of(i, j, 0), j // GPB, j % GPB
                        if g == 0:
                            v.wait_ge(f_ka, blk + 1)
                            after(v, f_kbc, blk)
                            v.tensor_tensor(by_s(k_tmp[:]), by_s(kv_ps[0:64, :]), over_s(c("k_turn")[0:64, :]), ALU.mult).then_inc(f_kt, 1)
                        if g == 1:
                            v.wait_ge(f_kt, blk + 1)
                            for m in range(2):
                                rows = slice(ROPE * m, ROPE * (m + 1))
                                ins_ = v.tensor_tensor(k_h[rows, half, :], k_tmp[0:ROPE, :], k_tmp[ROPE:2 * ROPE, :], ALU.add)
                            ins_.then_inc(f_kbc, 1)

        moe = top.enter_context(ExitStack())
        logits = sb(moe, "logits", [P, GROUPS, E])
        comb_t = sb(moe, "comb_t", [3 * (E + 1), TOK], BF16)
        z_f = yn_f
        with ExitStack() as ph:
            z2 = sb(ph, "z2", [P, 2, BLK])
            sums = sb(ph, "sums", [2 * S, 2, BLK])
            ms = sb(ph, "ms", [P, 2, 3, GPB])
            diag = sb(ph, "diag", [P, 2, GPB, P])
            s_ps = [ps(ph, f"s_ps{r}", [2 * S, BLK]) for r in range(2)]
            l_ps = [ps(ph, f"l_ps{r}", [P, GPB, 2 * S]) for r in range(2)]
            r_ps = [ps(ph, f"r_ps{r}", [P, BLK]) for r in range(2)]
            g_sq, g_s, g_sc, g_l, g_ms, g_rt, g_inv, g_lm, g_lb, g_dg, g_r, g_zn, g_sum = (
                sem(n) for n in ("g_sq", "g_s", "g_sc", "g_l", "g_ms", "g_rt", "g_inv", "g_lm", "g_lb", "g_dg", "g_r", "g_zn",
                                 "g_sum"))
            block = ph.enter_context(nc.Block())

            @block.gpsimd
            def _(eng):
                for i in pairs_of_blocks(pool):
                    pair = bass.ds(i * 2 * BLK, 2 * BLK)
                    pool.tensor_tensor(x_f[:, pair], x_f[:, pair], y_f[:, pair], ALU.add).then_inc(g_sum, 1)

            @block.tensor
            def _(pe):
                for credited in (g_ms, g_lm, g_zn, g_l):
                    pe.sem_inc(credited, 2)
                for i, j, live in skewed_blocks(pe, 2):
                    if live(1):
                        blk, half = 2 * i + j - 1, (j - 1) % 2
                        wait_apart(pe, g_sc, blk + 1)
                        wait_apart(pe, g_ms, blk + 1)
                        wait_apart(pe, g_lm, blk + 1)
                        for g in range(GPB):
                            ins_ = pe.transpose(l_ps[half][:, g, :], sums[:, half, g * P:(g + 1) * P], ident[0:2 * S, 0:2 * S])
                        ins_.then_inc(g_l, 1)
                    if live(2):
                        blk = 2 * i + j - 2
                        pe.wait_ge(g_dg, blk + 1)
                        pe.wait_ge(g_zn, blk + 1)
                        pe.matmul(r_ps[j][:], ones[:], diag[:, j].rearrange("p g t -> p (g t)"), start=True, stop=True)\
                            .then_inc(g_r, 1)
                    if live(0):
                        blk = 2 * i + j
                        after(pe, g_sc, blk - 1)
                        pe.matmul(s_ps[j][0:S, :], wgate[:], y_f[:, bass.ds(blk * BLK, BLK)], start=True, stop=True)
                        pe.wait_ge(g_sq, blk + 1)
                        pe.matmul(s_ps[j][S:2 * S, :], ones[:, 0:S], z2[:, j, :], start=True, stop=True).then_inc(g_s, 1)

            @block.scalar
            def _(eng):
                for i, j, live in skewed_blocks(act, 1):
                    if live(0):
                        blk = 2 * i + j
                        after(act, g_s, blk - 1)
                        act.activation(z2[:, j, :], y_f[:, bass.ds(blk * BLK, BLK)], ACT.Square).then_inc(g_sq, 1)
                    if live(1):
                        blk, half = 2 * i + j - 1, (j - 1) % 2
                        act.wait_ge(g_ms, blk + 3)
                        act.activation(ms[:, half, 1, :], ms[:, half, 0, :], ACT.Sqrt).then_inc(g_rt, 1)
                    if live(0):
                        blk = 2 * i + j
                        act.wait_ge(g_s, blk + 1)
                        act.wait_ge(g_l, blk + 1)
                        act.activation(sums[:, j, :], s_ps[j][:], ACT.Copy).then_inc(g_sc, 1)

            @block.vector
            def _(eng):
                v.sem_inc(g_r, 2)
                for i, j, live in skewed_blocks(v, 2):
                    if live(1):
                        blk, half = 2 * i + j - 1, (j - 1) % 2
                        v.wait_ge(g_l, blk + 3)
                        v.tensor_scalar(ms[:, half, 0, :], l_ps[half][:, :, S], 1.0 / C, EPS, ALU.mult, ALU.add).then_inc(g_ms, 1)
                    if live(2):
                        blk = 2 * i + j - 2
                        v.wait_ge(g_r, blk + 3)
                        at = bass.ds(blk * BLK, BLK)
                        v.tensor_tensor(z_f[:, at], y_f[:, at], r_ps[j][:], ALU.mult).then_inc(g_zn, 1)
                    if live(1):
                        blk, half = 2 * i + j - 1, (j - 1) % 2
                        lg = logits[:, bass.ds(blk * GPB, GPB), :]
                        v.wait_ge(g_rt, blk + 1)
                        v.reciprocal(ms[:, half, 2, :], ms[:, half, 1, :]).then_inc(g_inv, 1)
                        v.wait_ge(g_inv, blk + 1)
                        v.wait_ge(g_r, blk + 1)
                        for g in range(GPB):
                            ins_ = v.tensor_scalar(diag[:, half, g, :], ident, ms[:, half, 2, g:g + 1], None, ALU.mult)
                        ins_.then_inc(g_dg, 1)
                        v.tensor_tensor(lg, l_ps[half][:, :, 0:E], ms[:, half, 2, :].unsqueeze(2).to_broadcast([P, GPB, E]),
                                        ALU.mult).then_inc(g_lm, 1)
                        v.wait_ge(g_lm, blk + 3)
                        v.tensor_tensor(lg, lg, gate_b[:].unsqueeze(1).to_broadcast([P, GPB, E]), ALU.add).then_inc(g_lb, 1)

        with ExitStack() as ph:
            W = [P, GROUPS, E]
            best = sb(ph, "best", W)
            chosen = sb(ph, "chosen", [P, 2, GROUPS, E])
            rest = sb(ph, "rest", W)
            ex = sb(ph, "ex", W)
            top_of = sb(ph, "top_of", [P, 4, GROUPS])
            comb = sb(ph, "comb", [P, GROUPS, E + 1])
            left = sb(ph, "left", [P, GROUPS, E + 1])
            parts = sb(ph, "parts", [P, GROUPS, 3, E + 1], BF16)
            ident_b = sb(ph, "ident_b", [P, P], BF16)
            c_ps = [ps(ph, f"c_ps{n}", [3 * (E + 1), 8, P], BF16) for n in range(4)]
            k_step, k_shift, k_exp, k_parts, k_t = (sem(n) for n in ("k_step", "k_shift", "k_exp", "k_parts", "k_t"))
            block = ph.enter_context(nc.Block())

            @block.scalar
            def _(eng):
                act.wait_ge(k_shift, 1)
                act.activation(ex[:], ex[:], ACT.Exp).then_inc(k_exp, 1)

            @block.tensor
            def _(pe):
                pe.wait_ge(k_parts, 1)
                for n in range(GROUPS):
                    ins_ = pe.transpose(c_ps[n // 8][:, n % 8, :], parts[:, n].rearrange("p a e -> p (a e)"), ident_b[:])
                    if n % 8 == 7:
                        ins_.then_inc(k_t, 1)

            @block.vector
            def _(eng):
                count = [0]

                def done(ins_):
                    count[0] += 1
                    ins_.then_inc(k_step, 1)
                    v.wait_ge(k_step, count[0])

                def over_e(a):
                    return a.unsqueeze(2).to_broadcast(W)

                def choose(src, rnd):
                    done(v.tensor_reduce(top_of[:, rnd, :], src, AX_X, ALU.max))
                    done(v.tensor_tensor(best[:], src, over_e(top_of[:, rnd, :]), ALU.is_equal))
                    done(v.tensor_tensor(best[:], best[:], c("first").unsqueeze(1).to_broadcast(W), ALU.mult))
                    done(v.tensor_reduce(top_of[:, 2, :], best[:], AX_X, ALU.max))
                    done(v.tensor_tensor(chosen[:, rnd], best[:], over_e(top_of[:, 2, :]), ALU.is_equal))

                v.tensor_copy(ident_b[:], ident)
                v.memset(comb[:, :, E:E + 1], 1.0)
                choose(logits[:], 0)
                v.tensor_tensor(ex[:], logits[:], over_e(top_of[:, 0, :]), ALU.subtract).then_inc(k_shift, 1)
                done(v.tensor_scalar(rest[:], chosen[:, 0], -BIG, None, ALU.mult))
                done(v.tensor_tensor(rest[:], rest[:], logits[:], ALU.add))
                choose(rest[:], 1)
                done(v.tensor_tensor(rest[:], chosen[:, 0], chosen[:, 1], ALU.add))
                v.wait_ge(k_exp, 1)
                done(v.tensor_tensor(ex[:], ex[:], rest[:], ALU.mult))
                done(v.tensor_reduce(top_of[:, 2, :], ex[:], AX_X, ALU.add))
                done(v.reciprocal(top_of[:, 3, :], top_of[:, 2, :]))
                done(v.tensor_tensor(comb[:, :, 0:E], ex[:], over_e(top_of[:, 3, :]), ALU.mult))
                done(v.tensor_copy(parts[:, :, 0, :], comb[:]))
                done(v.tensor_tensor(left[:], comb[:], parts[:, :, 0, :], ALU.subtract))
                done(v.tensor_copy(parts[:, :, 1, :], left[:]))
                done(v.tensor_tensor(left[:], left[:], parts[:, :, 1, :], ALU.subtract))
                v.tensor_copy(parts[:, :, 2, :], left[:]).then_inc(k_parts, 1)
                for n in range(4):
                    v.wait_ge(k_t, n + 1)
                    ins_ = v.tensor_copy(comb_t[:, n * 8 * P:(n + 1) * 8 * P], c_ps[n][:].rearrange("p a t -> p (a t)"))
                done(ins_)

        with ExitStack() as ph:
            tanh = sb(ph, "tanh", [P, 2, BLK])
            gated = sb(ph, "gated", [P, 2, BLK])
            hidden = sb(ph, "hidden", [P, 2, BLK])
            total_f = sb(ph, "total_f", [P, 2, BLK])
            total_t = sb(ph, "total_t", [P, 2, GPB, C])
            g_ps, u_ps = ([ps(ph, f"{n}_ps{r}", [P, BLK]) for r in range(2)] for n in ("g", "u"))
            m_ps = ps(ph, "mix_ps", [P, BLK])
            dn_ps = [ps(ph, f"dn_ps{r}", [P, BLK]) for r in range(2)]
            ot_ps = ps(ph, "ot_ps", [P, BLK])
            h_g, h_u, h_m, h_th, h_a, h_b, h_h, h_d, h_dn, h_sum, h_t, h_tc = (
                sem(n) for n in ("h_g", "h_u", "h_m", "h_th", "h_a", "h_b", "h_h", "h_d", "h_dn", "h_sum", "h_t", "h_tc"))
            h_out = [sem("h_out0"), sem("h_out1")]
            block = ph.enter_context(nc.Block())
            SPAN = [P] * (PAIRS - 1) + [I]
            RING = 2 * PAIRS
            H_DOWN, H_TURN = 1, 2

            def pairs(eng):
                return slots(eng, H_TURN, RING, NBLK * PAIRS)

            def closes(j, lag):
                return (j - lag) % PAIRS == PAIRS - 1

            @block.sync
            def _(sp):
                for i, half in blocks(sp):
                    blk = 2 * i + half
                    sp.wait_ge(h_tc, blk + 1)
                    sp.dma_start(out_groups[:, bass.ds(blk * GPB, GPB), :], total_t[:, half]).then_inc(h_out[half], 16)
                for half in range(2):
                    sp.wait_ge(h_out[half], 16 * (NBLK // 2 + 1))

            @block.tensor
            def _(pe):
                pe.sem_inc(h_sum, 2)
                pe.sem_inc(h_t, 2)
                for i, j, live in pairs(pe):
                    if live(0):
                        m, p = RING * i + j, j % PAIRS
                        z = z_f[:, bass.ds((2 * i + j // PAIRS) * BLK, BLK)]
                        wait_apart(pe, h_a, m - 1)
                        if p < PAIRS - 1:
                            pe.matmul(g_ps[j % 2][:], wg[:, 2 * p:2 * p + 2, :], z, start=True, stop=True).then_inc(h_g, 1)
                            wait_apart(pe, h_b, m - 1)
                            pe.matmul(u_ps[j % 2][:], wu[:, 2 * p:2 * p + 2, :], z, start=True, stop=True).then_inc(h_u, 1)
                        else:
                            wait_apart(pe, h_b, m - 1)
                            pe.matmul(g_ps[j % 2][:], wg[:, 2 * p:2 * p + 2, :], z, start=True, stop=True).then_inc(h_g, 1)
                        wait_apart(pe, h_h, m)
                        pe.matmul(m_ps[:], pick[:, p, :], comb_t[:, bass.ds((2 * i + j // PAIRS) * BLK, BLK)],
                                  start=True, stop=True).then_inc(h_m, 1)
                    if live(H_DOWN):
                        m, r = RING * i + j - H_DOWN, (j - H_DOWN) % RING
                        blk, half, p = 2 * i + (j - H_DOWN) // PAIRS, r // PAIRS, r % PAIRS
                        w = SPAN[p]
                        wait_apart(pe, h_h, m + 1)
                        if p == 0:
                            wait_apart(pe, h_sum, blk + 1)
                        pe.matmul(dn_ps[half][:], wd[0:w, p, :], hidden[0:w, r % 2, :], start=(p == 0), stop=(p == PAIRS - 1),
                                  skip_group_check=True).then_inc(h_d, 1)
                    if live(H_TURN) and closes(j, H_TURN):
                        blk = 2 * i + (j - H_TURN) // PAIRS
                        half = (j - H_TURN) % RING // PAIRS
                        pe.wait_ge(h_sum, blk + 3)
                        after(pe, h_tc, blk)
                        for g in range(GPB):
                            ins_ = pe.transpose(ot_ps[:, g * P:(g + 1) * P], total_f[:, half, g * P:(g + 1) * P], ident)
                        ins_.then_inc(h_t, 1)

            @block.scalar
            def _(eng):
                for half in range(2):
                    act.sem_inc(h_out[half], 16)
                for i, j, live in pairs(act):
                    if live(0):
                        m, w = RING * i + j, SPAN[j % PAIRS]
                        act.wait_ge(h_g, m + 1)
                        after(act, h_a, m - 1)
                        act.activation(tanh[0:w, j % 2, :], g_ps[j % 2][0:w, :], ACT.Tanh, scale=0.5).then_inc(h_th, 1)
                    if live(H_TURN) and closes(j, H_TURN):
                        blk = 2 * i + (j - H_TURN) // PAIRS
                        half = (j - H_TURN) % RING // PAIRS
                        act.wait_ge(h_t, blk + 3)
                        uses = i if j >= H_TURN else i - 1
                        act.wait_ge(h_out[half], 16 * uses + 16)
                        act.activation(total_t[:, half].rearrange("p g c -> p (g c)"), ot_ps[:], ACT.Copy).then_inc(h_tc, 1)

            @block.vector
            def _(eng):
                for i, j, live in pairs(v):
                    if live(0):
                        m, p = RING * i + j, j % PAIRS
                        w = SPAN[p]
                        v.wait_ge(h_th, m + 1)
                        after(v, h_b, m)
                        v.scalar_tensor_tensor(out=gated[0:w, 0, :], in0=tanh[0:w, j % 2, :], scalar=1.0, in1=g_ps[j % 2][0:w, :],
                                               op0=ALU.add, op1=ALU.mult).then_inc(h_a, 1)
                        if p < PAIRS - 1:
                            v.wait_ge(h_u, (PAIRS - 1) * (2 * i + j // PAIRS) + p + 1)
                        up = u_ps[j % 2][:] if p < PAIRS - 1 else g_ps[j % 2][I:2 * I, :]
                        v.wait_ge(h_a, m + 1)
                        after(v, h_h, m)
                        v.tensor_tensor(gated[0:w, 1, :], gated[0:w, 0, :], up, ALU.mult).then_inc(h_b, 1)
                        v.wait_ge(h_m, m + 1)
                        v.wait_ge(h_b, m + 1)
                        after(v, h_d, m - 1)
                        v.tensor_tensor(hidden[0:w, j % 2, :], gated[0:w, 1, :], m_ps[0:w, :], ALU.mult).then_inc(h_h, 1)
                    if live(H_DOWN) and closes(j, H_DOWN):
                        blk = 2 * i + (j - H_DOWN) // PAIRS
                        half = (j - H_DOWN) % RING // PAIRS
                        v.wait_ge(h_d, PAIRS * (blk + 1))
                        v.wait_ge(h_t, blk + 1)
                        v.tensor_tensor(total_f[:, half, :], dn_ps[half][:], x_f[:, bass.ds(blk * BLK, BLK)],
                                        ALU.add).then_inc(h_sum, 1)


_INS = ["x", "itok_B_0_2", "itok_B_0_7", "L0_cond_W1", "L0_cond_b1", "L0_cond_v", "L0_ffn_g_info", "L0_ffn_W_qkv",
        "L0_ffn_W_proj", "L0_ffn_b_proj", "L1_cond_weight", "L1_cond_bias", "L1_ffn_w_ln1", "L1_ffn_Wq", "L1_ffn_Wkva",
        "L1_ffn_Wkvb", "L1_ffn_Wo", "L1_ffn_w_ln2", "L1_ffn_Wgate", "L1_ffn_expert_bias", "L1_ffn_Wg", "L1_ffn_Wu",
        "L1_ffn_Wd", "L1_ffn_sWg", "L1_ffn_sWu", "L1_ffn_sWd"]


def kernel(**inputs):
    import concourse.bacc as _bacc
    from concourse.bass_utils import run_bass_kernel_spmd as _run

    nc = _bacc.Bacc("TRN2", target_bir_lowering=False, num_devices=1)
    arrays, aps = {}, {}
    for name in _INS:
        a = np.ascontiguousarray(inputs[name])
        arrays[f"in_{name}_dram"] = a
        aps[name] = nc.dram_tensor(f"in_{name}_dram", a.shape, mybir.dt.from_np(a.dtype), kind="ExternalInput").ap()
    at, table = shape_constants()
    arrays["shape_constants_dram"] = table
    const = nc.dram_tensor("shape_constants_dram", table.shape, F32, kind="ExternalInput").ap()
    out = nc.dram_tensor("out_dram", (B, S, C), F32, kind="ExternalOutput").ap()
    build(nc, aps, const, at, out)
    r = _run(nc, [arrays], core_ids=[0])
    return r.results[0]["out_dram"]
```
